# Optimizing a Trainium2 kernel written in Bass

```python
import numpy as np
import jax
import jax.numpy as jnp

def _softmax(x, axis=-1):
    return jax.nn.softmax(x, axis=axis)

def _gelu(x):
    return jax.nn.gelu(x, approximate=True)

def _silu(x):
    return jax.nn.silu(x)

def _sigmoid(x):
    return jax.nn.sigmoid(x)

def _layernorm(x, axis=-1, eps=1e-05):
    m = jnp.mean(x, axis=axis, keepdims=True)
    v = jnp.var(x, axis=axis, keepdims=True)
    return (x - m) / jnp.sqrt(v + eps)

def _scatter_add(tgt, idx, src, axis=0):
    return tgt.at[idx].add(src)

def _segment_sum(src, seg, n):
    return jax.ops.segment_sum(src, seg, n)
kernel_name = 'mk_flamingo_gated_d2_seqx_r2_77bf70'

def setup_inputs(seed: int=0):
    np.random.seed(seed)
    _w = jnp.asarray

    def _rec_inputs():
        import jax
        import jax.numpy as jnp
        _rk = jax.random.key(seed)
        x = -0.0002928 + 1 * jax.random.normal(jax.random.fold_in(_rk, 1), (16, 512, 512), jnp.float32)
        _lenS = 512 - jax.random.randint(jax.random.fold_in(_rk, 7), (16,), 0, max(1, 512 // 4) + 1, jnp.int32)
        _lenS2 = 120 - jax.random.randint(jax.random.fold_in(_rk, 8), (16,), 0, max(1, 120 // 4) + 1, jnp.int32)
        _ctx_1024P = jax.random.normal(jax.random.fold_in(_rk, 11), (16, 16, 512), jnp.float32)
        _ctx_1024c = jax.random.dirichlet(jax.random.fold_in(_rk, 511), 0.3 * jnp.ones((16,), jnp.float32), (16, 120))
        _ctx_1024t = jnp.einsum('bsk,bkd->bsd', _ctx_1024c, _ctx_1024P)
        _ctx_1024t = _ctx_1024t * jax.lax.rsqrt(jnp.mean(jnp.square(_ctx_1024t)) + 1e-12) * 0.953939
        ctx_1024 = -1.39393e-06 + 0.999914 * (_ctx_1024t + 0.3 * jax.random.normal(jax.random.fold_in(_rk, 611), (16, 120, 512), jnp.float32))
        _g = jax.random.normal(jax.random.fold_in(_rk, 9001), (2, 2), jnp.float32)
        _g = jnp.sign(_g) * jnp.maximum(jnp.abs(_g), 1.0) + (_g == 0) * 1.0
        g_xattn = _g[0]
        g_ffn = _g[1]
        return (x, ctx_1024, g_xattn, g_ffn)
    x, ctx_1024, g_xattn, g_ffn = _rec_inputs()

    def _L0_xattn_setup():
        import jax, jax.numpy as jnp
        import numpy as np
        import math
        B, T, E, H = (2, 1024, 512, 16)
        D = E // H
        key = jax.random.key(seed)
        ks = jax.random.split(key, 8)
        s = 1.0 / math.sqrt(E)
        return {'input': jax.random.normal(ks[0], (B, T, E), jnp.float32), 'encoded_features': jax.random.normal(ks[1], (B, T, E), jnp.float32), 'Wq': jax.random.normal(ks[2], (E, E), jnp.float32) * s, 'bq': jnp.zeros((E,), jnp.float32), 'Wkv': jax.random.normal(ks[3], (E, 2 * E), jnp.float32) * s, 'bkv': jnp.zeros((2 * E,), jnp.float32), 'Wo': jax.random.normal(ks[4], (E, E), jnp.float32) * s, 'bo': jnp.zeros((E,), jnp.float32)}
    _L0_xattn_all = _L0_xattn_setup()
    _L0_xattn_in = {k: v for k, v in _L0_xattn_all.items() if k in ('Wq', 'bq', 'Wkv', 'bkv', 'Wo', 'bo')}
    del _L0_xattn_all

    def _L0_ffn_setup():
        import jax, jax.numpy as jnp
        import numpy as np
        B, S, D, E = (4, 2048, 512, 8)
        key = jax.random.key(seed)
        k1, k2, k3, k4, k5 = jax.random.split(key, 5)
        scale = 1.0 / np.sqrt(D)
        return {'x': jax.random.normal(k1, (B, S, D), dtype=jnp.float32), 'Wg': jax.random.normal(k2, (D, D), dtype=jnp.float32) * scale, 'bg': jnp.zeros((D,), dtype=jnp.float32), 'We': jax.random.normal(k3, (E, D, D), dtype=jnp.float32) * scale, 'be': jnp.zeros((E, D), dtype=jnp.float32)}
    _L0_ffn_all = _L0_ffn_setup()
    _L0_ffn_in = {k: v for k, v in _L0_ffn_all.items() if k in ('Wg', 'bg', 'We', 'be')}
    del _L0_ffn_all

    def _L1_xattn_setup():
        import jax, jax.numpy as jnp
        import numpy as np
        key = jax.random.key(seed)
        k1, k2, k3, k4 = jax.random.split(key, 4)
        B, S, D = (8, 1024, 512)
        query = jax.random.normal(k1, (B, S, D), dtype=jnp.float32)
        key_t = jax.random.normal(k2, (B, S, D), dtype=jnp.float32)
        value = jax.random.normal(k3, (B, S, D), dtype=jnp.float32)
        Wq = jax.random.normal(k4, (D, D), dtype=jnp.float32) * (1.0 / np.sqrt(D))
        bq = jnp.zeros((D,), dtype=jnp.float32)
        return {'query': query, 'key': key_t, 'value': value, 'Wq': Wq, 'bq': bq}
    _L1_xattn_all = _L1_xattn_setup()
    _L1_xattn_in = {k: v for k, v in _L1_xattn_all.items() if k in ('Wq', 'bq')}
    del _L1_xattn_all

    def _L1_ffn_setup():
        import jax, jax.numpy as jnp
        import numpy as np
        IN_FEATURES = 512
        OUT_FEATURES = 512
        B, S = (8, 2048)
        key = jax.random.key(seed)
        kx, kw = jax.random.split(key)
        x = jax.random.normal(kx, (B, S, IN_FEATURES), dtype=jnp.float32)
        weight = jax.random.normal(kw, (OUT_FEATURES, IN_FEATURES), dtype=jnp.float32) * 0.1
        bias = jnp.zeros((OUT_FEATURES,), dtype=jnp.float32)
        return {'x': x, 'weight': weight, 'bias': bias}
    _L1_ffn_all = _L1_ffn_setup()
    _L1_ffn_in = {k: v for k, v in _L1_ffn_all.items() if k in ('weight', 'bias')}
    del _L1_ffn_all
    return {'x': x, 'ctx_1024': ctx_1024, 'g_xattn': g_xattn, 'g_ffn': g_ffn, 'L0_xattn_Wq': _L0_xattn_in['Wq'], 'L0_xattn_bq': _L0_xattn_in['bq'], 'L0_xattn_Wkv': _L0_xattn_in['Wkv'], 'L0_xattn_bkv': _L0_xattn_in['bkv'], 'L0_xattn_Wo': _L0_xattn_in['Wo'], 'L0_xattn_bo': _L0_xattn_in['bo'], 'L0_ffn_Wg': _L0_ffn_in['Wg'], 'L0_ffn_bg': _L0_ffn_in['bg'], 'L0_ffn_We': _L0_ffn_in['We'], 'L0_ffn_be': _L0_ffn_in['be'], 'L1_xattn_Wq': _L1_xattn_in['Wq'], 'L1_xattn_bq': _L1_xattn_in['bq'], 'L1_ffn_weight': _L1_ffn_in['weight'], 'L1_ffn_bias': _L1_ffn_in['bias']}

def reference(x, ctx_1024, g_xattn, g_ffn, L0_xattn_Wq, L0_xattn_bq, L0_xattn_Wkv, L0_xattn_bkv, L0_xattn_Wo, L0_xattn_bo, L0_ffn_Wg, L0_ffn_bg, L0_ffn_We, L0_ffn_be, L1_xattn_Wq, L1_xattn_bq, L1_ffn_weight, L1_ffn_bias):
    import jax
    import jax.numpy as jnp

    def _L0_xattn_ref(input, encoded_features, Wq, bq, Wkv, bkv, Wo, bo):
        import jax, jax.numpy as jnp
        import numpy as np
        import math
        B, T, E, H = (2, 1024, 512, 16)
        D = E // H
        b, tq, _ = input.shape
        tk = encoded_features.shape[1]
        q = (input @ Wq + bq).reshape(b, tq, H, D).transpose(0, 2, 1, 3)
        kv = (encoded_features @ Wkv + bkv).reshape(b, tk, 2, H, D).transpose(2, 0, 3, 1, 4)
        k, v = (kv[0], kv[1])
        scores = jnp.einsum('bhqd,bhkd->bhqk', q, k) / math.sqrt(D)
        attn = jax.nn.softmax(scores, axis=2)
        out = jnp.einsum('bhqk,bhkd->bhqd', attn, v)
        out = out.transpose(0, 2, 1, 3).reshape(b, tq, H * D)
        return out @ Wo + bo

    def _L0_ffn_ref(x, Wg, bg, We, be):
        import jax, jax.numpy as jnp
        import numpy as np
        B, S, D, E = (4, 2048, 512, 8)
        probs = jax.nn.softmax(x @ Wg + bg, axis=-1)
        idx = jnp.argmax(probs, axis=-1)
        p = jnp.take_along_axis(probs, idx[..., None], axis=-1)[..., 0]
        e_idx = idx % We.shape[0]
        h = jax.nn.relu(jnp.einsum('bsd,edf->besf', x, We) + be[None, :, None, :])
        onehot = jax.nn.one_hot(e_idx, We.shape[0], dtype=x.dtype)
        out = jnp.einsum('besf,bse->bsf', h, onehot) * p[..., None]
        return out

    def _L1_xattn_ref(query, key, value, Wq, bq):
        import jax, jax.numpy as jnp
        import numpy as np
        q = query @ Wq + bq
        k = key @ Wq + bq
        v = value @ Wq + bq
        dim_key = jnp.asarray(k.shape[-1], dtype=jnp.float32)
        logits = jnp.einsum('bqd,bkd->bqk', q, k) / jnp.sqrt(dim_key)
        weights = jax.nn.softmax(logits, axis=-1)
        out = jnp.einsum('bqk,bkd->bqd', weights, v)
        return out

    def _L1_ffn_ref(x, weight, bias):
        import jax, jax.numpy as jnp
        import numpy as np
        IN_FEATURES = 512
        OUT_FEATURES = 512
        B, S = (8, 2048)
        w_scale = jnp.mean(jnp.abs(weight))
        q_weight = jnp.sign(weight) * (jnp.abs(weight) > 0.5 * w_scale).astype(weight.dtype)
        i_scale = jnp.max(jnp.abs(x)) / 127.0
        q_input = jnp.clip(jnp.round(x / i_scale), -128.0, 127.0)
        out = jnp.einsum('bsk,ok->bso', q_input, q_weight) * w_scale * i_scale
        out = out + bias
        return out
    x = x + jnp.tanh(g_xattn[0]) * _L0_xattn_ref(_layernorm(x, axis=-1), ctx_1024, L0_xattn_Wq, L0_xattn_bq, L0_xattn_Wkv, L0_xattn_bkv, L0_xattn_Wo, L0_xattn_bo)
    x = x + jnp.tanh(g_ffn[0]) * _L0_ffn_ref(_layernorm(x, axis=-1), L0_ffn_Wg, L0_ffn_bg, L0_ffn_We, L0_ffn_be)
    x = x + jnp.tanh(g_xattn[1]) * _L1_xattn_ref(_layernorm(x, axis=-1), ctx_1024, ctx_1024, L1_xattn_Wq, L1_xattn_bq)
    x = x + jnp.tanh(g_ffn[1]) * _L1_ffn_ref(_layernorm(x, axis=-1), L1_ffn_weight, L1_ffn_bias)
    return x

_drawn_inputs = setup_inputs


def setup_inputs(seed=0):
    import zlib

    import numpy as np

    out = dict(_drawn_inputs(seed))
    spreads = {'g_ffn': (-1.0, 0.2),
     'L0_xattn_bq': (0.0, 0.8),
     'L0_xattn_bkv': (0.0, 0.318),
     'L0_xattn_bo': (0.0, 0.1),
     'L0_ffn_bg': (0.0, 0.8),
     'L0_ffn_be': (0.0, 0.8),
     'L1_xattn_bq': (0.0, 0.1),
     'L1_ffn_bias': (0.0, 0.1)}
    factors = {'L0_ffn_Wg': 4.011, 'L0_ffn_We': 3.892}
    for name, (base, spread) in spreads.items():
        noise = np.random.default_rng([zlib.crc32(name.encode()), seed]).standard_normal(out[name].shape)
        drawn = base * np.exp(spread * noise) if base else spread * noise
        out[name] = jnp.asarray(drawn.astype(out[name].dtype))
    for name, factor in factors.items():
        out[name] = (out[name] * factor).astype(out[name].dtype)
    return out
```

```python
from contextlib import ExitStack

import concourse.bass as bass
from concourse import mybir

F32 = mybir.dt.float32
F32R = mybir.dt.float32r
BF16 = mybir.dt.bfloat16
U32 = mybir.dt.uint32
I32 = mybir.dt.int32
ALU = mybir.AluOpType
ACT = mybir.ActivationFunctionType
AX_X = mybir.AxisListType.X

P = 128
BATCHES, SEQ, D = 16, 512, 512
KEYS = 120
TILES = SEQ // P
CHUNKS = D // P
HEADS = 16
HEAD = D // HEADS
GROUP = P // HEAD
GROUPS = HEADS // GROUP
EXPERTS = 8
REGION = BATCHES * SEQ + P
ROW = D + 3
EPS = 1e-5


class Memory:

    def __init__(self, nc, ctx, phase=""):
        self.nc, self.ctx, self.phase, self.sems = nc, ctx, phase, []

    def sbuf(self, name, shape, dtype=F32):
        return self.ctx.enter_context(self.nc.sbuf_tensor(self.phase + name, shape, dtype))

    def psum(self, name, shape, dtype=F32):
        return self.ctx.enter_context(self.nc.psum_tensor(self.phase + name, shape, dtype))

    def sem(self, name):
        self.sems.append(self.nc.alloc_semaphore(name=self.phase + name))
        return self.sems[-1]

    def clear_semaphores(self):
        self.nc.clear_and_free_semaphores(self.sems)
        self.nc.all_engine_barrier()


def three_pass(pe, out, left, right, first=True, last=True, k=P):
    (left_hi, left_lo), (right_hi, right_lo) = left, right
    pe.matmul(out, left_lo, right_hi, start=first, stop=False)
    pe.matmul(out, left_hi, right_lo, start=False, stop=False)
    return pe.matmul(out, left_hi, right_hi, start=False, stop=last)


def prepare(nc, hold, t, consts):
    with ExitStack() as ctx:
        mem = Memory(nc, ctx, "prepare_")
        raw = [mem.sbuf(f"raw_weight{i}", [P, CHUNKS, D]) for i in range(3)]
        wk, wv, w1, w1t = [[mem.sbuf(f"{n}_{h}", [P, CHUNKS, D], F32R) for h in ("hi", "lo")]
                           for n in ("wk", "wv", "w1", "w1t")]
        bk_row = mem.sbuf("bk_row", [P, D])
        bv_row = mem.sbuf("bv_row", [P, D])
        b1_row = mem.sbuf("b1_row", [P, D])
        context = mem.sbuf("context", [P, D])
        context_t = [mem.sbuf(f"context_t_{h}", [P, CHUNKS, KEYS], F32R) for h in ("hi", "lo")]
        k0 = mem.sbuf("k0", [P, D])
        v0 = mem.sbuf("v0", [P, D])
        k1 = mem.sbuf("k1", [P, D])
        v1 = mem.sbuf("v1", [P, 2, D], F32R)
        k0_t = mem.sbuf("k0_t", [P, 2, CHUNKS, KEYS], F32R)
        k1_t = mem.sbuf("k1_t", [P, 2, CHUNKS, KEYS], F32R)
        fold = mem.sbuf("fold", [P, D])
        fold_t = mem.sbuf("fold_t", [P, 2, CHUNKS, KEYS], F32R)
        fold_bias = mem.sbuf("fold_bias", [P, 1])
        product = mem.sbuf("product", [P, D])

        k1_bank, k0_bank, v0_bank, fold_bank = [mem.psum(n, [P, D]) for n in (
            "k1_bank", "k0_bank", "v0_bank", "fold_bank")]
        fold_t_bank, k1_t_bank, context_t_bank, k0_t_bank = [mem.psum(n, [P, CHUNKS, P]) for n in (
            "fold_t_bank", "k1_t_bank", "context_t_bank", "k0_t_bank")]

        sum_banks = (k1_bank, k0_bank, v0_bank, fold_bank)
        raw_loaded = [mem.sem(f"raw_loaded{i}") for i in range(3)]
        rows_loaded = mem.sem("rows_loaded")
        weight_hi, weight_lo = mem.sem("weight_hi"), mem.sem("weight_lo")
        w1_turned, w1t_hi, w1t_lo = mem.sem("w1_turned"), mem.sem("w1t_hi"), mem.sem("w1t_lo")
        context_loaded, context_turned = mem.sem("context_loaded"), mem.sem("context_turned")
        context_hi, context_lo = mem.sem("context_hi"), mem.sem("context_lo")
        k1_summed, k1_ready, k1_turned = mem.sem("k1_summed"), mem.sem("k1_ready"), mem.sem("k1_turned")
        k1_hi, k1_lo, v1_hi, v1_lo = [mem.sem(n) for n in ("k1_hi", "k1_lo", "v1_hi", "v1_lo")]
        k0_summed, k0_ready, k0_turned = mem.sem("k0_summed"), mem.sem("k0_ready"), mem.sem("k0_turned")
        k0_hi, k0_lo = mem.sem("k0_hi"), mem.sem("k0_lo")
        v0_summed, v0_ready = mem.sem("v0_summed"), mem.sem("v0_ready")
        fold_summed, fold_ready, fold_turned = [mem.sem(n) for n in ("fold_summed", "fold_ready", "fold_turned")]
        fold_hi, fold_lo, bias_ready = mem.sem("fold_hi"), mem.sem("fold_lo"), mem.sem("bias_ready")
        k0_stored, v0_stored, v1_stored, fold_stored, bias_stored = [mem.sem(n) for n in (
            "k0_stored", "v0_stored", "v1_stored", "fold_stored", "bias_stored")]

        def rows(w):
            return w.rearrange("(c p) n -> p c n", p=P)

        def chunks(tile):
            return tile.rearrange("p (c n) -> p c n", c=CHUNKS)

        weights = [(rows(t["L0_xattn_Wkv"][:, 0:D]), wk), (rows(t["L0_xattn_Wkv"][:, D:2 * D]), wv),
                   (rows(t["L1_xattn_Wq"]), w1), (rows(t["L0_xattn_Wq"]), hold["wq"]),
                   (rows(t["L0_xattn_Wo"]), hold["wo"]), (rows(t["L0_ffn_Wg"]), hold["wg"])]
        W1 = 2

        ctx.callback(mem.clear_semaphores)
        block = ctx.enter_context(nc.Block())

        @block.sync
        def _(sp):
            sp.dma_start(context[0:KEYS, :], t["ctx_1024"][0]).then_inc(context_loaded, 16)
            for n, (src, _) in enumerate(weights):
                if n >= 3:
                    sp.wait_ge(weight_lo, n - 2)
                if n == 3 + W1:
                    sp.wait_ge(w1_turned, CHUNKS)
                sp.dma_start(raw[n % 3][:], src).then_inc(raw_loaded[n % 3], 16)
                if n == 1:
                    for row, src in ((bk_row, t["L0_xattn_bkv"][0:D]), (bv_row, t["L0_xattn_bkv"][D:2 * D]),
                                     (b1_row, t["L1_xattn_bq"])):
                        sp.dma_start(row[:], src.partition_broadcast(P)).then_inc(rows_loaded, 16)

            def stores(b, last):
                if not last:
                    sp.wait_ge(context_turned, b + 1)
                    sp.dma_start(context[0:KEYS, :], t["ctx_1024"][b + 1]).then_inc(context_loaded, 16)
                sp.wait_ge(v1_lo, b + 1)
                sp.dma_start(t["v1_pairs"][b], v1[0:KEYS].bitcast(F32)).then_inc(v1_stored, 16)
                sp.wait_ge(bias_ready, b + 1)
                sp.dma_start(t["fold_biases"][b], fold_bias[0:KEYS]).then_inc(bias_stored, 16)
                sp.wait_ge(v0_ready, b + 1)
                sp.dma_start(t["v0_rows"][b], v0[0:KEYS]).then_inc(v0_stored, 16)
                sp.wait_ge(k0_lo, b + 1)
                sp.dma_start(t["k0_pairs"][b], k0_t[:].bitcast(F32)).then_inc(k0_stored, 16)
                sp.wait_ge(fold_lo, b + 1)
                sp.dma_start(t["fold_pairs"][b], fold_t[:].bitcast(F32)).then_inc(fold_stored, 16)

            with sp.Fori(0, BATCHES - 1) as b:
                stores(b, False)
            stores(BATCHES - 1, True)
            for s in (k0_stored, v0_stored, v1_stored, fold_stored, bias_stored):
                sp.wait_ge(s, 16 * BATCHES)

        @block.tensor
        def _(pe):
            def turn(bank, source, done):
                for c in range(CHUNKS):
                    last = pe.transpose(bank[:, c, 0:KEYS], source[0:KEYS, c * P:(c + 1) * P],
                                        consts["ident"][0:KEYS, 0:KEYS])
                last.then_inc(done, 1)

            def project(bank, left, right, done):
                for c in range(CHUNKS):
                    last = three_pass(pe, bank[0:KEYS, :], [x[:, c, :] for x in left],
                                      [x[:, c, :] for x in right], c == 0, c == CHUNKS - 1)
                last.then_inc(done, 1)

            def turn_context(b):
                pe.wait_ge(context_loaded, 16 * (b + 1))
                turn(context_t_bank, context, context_turned)

            pe.wait_ge(consts["ready"], consts["made"])
            pe.wait_ge(raw_loaded[W1], 16)
            for j, bank in enumerate(sum_banks):
                for c in range(CHUNKS):
                    last = pe.transpose(bank[:, c * P:(c + 1) * P], raw[W1][:, c, j * P:(j + 1) * P],
                                        consts["ident"][:])
                last.then_inc(w1_turned, 1)
            turn_context(0)
            pe.wait_ge(weight_lo, W1 + 1)
            pe.wait_ge(w1t_lo, CHUNKS)

            def batch(b, last):
                pe.wait_ge(context_lo, b + 1)
                pe.wait_ge(k1_ready, b)
                project(k1_bank, context_t, w1, k1_summed)
                pe.wait_ge(k0_ready, b)
                project(k0_bank, context_t, wk, k0_summed)
                pe.wait_ge(k1_ready, b + 1)
                pe.wait_ge(k1_lo, b)
                turn(k1_t_bank, k1, k1_turned)
                pe.wait_ge(v0_ready, b)
                project(v0_bank, context_t, wv, v0_summed)
                if not last:
                    turn_context(b + 1)
                pe.wait_ge(k1_lo, b + 1)
                pe.wait_ge(fold_ready, b)
                project(fold_bank, [k1_t[:, h] for h in range(2)], w1t, fold_summed)
                pe.wait_ge(k0_ready, b + 1)
                pe.wait_ge(k0_lo, b)
                turn(k0_t_bank, k0, k0_turned)
                pe.wait_ge(fold_ready, b + 1)
                pe.wait_ge(fold_lo, b)
                turn(fold_t_bank, fold, fold_turned)

            with pe.Fori(0, BATCHES - 1) as b:
                batch(b, False)
            batch(BATCHES - 1, True)

        @block.scalar
        def _(act):
            def high(out, bank, turned, n, done):
                act.wait_ge(turned, n)
                act.activation(out, bank, ACT.Copy).then_inc(done, 1)

            for n, (_, (hi, _)) in enumerate(weights):
                act.wait_ge(raw_loaded[n % 3], 16 * (n // 3 + 1))
                act.activation(hi[:], raw[n % 3][:], ACT.Copy).then_inc(weight_hi, 1)
                if n == W1:
                    for j, bank in enumerate(sum_banks):
                        high(w1t[0][:, j, :], bank[:], w1_turned, j + 1, w1t_hi)
                    high(context_t[0][:], context_t_bank[:, :, 0:KEYS], context_turned, 1, context_hi)

            def batch(b, last):
                act.wait_ge(k1_ready, b + 1)
                act.wait_ge(v1_stored, 16 * b)
                act.activation(v1[0:KEYS, 0], k1[0:KEYS, :], ACT.Copy).then_inc(v1_hi, 1)
                high(k1_t[:, 0], k1_t_bank[:, :, 0:KEYS], k1_turned, b + 1, k1_hi)
                if not last:
                    high(context_t[0][:], context_t_bank[:, :, 0:KEYS], context_turned, b + 2, context_hi)
                act.wait_ge(fold_turned, b)
                act.wait_ge(fold_summed, b + 1)
                act.activation(fold[0:KEYS, :], fold_bank[0:KEYS, :], ACT.Copy).then_inc(fold_ready, 1)
                act.wait_ge(k0_stored, 16 * b)
                high(k0_t[:, 0], k0_t_bank[:, :, 0:KEYS], k0_turned, b + 1, k0_hi)
                act.wait_ge(fold_stored, 16 * b)
                high(fold_t[:, 0], fold_t_bank[:, :, 0:KEYS], fold_turned, b + 1, fold_hi)

            with act.Fori(0, BATCHES - 1) as b:
                batch(b, False)
            batch(BATCHES - 1, True)

        @block.vector
        def _(dve):
            def low(out, whole, hi, high_done, n, done):
                dve.wait_ge(high_done, n)
                dve.tensor_tensor(out, whole, hi.bitcast(F32), ALU.subtract).then_inc(done, 1)

            for n, (_, (hi, lo)) in enumerate(weights):
                low(lo[:], raw[n % 3][:], hi[:], weight_hi, n + 1, weight_lo)
                if n == W1:
                    for j, bank in enumerate(sum_banks):
                        low(w1t[1][:, j, :], bank[:], w1t[0][:, j, :], w1t_hi, j + 1, w1t_lo)
                    low(context_t[1][:], context_t_bank[:, :, 0:KEYS], context_t[0][:], context_hi, 1, context_lo)
            dve.wait_ge(rows_loaded, 16 * 3)

            def batch(b, last):
                dve.wait_ge(k1_turned, b)
                dve.wait_ge(v1_lo, b)
                dve.wait_ge(k1_summed, b + 1)
                dve.tensor_tensor(k1[0:KEYS], k1_bank[0:KEYS], b1_row[0:KEYS], ALU.add).then_inc(k1_ready, 1)
                dve.wait_ge(k0_turned, b)
                dve.wait_ge(k0_summed, b + 1)
                dve.tensor_tensor(k0[0:KEYS], k0_bank[0:KEYS], bk_row[0:KEYS], ALU.add).then_inc(k0_ready, 1)
                dve.wait_ge(k1_ready, b + 1)
                dve.wait_ge(bias_stored, 16 * b)
                dve.scalar_tensor_tensor(product[0:KEYS], k1[0:KEYS], D ** -0.5, b1_row[0:KEYS], ALU.mult,
                                         ALU.mult, accum_out=fold_bias[0:KEYS, :]).then_inc(bias_ready, 1)
                low(v1[0:KEYS, 1], k1[0:KEYS], v1[0:KEYS, 0], v1_hi, b + 1, v1_lo)
                low(k1_t[:, 1], k1_t_bank[:, :, 0:KEYS], k1_t[:, 0], k1_hi, b + 1, k1_lo)
                dve.wait_ge(v0_stored, 16 * b)
                dve.wait_ge(v0_summed, b + 1)
                dve.tensor_tensor(v0[0:KEYS], v0_bank[0:KEYS], bv_row[0:KEYS], ALU.add).then_inc(v0_ready, 1)
                if not last:
                    low(context_t[1][:], context_t_bank[:, :, 0:KEYS], context_t[0][:], context_hi, b + 2,
                        context_lo)
                low(k0_t[:, 1], k0_t_bank[:, :, 0:KEYS], k0_t[:, 0], k0_hi, b + 1, k0_lo)
                low(fold_t[:, 1], fold_t_bank[:, :, 0:KEYS], fold_t[:, 0], fold_hi, b + 1, fold_lo)

            with dve.Fori(0, BATCHES - 1) as b:
                batch(b, False)
            batch(BATCHES - 1, True)


def constants(nc, mem, t):
    c = {"ident": mem.sbuf("ident", [P, P]), "ident_half": mem.sbuf("ident_half", [P, P], BF16),
         "before": mem.sbuf("before", [P, P], BF16), "ones": mem.sbuf("ones", [P, P], BF16),
         "numbers": mem.sbuf("numbers", [P, EXPERTS]), "own": mem.sbuf("own", [P, EXPERTS]),
         "gates": mem.sbuf("gates", [P, 4])}
    c["ready"], filled, c["made"] = mem.sem("constants_ready"), mem.sem("constants_filled"), 6
    gates_loaded = mem.sem("gates_loaded")
    c["passed"] = mem.sem("passed")
    count = mem.sbuf("count", [P, EXPERTS], I32)
    count_own = mem.sbuf("count_own", [P, EXPERTS], I32)
    with nc.Block() as block:
        @block.gpsimd
        def _(pool):
            pool.memset(c["ident"][:], 0.0).then_inc(filled, 1)
            pool.memset(c["ident_half"][:], 0.0).then_inc(filled, 1)
            pool.memset(c["ones"][:], 1.0).then_inc(filled, 1)
            pool.iota(count[:], [[1, EXPERTS]], base=0, channel_multiplier=0).then_inc(filled, 1)
            pool.iota(count_own[:], [[REGION, EXPERTS]], base=0, channel_multiplier=1).then_inc(filled, 1)
            pool.wait_ge(filled, 5)
            pool.tensor_copy(c["numbers"][:], count[:]).then_inc(c["ready"], 1)
            pool.tensor_copy(c["own"][:], count_own[:]).then_inc(c["ready"], 1)
            for out, source, keep, fill in ((c["ident"], c["ident"], ALU.not_equal, 1.0),
                                            (c["ident_half"], c["ident_half"], ALU.not_equal, 1.0),
                                            (c["before"], c["ones"], ALU.is_gt, 0.0)):
                pool.affine_select(out=out[:], in_=source[:], compare_op=keep, fill=fill, base=0,
                                   pattern=[[1, P]], channel_multiplier=-1).then_inc(c["ready"], 1)

        @block.sync
        def _(sp):
            sp.dma_start(c["gates"][:, 0:2], t["g_xattn"].partition_broadcast(P)).then_inc(gates_loaded, 16)
            sp.dma_start(c["gates"][:, 2:4], t["g_ffn"].partition_broadcast(P)).then_inc(gates_loaded, 16)

        @block.scalar
        def _(act):
            act.wait_ge(gates_loaded, 32)
            act.activation(c["gates"][:], c["gates"][:], ACT.Tanh).then_inc(c["ready"], 1)
            act.wait_ge(c["ready"], 6)
    return c


def scratch(nc):
    def table(name, shape, dtype=F32):
        return nc.dram_tensor(name, shape, dtype).ap()

    return {"k0_pairs": table("k0_pairs", [BATCHES, P, 2, CHUNKS, KEYS]),
            "fold_pairs": table("fold_pairs", [BATCHES, P, 2, CHUNKS, KEYS]),
            "v0_rows": table("v0_rows", [BATCHES, KEYS, D]),
            "v1_pairs": table("v1_pairs", [BATCHES, KEYS, 2, D]),
            "fold_biases": table("fold_biases", [BATCHES, KEYS, 1]),
            "routed": table("routed", [(EXPERTS * REGION + EXPERTS * P), ROW]),
            "results": table("results", [(BATCHES * TILES + EXPERTS) * P, D])}


class Ring:

    def __init__(self, start):
        self.start, self.k = start, 0

    def take(self):
        k, self.k = self.k, self.k + 1
        return self.start + k, k % 2


def wait(eng, sem, n):
    if not isinstance(n, int) or n > 0:
        eng.wait_ge(sem, n)


def wait_apart(eng, sem, n, passed):
    wait(eng, sem, n)
    if not isinstance(n, int):
        eng.sem_inc(passed, 1)


def attend_and_route(nc, hold, t, consts, keep):
    with ExitStack() as ctx:
        mem = Memory(nc, ctx, "attend_")
        wq, wo, wg = hold["wq"], hold["wo"], hold["wg"]
        bq_cols, bo_row, bg_row = mem.sbuf("bq_cols", [P, CHUNKS]), mem.sbuf("bo_row", [P, D]), mem.sbuf("bg_row", [P, D])
        x = mem.sbuf("x", [P, 2, TILES, D])
        stats, moments = mem.sbuf("stats", [P, TILES, 6]), mem.sbuf("moments", [P, TILES, 2])
        spread, istd, offset = [mem.sbuf(n, [P, TILES]) for n in ("spread", "istd", "offset")]
        half = mem.sbuf("half", [P, TILES])
        xn = mem.sbuf("xn", [P, TILES, D])
        x_t = [mem.sbuf(f"x_t_{h}", [P, CHUNKS, SEQ], F32R) for h in ("hi", "lo")]
        q = [mem.sbuf(f"q_{h}", [P, 2, SEQ], F32R) for h in ("hi", "lo")]
        q_stack = mem.sbuf("q_stack", [P, 2, GROUP, SEQ], F32R)
        k_stack = mem.sbuf("k_stack", [P, GROUPS, GROUP, KEYS], F32R)
        peak, shift, total, share = [mem.sbuf(n, [P, 2, GROUP]) for n in ("peak", "shift", "total", "share")]
        weights = mem.sbuf("weights", [P, 2, GROUP, SEQ])
        v = mem.sbuf("v", [P, D])
        v_shared = mem.sbuf("v_shared", [P, 2, GROUP, HEAD])
        out_t = [mem.sbuf(f"out_t_{h}", [P, GROUPS, SEQ], F32R) for h in ("hi", "lo")]
        x1 = mem.sbuf("x1", [P, TILES, ROW])
        stats1, moments1 = mem.sbuf("stats1", [P, TILES, 6]), mem.sbuf("moments1", [P, TILES, 2])
        spread1, minus_mean1 = mem.sbuf("spread1", [P, TILES]), mem.sbuf("minus_mean1", [P, TILES])
        xn1 = mem.sbuf("xn1", [P, TILES, D])
        x1_t = [mem.sbuf(f"x1_t_{h}", [P, 2, CHUNKS, P], F32R) for h in ("hi", "lo")]
        logits = mem.sbuf("logits", [P, 2, D])
        best, minus_best = mem.sbuf("best", [P, TILES, 8]), mem.sbuf("minus_best", [P, TILES])
        best_at = mem.sbuf("best_at", [P, TILES, 8], U32)
        mass, chance = mem.sbuf("mass", [P, TILES]), mem.sbuf("chance", [P, TILES])
        expert_u, expert = mem.sbuf("expert_u", [P, TILES], U32), mem.sbuf("expert", [P, TILES])
        one_hot = mem.sbuf("one_hot", [P, TILES, EXPERTS], BF16)
        rank, rank_own = mem.sbuf("rank", [P, TILES, EXPERTS]), mem.sbuf("rank_own", [P, TILES, EXPERTS])
        rank_sum = mem.sbuf("rank_sum", [P, TILES])
        place = mem.sbuf("place", [P, TILES], U32)

        score = mem.psum("score", [P, GROUP, SEQ])
        sums = mem.psum("sums", [P, 2, D])
        turns = mem.psum("turns", [P, 2, CHUNKS, P])

        S = {n: mem.sem(n) for n in (
            "rows_loaded", "row_scaled", "x_loaded", "k_loaded", "v_loaded", "filled", "stats_made",
            "moments_made", "spread_made", "istd_made", "mean_turned", "offset_made", "xn_ready",
            "x_biased", "sum_ready", "sum_done", "turn_ready", "turn_done", "x_hi", "q_hi", "q_stacked0",
            "q_stacked1", "scored", "peaked", "shifted", "weighed", "inverted", "v_ready", "out_hi",
            "stats1_made", "moments1_made", "spread1_made", "mean1_turned", "istd1_made", "offset1_made",
            "xn1_ready", "x1_hi", "best_made", "best_turned", "best_found", "massed", "expert_read",
            "expert_made", "one_hot_made", "chance_made", "rank_picked", "rank_summed", "placed",
            "place_kept", "counted", "scattered")}
        q_stacked = (S["q_stacked0"], S["q_stacked1"])
        STACK = 16 * 3 * GROUP
        SUMS, SUMS_FIRST = 14, 8
        QUERY_AT = (0, 3, 5, 7)
        TURNS = 12

        def sum_ring(b):
            return Ring(0 if isinstance(b, int) and b == 0 else SUMS * b - (SUMS - SUMS_FIRST))

        def turn_ring(b):
            if isinstance(b, int) and b in (0, BATCHES):
                return Ring(TILES if b == 0 else TURNS * b - TILES)
            return Ring(TURNS * b)

        def iterations(eng, iteration):
            iteration(0, 0, route=False, attend=True, prefetch=True)
            with eng.Fori(0, BATCHES // 2 - 1) as pair:
                for odd in range(2):
                    iteration(2 * pair + 1 + odd, 1 - odd, route=True, attend=True, prefetch=True)
            iteration(BATCHES - 1, 1, route=True, attend=True, prefetch=False)
            iteration(BATCHES, 0, route=True, attend=False, prefetch=False)

        passed = consts["passed"]
        ctx.callback(mem.clear_semaphores)
        block = ctx.enter_context(nc.Block())

        @block.sync
        def _(sp):
            def load_x(b, odd, start=0):
                wait(sp, S["sum_done"], start)
                sp.dma_start(x[:, odd], t["x"][b].rearrange("(t p) d -> p t d", p=P)).then_inc(S["x_loaded"], 16)

            def load_keys(b):
                pairs = t["k0_pairs"][b].rearrange("(g d) h m n -> g d h m n", d=HEAD)
                wait(sp, S["scored"], HEADS * b)
                for block_of, part in enumerate((0, 0, 1)):
                    for g in range(GROUP):
                        sp.dma_start(k_stack[HEAD * block_of:HEAD * (block_of + 1), :, g, :].bitcast(F32),
                                     pairs[g, :, part]).then_inc(S["k_loaded"], 16)

            def load_values(b):
                wait(sp, S["v_ready"], GROUPS * b)
                sp.dma_start(v[0:KEYS], t["v0_rows"][b]).then_inc(S["v_loaded"], 16)

            def stack(b, m, query_at):
                wait_apart(sp, S["scored"], HEADS * b + GROUP * (m - 1), passed)
                sp.wait_ge(S["sum_done"], query_at + 1)
                for g in range(GROUP):
                    for block_of, part in enumerate((0, 1, 0)):
                        sp.dma_start(q_stack[HEAD * block_of:HEAD * (block_of + 1), m % 2, g, :].bitcast(F32),
                                     q[part][HEAD * g:HEAD * (g + 1), m % 2, :].bitcast(F32)
                                     ).then_inc(q_stacked[m % 2], 16)

            load_x(0, 0)
            for to, source in ((bo_row, "L0_xattn_bo"), (bg_row, "L0_ffn_bg")):
                sp.dma_start(to[:], t[source].partition_broadcast(P)).then_inc(S["rows_loaded"], 16)
            sp.dma_start(bq_cols[:], t["L0_xattn_bq"].rearrange("(c p) -> p c", p=P),
                         allow_slow_non_contiguous=True).then_inc(S["rows_loaded"], 16)
            load_keys(0)
            load_values(0)

            def iteration(b, odd, route, attend, prefetch):
                if not attend:
                    return
                start = sum_ring(b).start
                if prefetch:
                    load_x(b + 1, 1 - odd, start)
                for m in range(GROUPS):
                    stack(b, m, start + (QUERY_AT[m] if route else m))
                if prefetch:
                    load_keys(b + 1)
                    load_values(b + 1)

            iterations(sp, iteration)

        @block.tensor
        def _(pe):
            def turn(ring, source, keys=P):
                n, bank = ring.take()
                wait(pe, S["turn_done"], n - 1)
                for c in range(CHUNKS):
                    last = pe.transpose(turns[:, bank, c, :], source[:, c * P:(c + 1) * P], consts["ident"][:])
                last.then_inc(S["turn_ready"], 1)
                return n + 1

            def project(ring, left, right):
                n, bank = ring.take()
                wait(pe, S["sum_done"], n - 1)
                for c in range(CHUNKS):
                    last = three_pass(pe, sums[:, bank, :], left(c), right(c), c == 0, c == CHUNKS - 1)
                last.then_inc(S["sum_ready"], 1)

            def turn_x(ring, b):
                for i in range(TILES):
                    pe.wait_ge(S["xn_ready"], TILES * b + i + 1)
                    turn(ring, xn[:, i])

            def turn_routed(ring, b, i):
                pe.wait_ge(S["xn1_ready"], TILES * b + i + 1)
                return turn(ring, xn1[:, i])

            def gate(ring, i, turned):
                pe.wait_ge(S["turn_done"], turned)
                project(ring, lambda c: [h[:, i % 2, c, :] for h in x1_t], lambda c: [h[:, c, :] for h in wg])

            def query(ring, b, m):
                project(ring, lambda c: [h[:, c, m * P:(m + 1) * P] for h in wq], lambda c: [h[:, c, :] for h in x_t])

            def scores(b, m):
                pe.wait_ge(q_stacked[m % 2], STACK * (2 * b + m // 2 + 1))
                pe.wait_ge(S["k_loaded"], 16 * 3 * GROUP * (b + 1))
                for g in range(GROUP):
                    wait(pe, S["weighed"], HEADS * b + GROUP * (m - 1) + g + 1)
                    pe.matmul(score[0:KEYS, g, :], k_stack[0:3 * HEAD, m, g, :], q_stack[0:3 * HEAD, m % 2, g, :],
                              start=True, stop=True).then_inc(S["scored"], 1)

            def weigh(ring, b, m):
                n, bank = ring.take()
                wait(pe, S["turn_done"], n - 1)
                pe.wait_ge(S["v_ready"], GROUPS * b + m + 1)
                for g in range(GROUP):
                    last = pe.matmul(turns[HEAD * g:HEAD * (g + 1), bank].rearrange("p c n -> p (c n)"),
                                     v_shared[0:KEYS, m % 2, g, :], weights[0:KEYS, m % 2, g, :], start=True, stop=True,
                                     tile_position=(0, HEAD * g))
                last.then_inc(S["turn_ready"], 1)
                return n + 1

            def back(ring, i, turned):
                pe.wait_ge(S["turn_done"], turned)
                project(ring, lambda c: [h[:, c, i * P:(i + 1) * P] for h in out_t], lambda c: [h[:, c, :] for h in wo])

            def ranks(ring, b):
                n, bank = ring.take()
                wait(pe, S["sum_done"], n - 1)
                pe.wait_ge(S["one_hot_made"], b + 1)
                out = sums[:, bank, 0:TILES * EXPERTS].rearrange("p (i e) -> p i e", e=EXPERTS)
                last = pe.matmul(out, consts["before"][:], one_hot[:], start=True, stop=False)
                for i in range(TILES - 1):
                    rest = TILES - 1 - i
                    last = pe.matmul(out[:, i + 1:TILES, :], consts["ones"][:],
                                     one_hot[:, i:i + 1, :].broadcast_to([P, rest, EXPERTS]), start=False,
                                     stop=i == TILES - 2)
                last.then_inc(S["sum_ready"], 1)
                n, bank = ring.take()
                wait(pe, S["sum_done"], n - 1)
                for i in range(TILES):
                    last = pe.matmul(sums[:, bank, 0:EXPERTS], consts["ones"][:], one_hot[:, i, :],
                                     start=i == 0, stop=i == TILES - 1)
                last.then_inc(S["sum_ready"], 1)

            turn_x(Ring(0), 0)

            def iteration(b, odd, route, attend, prefetch):
                s, r, p, turned = sum_ring(b), turn_ring(b), b - 1, {}
                if route:
                    turned[0] = turn_routed(r, p, 0)
                if attend:
                    pe.wait_ge(S["turn_done"], r.start - (1 if route else 0))
                    query(s, b, 0)
                if route:
                    turned[1] = turn_routed(r, p, 1)
                    gate(s, 0, turned[0])
                    turned[2] = turn_routed(r, p, 2)
                    gate(s, 1, turned[1])
                if attend:
                    scores(b, 0)
                    query(s, b, 1)
                if route:
                    gate(s, 2, turned[2])
                if attend:
                    weigh(r, b, 0)
                    scores(b, 1)
                if route:
                    turned[3] = turn_routed(r, p, 3)
                if attend:
                    query(s, b, 2)
                if route:
                    gate(s, 3, turned[3])
                if attend:
                    weigh(r, b, 1)
                    scores(b, 2)
                    query(s, b, 3)
                if route:
                    ranks(s, p)
                if attend:
                    weigh(r, b, 2)
                if prefetch:
                    turn_x(r, b + 1)
                if attend:
                    scores(b, 3)
                    turned = weigh(r, b, 3)
                    for i in range(TILES):
                        back(s, i, turned)

            iterations(pe, iteration)

        @block.scalar
        def _(act):
            def turned_hi(ring, out, done):
                n, bank = ring.take()
                act.wait_ge(S["turn_ready"], n + 1)
                act.activation(out, turns[:, bank], ACT.Copy).then_inc(S[done], 1)

            def skip_sums(ring, k):
                for _ in range(k):
                    ring.take()

            def x_hi(ring):
                for i in range(TILES):
                    turned_hi(ring, x_t[0][:, :, i * P:(i + 1) * P], "x_hi")

            def routed_hi(ring, i):
                turned_hi(ring, x1_t[0][:, i % 2], "x1_hi")

            def query_hi(ring, b, m):
                n, bank = ring.take()
                act.wait_ge(S["sum_ready"], n + 1)
                wait(act, q_stacked[m % 2], STACK * (2 * b + m // 2))
                act.activation(q[0][:, m % 2, :], sums[:, bank, :], ACT.Identity,
                               bias=bq_cols[:, m:m + 1]).then_inc(S["q_hi"], 1)

            def weights_of(b, m):
                act.wait_ge(S["shifted"], GROUPS * b + m + 1)
                for g in range(GROUP):
                    act.activation(weights[0:KEYS, m % 2, g, :], score[0:KEYS, g, :], ACT.Exp,
                                   bias=shift[0:KEYS, m % 2, g:g + 1], scale=HEAD ** -0.5,
                                   accum_out=total[0:KEYS, m % 2, g:g + 1]).then_inc(S["weighed"], 1)

            def out_hi(ring, m):
                n, bank = ring.take()
                act.wait_ge(S["turn_ready"], n + 1)
                act.activation(out_t[0][:, m, :], turns[:, bank].rearrange("p c n -> p (c n)"), ACT.Copy
                               ).then_inc(S["out_hi"], 1)

            def gate_mass(b, i):
                act.wait_ge(S["best_turned"], TILES * b + i + 1)
                act.wait_ge(S["best_found"], TILES * b + i + 1)
                act.activation(logits[:, i % 2, :], logits[:, i % 2, :], ACT.Exp, bias=minus_best[:, i:i + 1],
                               accum_out=mass[:, i:i + 1]).then_inc(S["massed"], 1)

            act.wait_ge(S["rows_loaded"], 16 * 3)
            x_hi(Ring(0))

            def iteration(b, odd, route, attend, prefetch):
                s, r, p = sum_ring(b), turn_ring(b), b - 1
                if route:
                    routed_hi(r, 0)
                if attend:
                    query_hi(s, b, 0)
                if route:
                    routed_hi(r, 1)
                    routed_hi(r, 2)
                    gate_mass(p, 0)
                    skip_sums(s, 2)
                if attend:
                    weights_of(b, 0)
                    query_hi(s, b, 1)
                if route:
                    gate_mass(p, 1)
                    skip_sums(s, 1)
                if attend:
                    out_hi(r, 0)
                    weights_of(b, 1)
                if route:
                    routed_hi(r, 3)
                if attend:
                    query_hi(s, b, 2)
                if route:
                    gate_mass(p, 2)
                    skip_sums(s, 1)
                if attend:
                    out_hi(r, 1)
                    weights_of(b, 2)
                    query_hi(s, b, 3)
                if route:
                    gate_mass(p, 3)
                if attend:
                    out_hi(r, 2)
                if prefetch:
                    x_hi(r)
                if attend:
                    weights_of(b, 3)
                    out_hi(r, 3)

            iterations(act, iteration)

        @block.vector
        def _(dve):
            def turned_lo(ring, hi, lo, hi_done, n_hi):
                n, bank = ring.take()
                dve.wait_ge(S[hi_done], n_hi)
                dve.tensor_tensor(lo, turns[:, bank], hi.bitcast(F32), ALU.subtract
                                  ).then_inc(S["turn_done"], 1)

            def x_lo(ring, b):
                for i in range(TILES):
                    hi, lo = [h[:, :, i * P:(i + 1) * P] for h in x_t]
                    turned_lo(ring, hi, lo, "x_hi", TILES * b + i + 1)

            def routed_lo(ring, b, i):
                hi, lo = [h[:, i % 2] for h in x1_t]
                turned_lo(ring, hi, lo, "x1_hi", TILES * b + i + 1)

            def query_lo(ring, b, m):
                n, bank = ring.take()
                dve.wait_ge(S["q_hi"], GROUPS * b + m + 1)
                dve.scalar_tensor_tensor(q[1][:, m % 2, :], sums[:, bank, :], bq_cols[:, m:m + 1],
                                         q[0][:, m % 2, :].bitcast(F32), ALU.add, ALU.subtract
                                         ).then_inc(S["sum_done"], 1)

            def out_lo(ring, b, m):
                n, bank = ring.take()
                dve.wait_ge(S["out_hi"], GROUPS * b + m + 1)
                dve.tensor_tensor(out_t[1][:, m, :], turns[:, bank].rearrange("p c n -> p (c n)"),
                                  out_t[0][:, m, :].bitcast(F32), ALU.subtract
                                  ).then_inc(S["turn_done"], 1)

            def peaks(b, m):
                n = GROUPS * b + m + 1
                dve.wait_ge(S["scored"], GROUP * n)
                dve.tensor_reduce(peak[0:KEYS, m % 2, :], score[0:KEYS], AX_X, ALU.max).then_inc(S["peaked"], 1)
                dve.wait_ge(S["peaked"], n)
                dve.tensor_scalar(shift[0:KEYS, m % 2, :], peak[0:KEYS, m % 2, :], -(HEAD ** -0.5), None, ALU.mult
                                  ).then_inc(S["shifted"], 1)

            def share_values(b, m):
                n = GROUPS * b + m + 1
                dve.wait_ge(S["weighed"], GROUP * n)
                dve.reciprocal(share[0:KEYS, m % 2, :], total[0:KEYS, m % 2, :]).then_inc(S["inverted"], 1)
                dve.wait_ge(S["v_loaded"], 16 * (b + 1))
                dve.wait_ge(S["inverted"], n)
                dve.tensor_tensor(v_shared[0:KEYS, m % 2], v[0:KEYS, m * P:(m + 1) * P].rearrange("p (g d) -> p g d", d=HEAD),
                                  share[0:KEYS, m % 2, :].unsqueeze(2).broadcast_to([KEYS, GROUP, HEAD]), ALU.mult
                                  ).then_inc(S["v_ready"], 1)

            def tile_stats(b, odd, i):
                if i == 0:
                    dve.wait_ge(S["x_loaded"], 16 * (b + 1))
                    wait(dve, S["xn_ready"], TILES * b)
                dve.bn_stats(stats[:, i, :], x[:, odd, i, :]).then_inc(S["stats_made"], 1)

            def batch_moments(b):
                for i in range(TILES):
                    wait_apart(dve, S["stats_made"], TILES * b + i + 1, passed)
                    dve.bn_aggr(moments[:, i, :], stats[:, i, :]).then_inc(S["moments_made"], 1)

            def gate_logits(ring, b, i):
                n, bank = ring.take()
                dve.wait_ge(S["sum_ready"], n + 1)
                wait(dve, S["massed"], TILES * b + max(i - 1, 0))
                dve.tensor_tensor(logits[:, i % 2, :], sums[:, bank, :], bg_row[:], ALU.add
                                  ).then_inc(S["sum_done"], 1)
                return n + 1

            def gate_best(b, i, logits_at):
                n = TILES * b + i + 1
                wait_apart(dve, S["sum_done"], logits_at, passed)
                dve.max(best[:, i, :], logits[:, i % 2, :]).then_inc(S["best_made"], 1)
                dve.wait_ge(S["best_made"], n)
                dve.tensor_scalar(minus_best[:, i:i + 1], best[:, i, 0:1], -1.0, None, ALU.mult
                                  ).then_inc(S["best_turned"], 1)
                dve.max_index(best_at[:, i, :], best[:, i, :], logits[:, i % 2, :]).then_inc(S["best_found"], 1)

            def choose(b):
                dve.wait_ge(S["best_found"], TILES * (b + 1))
                dve.tensor_scalar(expert_u[:], best_at[:, :, 0], EXPERTS - 1, None, ALU.bitwise_and
                                  ).then_inc(S["expert_read"], 1)
                dve.wait_ge(S["expert_read"], b + 1)
                dve.tensor_copy(expert[:], expert_u[:]).then_inc(S["expert_made"], 1)
                dve.wait_ge(S["expert_made"], b + 1)
                dve.tensor_tensor(one_hot[:], consts["numbers"][:].unsqueeze(1).broadcast_to([P, TILES, EXPERTS]),
                                  expert[:].unsqueeze(2).broadcast_to([P, TILES, EXPERTS]), ALU.is_equal
                                  ).then_inc(S["one_hot_made"], 1)

            def place_rows(ring, b, start):
                n, bank = ring.take()
                dve.wait_ge(S["sum_ready"], n + 1)
                dve.wait_ge(S["sum_done"], start)
                dve.tensor_tensor(rank[:], sums[:, bank, 0:TILES * EXPERTS].rearrange("p (i e) -> p i e", e=EXPERTS),
                                  keep["counts"][:].unsqueeze(1).broadcast_to([P, TILES, EXPERTS]), ALU.add
                                  ).then_inc(S["sum_done"], 1)
                dve.wait_ge(S["sum_done"], n + 1)
                n, bank = ring.take()
                dve.wait_ge(S["sum_ready"], n + 1)
                dve.tensor_tensor(keep["counts"][:], keep["counts"][:], sums[:, bank, 0:EXPERTS], ALU.add
                                  ).then_inc(S["sum_done"], 1)
                dve.tensor_tensor(rank_own[:], rank[:], one_hot[:], ALU.mult).then_inc(S["rank_picked"], 1)
                dve.wait_ge(S["rank_picked"], b + 1)
                dve.tensor_reduce(rank_sum[:], rank_own[:], AX_X, ALU.add).then_inc(S["rank_summed"], 1)
                dve.wait_ge(S["rank_summed"], b + 1)
                wait(dve, S["scattered"], 16 * TILES * b)
                dve.scalar_tensor_tensor(place[:], expert[:], float(REGION), rank_sum[:], ALU.mult, ALU.add
                                         ).then_inc(S["placed"], 1)
                dve.wait_ge(S["placed"], b + 1)
                dve.tensor_copy(keep["places"][:, bass.ds(TILES * b, TILES)], place[:]).then_inc(S["place_kept"], 1)

            def chances(b):
                dve.wait_ge(S["massed"], TILES * (b + 1))
                dve.reciprocal(chance[:], mass[:]).then_inc(S["chance_made"], 1)
                dve.wait_ge(S["chance_made"], 2 * b + 1)
                dve.tensor_scalar(x1[:, :, D + 2], chance[:], consts["gates"][:, 2:3], None, ALU.mult
                                  ).then_inc(S["chance_made"], 1)

            def add_up(ring, b, odd, i):
                n, bank = ring.take()
                dve.wait_ge(S["sum_ready"], n + 1)
                if i == 0:
                    wait(dve, S["scattered"], 16 * TILES * b)
                dve.wait_ge(S["x_biased"], TILES * b + i + 1)
                dve.scalar_tensor_tensor(x1[:, i, 0:D], sums[:, bank, :], consts["gates"][:, 0:1], x[:, odd, i, :],
                                         ALU.mult, ALU.add).then_inc(S["sum_done"], 1)
                if i == 0:
                    wait(dve, S["xn1_ready"], TILES * b)
                dve.wait_ge(S["sum_done"], n + 1)
                dve.bn_stats(stats1[:, i, :], x1[:, i, 0:D]).then_inc(S["stats1_made"], 1)
                wait_apart(dve, S["stats1_made"], TILES * b + i + 1, passed)
                dve.bn_aggr(moments1[:, i, :], stats1[:, i, :]).then_inc(S["moments1_made"], 1)

            dve.memset(keep["counts"][:], 0.0).then_inc(S["counted"], 1)
            dve.wait_ge(S["counted"], 1)
            dve.wait_ge(S["rows_loaded"], 16 * 3)
            dve.tensor_scalar(bo_row[:], bo_row[:], consts["gates"][:, 0:1], None, ALU.mult).then_inc(S["row_scaled"], 1)
            for i in range(TILES):
                tile_stats(0, 0, i)
            batch_moments(0)
            x_lo(Ring(0), 0)

            def iteration(b, odd, route, attend, prefetch):
                s, r, p = sum_ring(b), turn_ring(b), b - 1
                if route:
                    routed_lo(r, p, 0)
                if attend:
                    query_lo(s, b, 0)
                if route:
                    routed_lo(r, p, 1)
                    at = gate_logits(s, p, 0)
                    routed_lo(r, p, 2)
                    gate_best(p, 0, at)
                    at = gate_logits(s, p, 1)
                if attend:
                    peaks(b, 0)
                if route:
                    gate_best(p, 1, at)
                if attend:
                    query_lo(s, b, 1)
                if prefetch:
                    tile_stats(b + 1, 1 - odd, 0)
                    tile_stats(b + 1, 1 - odd, 1)
                if attend:
                    share_values(b, 0)
                if route:
                    at = gate_logits(s, p, 2)
                if attend:
                    out_lo(r, b, 0)
                    peaks(b, 1)
                if route:
                    routed_lo(r, p, 3)
                    gate_best(p, 2, at)
                if attend:
                    query_lo(s, b, 2)
                if prefetch:
                    tile_stats(b + 1, 1 - odd, 2)
                    tile_stats(b + 1, 1 - odd, 3)
                    batch_moments(b + 1)
                if attend:
                    share_values(b, 1)
                if route:
                    at = gate_logits(s, p, 3)
                if attend:
                    out_lo(r, b, 1)
                    peaks(b, 2)
                if route:
                    gate_best(p, 3, at)
                    choose(p)
                if attend:
                    query_lo(s, b, 3)
                    share_values(b, 2)
                if route:
                    place_rows(s, p, s.start)
                    chances(p)
                if attend:
                    out_lo(r, b, 2)
                if prefetch:
                    x_lo(r, b + 1)
                if attend:
                    peaks(b, 3)
                    share_values(b, 3)
                    out_lo(r, b, 3)
                    for i in range(TILES):
                        add_up(s, b, odd, i)

            iterations(dve, iteration)
            dve.wait_ge(S["place_kept"], BATCHES)

        @block.gpsimd
        def _(pool):
            pool.memset(half[:], -0.5).then_inc(S["filled"], 1)
            pool.wait_ge(S["filled"], 1)

            def normalize(b, odd):
                wait_apart(pool, S["moments_made"], TILES * (b + 1), passed)
                pool.tensor_scalar(spread[:], moments[:, :, 1], EPS, None, ALU.add).then_inc(S["spread_made"], 1)
                pool.tensor_scalar(offset[:], moments[:, :, 0], -1.0, None, ALU.mult).then_inc(S["mean_turned"], 1)
                pool.wait_ge(S["spread_made"], b + 1)
                pool.tensor_tensor(istd[:], spread[:], half[:], ALU.pow).then_inc(S["istd_made"], 1)
                pool.wait_ge(S["mean_turned"], b + 1)
                pool.wait_ge(S["istd_made"], b + 1)
                pool.tensor_tensor(offset[:], offset[:], istd[:], ALU.mult).then_inc(S["offset_made"], 1)
                wait_apart(pool, S["offset_made"], b + 1, passed)
                wait_apart(pool, S["x_hi"], TILES * b, passed)
                for i in range(TILES):
                    pool.tensor_scalar(xn[:, i, :], x[:, odd, i, :], istd[:, i:i + 1], offset[:, i:i + 1],
                                       ALU.mult, ALU.add).then_inc(S["xn_ready"], 1)
                pool.wait_ge(S["row_scaled"], 1)

            def add_bias(b, odd):
                for i in range(TILES):
                    pool.wait_ge(S["xn_ready"], TILES * b + i + 1)
                    pool.tensor_tensor(x[:, odd, i, :], x[:, odd, i, :], bo_row[:], ALU.add
                                       ).then_inc(S["x_biased"], 1)

            def normalize_routed(b, i):
                n = TILES * b + i + 1
                wait_apart(pool, S["moments1_made"], n, passed)
                pool.tensor_scalar(spread1[:, i:i + 1], moments1[:, i, 1:2], EPS, None, ALU.add).then_inc(S["spread1_made"], 1)
                pool.tensor_scalar(minus_mean1[:, i:i + 1], moments1[:, i, 0:1], -1.0, None, ALU.mult).then_inc(S["mean1_turned"], 1)
                pool.wait_ge(S["spread1_made"], n)
                pool.tensor_tensor(x1[:, i, D:D + 1], spread1[:, i:i + 1], half[:, 0:1], ALU.pow).then_inc(S["istd1_made"], 1)
                pool.wait_ge(S["mean1_turned"], n)
                pool.wait_ge(S["istd1_made"], n)
                pool.tensor_tensor(x1[:, i, D + 1:D + 2], minus_mean1[:, i:i + 1], x1[:, i, D:D + 1], ALU.mult
                                   ).then_inc(S["offset1_made"], 1)
                wait_apart(pool, S["offset1_made"], n, passed)
                pool.tensor_scalar(xn1[:, i, :], x1[:, i, 0:D], x1[:, i, D:D + 1], x1[:, i, D + 1:D + 2],
                                   ALU.mult, ALU.add).then_inc(S["xn1_ready"], 1)

            def scatter(b):
                pool.wait_ge(S["placed"], b + 1)
                wait_apart(pool, S["chance_made"], 2 * (b + 1), passed)
                for i in range(TILES):
                    pool.indirect_dma_start(t["routed"], bass.IndirectOffsetOnAxis(ap=place[:, i:i + 1], axis=0),
                                            x1[:, i, :], None).then_inc(S["scattered"], 16)

            normalize(0, 0)
            add_bias(0, 0)

            def iteration(b, odd, route, attend, prefetch):
                if prefetch:
                    normalize(b + 1, 1 - odd)
                if route:
                    scatter(b - 1)
                if prefetch:
                    add_bias(b + 1, 1 - odd)
                if attend:
                    for i in range(TILES):
                        normalize_routed(b, i)

            iterations(pool, iteration)
            pool.wait_ge(S["scattered"], 16 * TILES * BATCHES)


PLACES = BATCHES * TILES
SLOTS = BATCHES * TILES + EXPERTS


def run_experts(nc, t, consts, keep):
    with ExitStack() as ctx:
        mem = Memory(nc, ctx, "experts_")
        AHEAD, BUFFERS = 3, 4
        padded, padded_tiles = mem.sbuf("padded", [P, EXPERTS], I32), mem.sbuf("padded_tiles", [P, EXPERTS], I32)
        tiles, ends, stride = [mem.sbuf(n, [P, EXPERTS]) for n in ("tiles", "ends", "stride")]
        slot_i, slot = mem.sbuf("slot_i", [P, SLOTS], I32), mem.sbuf("slot", [P, SLOTS])
        past, past_rows = mem.sbuf("past", [P, SLOTS, EXPERTS]), mem.sbuf("past_rows", [P, SLOTS, EXPERTS])
        expert, row = mem.sbuf("expert", [P, SLOTS]), mem.sbuf("row", [P, SLOTS])
        expert_of, row_of = mem.sbuf("expert_of", [P, SLOTS], I32), mem.sbuf("row_of", [P, SLOTS], I32)
        routed_at, moved_by = mem.sbuf("routed_at", [P, PLACES]), mem.sbuf("moved_by", [P, PLACES])
        moves = mem.sbuf("moves", [P, PLACES, EXPERTS - 1])
        pad_at, zeros = mem.sbuf("pad_at", [P, EXPERTS], U32), mem.sbuf("zeros", [P, ROW])

        raw = [mem.sbuf(f"raw{i}", [P, CHUNKS, D]) for i in range(2)]
        w = [mem.sbuf(f"w_{h}", [P, EXPERTS, CHUNKS, D], F32R) for h in ("hi", "lo")]
        be_rows = mem.sbuf("be_rows", [P, EXPERTS, D])
        x = [mem.sbuf(f"x{i}", [P, ROW]) for i in range(BUFFERS)]
        xn = [mem.sbuf(f"xn{i}", [P, D]) for i in range(2)]
        x_t = [[mem.sbuf(f"x_t{i}_{h}", [P, CHUNKS, P], F32R) for h in ("hi", "lo")] for i in range(2)]
        before, after = [[mem.sbuf(f"{n}{i}", [P, D]) for i in range(2)] for n in ("before", "after")]
        turns, sums = mem.psum("turns", [P, 2, CHUNKS, P]), mem.psum("sums", [P, 2, D])

        planned, slots_made, zeros_made, pads_placed, pads_written = [mem.sem(n) for n in (
            "planned", "slots_made", "zeros_made", "pads_placed", "pads_written")]
        raw_loaded = [mem.sem(f"raw_loaded{i}") for i in range(2)]
        rows_loaded, weight_hi, weight_lo = mem.sem("rows_loaded"), mem.sem("weight_hi"), mem.sem("weight_lo")
        loaded = [mem.sem(f"loaded{i}") for i in range(BUFFERS)]
        stored = [mem.sem(f"stored{i}") for i in range(BUFFERS)]
        normalized, turned, turned_hi, turned_lo = [mem.sem(n) for n in (
            "normalized", "turned", "turned_hi", "turned_lo")]
        summed, biased, clipped, mixed = [mem.sem(n) for n in ("summed", "biased", "clipped", "mixed")]
        PLAN = 12
        moved = mem.sem("moved")

        passed = consts["passed"]
        ctx.callback(mem.clear_semaphores)
        block = ctx.enter_context(nc.Block())

        def tiles_in_turn(eng, tile):
            rounds = SLOTS // BUFFERS
            with eng.Fori(0, rounds - 1) as i:
                for k in range(BUFFERS):
                    tile(i, k, BUFFERS)
            for k in range(BUFFERS):
                tile(rounds - 1, k, BUFFERS - 1 - k)

        def expert_weights(e):
            return t["L0_ffn_We"][e].rearrange("(c p) n -> p c n", p=P)

        @block.gpsimd
        def _(pool):
            pool.iota(slot_i[:], [[1, SLOTS]], base=0, channel_multiplier=0).then_inc(slots_made, 1)
            pool.memset(zeros[:], 0.0).then_inc(zeros_made, 1)
            for e in range(2):
                pool.dma_start(raw[e][:], expert_weights(e)).then_inc(raw_loaded[e], 16)
            pool.wait_ge(zeros_made, 1)
            for e in range(EXPERTS):
                pool.dma_start(t["routed"][EXPERTS * REGION + e * P:EXPERTS * REGION + (e + 1) * P, :], zeros[:]
                               ).then_inc(pads_written, 16)
            pool.wait_ge(pads_placed, 1)
            for e in range(EXPERTS):
                pool.indirect_dma_start(t["routed"], bass.IndirectOffsetOnAxis(ap=pad_at[:, e:e + 1], axis=0),
                                        zeros[:], None).then_inc(pads_written, 16)
            for e in range(2, EXPERTS):
                pool.wait_ge(weight_lo, e - 1)
                pool.dma_start(raw[e % 2][:], expert_weights(e)).then_inc(raw_loaded[e % 2], 16)

        @block.sync
        def _(sp):
            def place_of(n):
                at = sp.value_load(row_of[0:1, bass.ds(n, 1)], min_val=0, max_val=EXPERTS * (REGION + P) - P)
                return t["routed"][bass.ds(at, P), :]

            def load(n, k):
                sp.dma_start(x[k][:], place_of(n)).then_inc(loaded[k], 16)

            def tile(i, k, left):
                n = i * BUFFERS + k
                if left >= AHEAD:
                    wait_apart(sp, stored[k - 1], 16 * (i + (k > 0)), passed)
                    load(n + AHEAD, (k + AHEAD) % BUFFERS)
                wait_apart(sp, mixed, n + 1, passed)
                sp.dma_start(results[bass.ds(n, 1)].squeeze(0), x[k][:, 0:D]).then_inc(stored[k], 16)

            results = t["results"].rearrange("(n p) d -> n p d", p=P)
            for e in range(EXPERTS):
                sp.dma_start(be_rows[:, e, :], t["L0_ffn_be"][e].partition_broadcast(P)).then_inc(rows_loaded, 16)
            sp.wait_ge(planned, PLAN)
            sp.wait_ge(pads_written, 16 * 2 * EXPERTS)
            for n in range(AHEAD):
                load(n, n)
            tiles_in_turn(sp, tile)
            for k in range(BUFFERS):
                sp.wait_ge(stored[k], 16 * SLOTS // BUFFERS)

        @block.vector
        def _(dve):
            def step(ins, n):
                ins.then_inc(planned, 1)
                dve.wait_ge(planned, n)

            def wide(small):
                return small.unsqueeze(1).broadcast_to([P, SLOTS, EXPERTS])

            counts = keep["counts"]
            dve.tensor_tensor(pad_at[:], consts["own"][:], counts[:], ALU.add).then_inc(pads_placed, 1)
            step(dve.tensor_scalar(padded[:], counts[:], float(P - 1), None, ALU.add), 1)
            step(dve.tensor_scalar(padded_tiles[:], padded[:], P.bit_length() - 1, None, ALU.arith_shift_right), 2)
            step(dve.tensor_copy(tiles[:], padded_tiles[:]), 3)
            dve.tensor_scalar(stride[:], tiles[:], -float(P), float(REGION), ALU.mult, ALU.add).then_inc(planned, 1)
            dve.wait_ge(planned, 4)
            step(dve.tensor_tensor_scan(ends[:], tiles[:], tiles[:], 0.0, ALU.add, ALU.bypass), 5)
            dve.wait_ge(slots_made, 1)
            step(dve.tensor_copy(slot[:], slot_i[:]), 6)
            step(dve.tensor_tensor(past[:], slot[:].unsqueeze(2).broadcast_to([P, SLOTS, EXPERTS]), wide(ends[:]),
                                   ALU.is_ge), 7)
            step(dve.tensor_reduce(expert[:], past[:], AX_X, ALU.add), 8)
            step(dve.tensor_tensor(past_rows[:], past[:], wide(stride[:]), ALU.mult), 9)
            step(dve.tensor_reduce(row[:], past_rows[:], AX_X, ALU.add), 10)
            dve.tensor_scalar(expert_of[:], expert[:], float(EXPERTS - 1), None, ALU.min).then_inc(planned, 1)
            dve.scalar_tensor_tensor(row_of[:], slot[:], float(P), row[:], ALU.mult, ALU.add).then_inc(planned, 1)

            dve.tensor_copy(routed_at[:], keep["places"][:]).then_inc(moved, 1)
            dve.wait_ge(moved, 1)
            for e in range(EXPERTS - 1):
                dve.tensor_scalar(moves[:, :, e], routed_at[:], float((e + 1) * REGION), stride[:, e:e + 1],
                                  ALU.is_ge, ALU.mult).then_inc(moved, 1)
            dve.wait_ge(moved, EXPERTS)
            dve.tensor_reduce(moved_by[:], moves[:], AX_X, ALU.add).then_inc(moved, 1)
            dve.wait_ge(moved, EXPERTS + 1)
            dve.tensor_tensor(keep["places"][:], routed_at[:], moved_by[:], ALU.subtract).then_inc(moved, 1)
            dve.wait_ge(moved, EXPERTS + 2)

            for e in range(EXPERTS):
                dve.wait_ge(weight_hi, e + 1)
                dve.tensor_tensor(w[1][:, e], raw[e % 2][:], w[0][:, e].bitcast(F32), ALU.subtract
                                  ).then_inc(weight_lo, 1)
            dve.wait_ge(rows_loaded, 16 * EXPERTS)

            def turn_lo(n, k):
                dve.wait_ge(turned_hi, n + 1)
                hi, lo = x_t[k % 2]
                dve.tensor_tensor(lo[:], turns[:, k % 2], hi[:].bitcast(F32), ALU.subtract).then_inc(turned_lo, 1)

            turn_lo(0, 0)

            def tile(i, k, left):
                n = i * BUFFERS + k
                if left:
                    turn_lo(n + 1, k + 1)
                e = dve.value_load(expert_of[0:1, bass.ds(n, 1)], min_val=0, max_val=EXPERTS - 1)
                dve.wait_ge(summed, n + 1)
                wait(dve, clipped, n - 1 if isinstance(n, int) or k > 0 else n)
                dve.tensor_tensor(before[k % 2][:], sums[:, k % 2, :], be_rows[:, bass.ds(e, 1), :].squeeze(1), ALU.add
                                  ).then_inc(biased, 1)
                dve.wait_ge(clipped, n + 1)
                dve.scalar_tensor_tensor(x[k][:, 0:D], after[k % 2][:], x[k][:, D + 2:D + 3], x[k][:, 0:D],
                                         ALU.mult, ALU.add).then_inc(mixed, 1)

            tiles_in_turn(dve, tile)

        @block.scalar
        def _(act):
            for e in range(EXPERTS):
                act.wait_ge(raw_loaded[e % 2], 16 * (e // 2 + 1))
                act.activation(w[0][:, e], raw[e % 2][:], ACT.Copy).then_inc(weight_hi, 1)

            def normalize(loads, n, k):
                act.wait_ge(loaded[k], 16 * loads)
                act.activation(xn[k % 2][:], x[k][:, 0:D], ACT.Identity, bias=x[k][:, D + 1:D + 2],
                               scale=x[k][:, D:D + 1]).then_inc(normalized, 1)

            def turn_hi(n, k):
                act.wait_ge(turned, n + 1)
                act.activation(x_t[k % 2][0][:], turns[:, k % 2], ACT.Copy).then_inc(turned_hi, 1)

            normalize(1, 0, 0)
            normalize(1, 1, 1)
            turn_hi(0, 0)

            def tile(i, k, left):
                n = i * BUFFERS + k
                if left:
                    turn_hi(n + 1, k + 1)
                if left > 1:
                    normalize(i + 1 + (k + 2) // BUFFERS, n + 2, (k + 2) % BUFFERS)
                act.wait_ge(biased, n + 1)
                wait(act, mixed, n - 1 if isinstance(n, int) or k > 0 else n)
                act.activation(after[k % 2][:], before[k % 2][:], ACT.Relu).then_inc(clipped, 1)

            tiles_in_turn(act, tile)

        @block.tensor
        def _(pe):
            def turn(n, k):
                pe.wait_ge(normalized, n + 1)
                for c in range(CHUNKS):
                    last = pe.transpose(turns[:, k % 2, c, :], xn[k % 2][:, c * P:(c + 1) * P], consts["ident"][:])
                last.then_inc(turned, 1)

            pe.wait_ge(planned, PLAN)
            turn(0, 0)
            pe.wait_ge(weight_lo, EXPERTS)

            def tile(i, k, left):
                n = i * BUFFERS + k
                if left:
                    turn(n + 1, k + 1)
                e = pe.value_load(expert_of[0:1, bass.ds(n, 1)], min_val=0, max_val=EXPERTS - 1)
                pe.wait_ge(turned_lo, n + 1)
                wait(pe, biased, n - 1 if isinstance(n, int) or k > 0 else n)
                for c in range(CHUNKS):
                    last = three_pass(pe, sums[:, k % 2, :], [h[:, c, :] for h in x_t[k % 2]],
                                      [h[:, bass.ds(e, 1), c, :].squeeze(1) for h in w], c == 0, c == CHUNKS - 1)
                last.then_inc(summed, 1)

            tiles_in_turn(pe, tile)


WEIGHT_COUNT = float(D * D)
ROUNDER = 1.5 * 2 ** 23


def quantize_weights(nc, t, consts, keep):
    with ExitStack() as ctx:
        mem = Memory(nc, ctx, "quantize_")
        w = mem.sbuf("w", [P, CHUNKS, D])
        above, below = mem.sbuf("above", [P, CHUNKS, D]), mem.sbuf("below", [P, CHUNKS, D])
        ternary = mem.sbuf("ternary", [P, CHUNKS, D], BF16)
        magnitude, total, threshold = [mem.sbuf(n, [P, 1]) for n in ("magnitude", "total", "threshold")]
        turns = mem.psum("turns", [P, CHUNKS, 2 * D], BF16)
        loaded, magnitudes_summed, totalled, thresholds_made, compared, made, turned, kept = [mem.sem(n) for n in (
            "loaded", "magnitudes_summed", "totalled", "thresholds_made", "compared", "made", "turned", "kept")]
        ctx.callback(mem.clear_semaphores)
        with nc.Block() as block:
            @block.sync
            def _(sp):
                sp.dma_start(w[:], t["L1_ffn_weight"].rearrange("(c p) k -> p c k", p=P)).then_inc(loaded, 16)

            @block.gpsimd
            def _(pool):
                pool.wait_ge(magnitudes_summed, 1)
                pool.partition_all_reduce(total[:], magnitude[:], P, bass.bass_isa.ReduceOp.add).then_inc(totalled, 1)

            @block.vector
            def _(dve):
                dve.wait_ge(loaded, 16)
                dve.tensor_reduce(magnitude[:], w[:], mybir.AxisListType.XY, ALU.add, apply_absolute_value=True
                                  ).then_inc(magnitudes_summed, 1)
                dve.wait_ge(totalled, 1)
                dve.tensor_scalar(keep["w_scale"][:], total[:], 1 / WEIGHT_COUNT, None, ALU.mult).then_inc(thresholds_made, 1)
                dve.tensor_scalar(threshold[:], total[:], 0.5 / WEIGHT_COUNT, None, ALU.mult).then_inc(thresholds_made, 1)
                dve.wait_ge(thresholds_made, 2)
                dve.tensor_scalar(above[:], w[:], threshold[:], None, ALU.is_gt).then_inc(compared, 1)
                dve.tensor_scalar(below[:], w[:], -1.0, threshold[:], ALU.mult, ALU.is_gt).then_inc(compared, 1)
                dve.wait_ge(compared, 2)
                dve.tensor_tensor(ternary[:], above[:], below[:], ALU.subtract).then_inc(made, 1)

            @block.tensor
            def _(pe):
                pe.wait_ge(made, 1)
                pe.wait_ge(consts["ready"], consts["made"])
                for c in range(CHUNKS):
                    for o in range(CHUNKS):
                        last = pe.transpose(turns[:, c, o * P:(o + 1) * P], ternary[:, o, c * P:(c + 1) * P],
                                            consts["ident_half"][:])
                    last.then_inc(turned, 1)

            @block.scalar
            def _(act):
                for c in range(CHUNKS):
                    act.wait_ge(turned, c + 1)
                    act.activation(keep["ternary_t"][:, c, :], turns[:, c, 0:D], ACT.Copy).then_inc(kept, 1)
                act.wait_ge(kept, CHUNKS)


def attend_context(nc, t, consts, keep, x3):
    with ExitStack() as ctx:
        mem = Memory(nc, ctx, "context_")
        BUFFERS = 3
        place = [mem.sbuf(f"place{i}", [P, TILES], U32) for i in range(2)]
        x = [mem.sbuf(f"x{i}", [P, TILES, D]) for i in range(BUFFERS)]
        stats, moments = mem.sbuf("stats", [P, TILES, 6]), mem.sbuf("moments", [P, TILES, 2])
        stats3, moments3 = mem.sbuf("stats3", [P, TILES, 6]), mem.sbuf("moments3", [P, TILES, 2])
        spread, istd, offset, half = [mem.sbuf(n, [P, TILES]) for n in ("spread", "istd", "offset", "half")]
        spread3 = mem.sbuf("spread3", [P, TILES])
        istd3, offset3 = [[mem.sbuf(f"{n}{i}", [P, TILES]) for i in range(2)] for n in ("istd3_", "offset3_")]
        xn = mem.sbuf("xn", [P, TILES, D])
        x_t = [mem.sbuf(f"x_t_{h}", [P, CHUNKS, SEQ], F32R) for h in ("hi", "lo")]
        keys = mem.sbuf("keys", [P, 2, CHUNKS, KEYS], F32R)
        key_bias = mem.sbuf("key_bias", [P, 1])
        values = mem.sbuf("values", [P, 2, D], F32R)
        scores = mem.sbuf("scores", [P, SEQ])
        peak, minus_peak = mem.sbuf("peak", [P, TILES]), mem.sbuf("minus_peak", [P, TILES])
        probs = mem.sbuf("probs", [P, TILES, KEYS])
        total = mem.sbuf("total", [P, TILES])
        share, gain = mem.sbuf("share", [P, TILES]), mem.sbuf("gain", [P, TILES])
        probs_t = [mem.sbuf(f"probs_t_{h}", [P, SEQ], F32R) for h in ("hi", "lo")]
        x3n = [mem.sbuf(f"x3n{i}", [P, D]) for i in range(2)]
        largest = mem.sbuf("largest", [P, TILES])

        score_bank, score_turns, prob_turns = mem.psum("score_bank", [P, SEQ]), mem.psum("score_turns", [P, TILES, P]), \
            mem.psum("prob_turns", [P, TILES, P])
        turns, sums = mem.psum("turns", [P, 2, CHUNKS, P]), mem.psum("sums", [P, 2, D])

        S = {n: mem.sem(n) for n in (
            "filled", "placed", "gathered", "keys_loaded", "bias_loaded", "values_loaded",
            "stats_made", "moments_made", "spread_made", "mean_turned", "istd_made", "offset_made", "xn_ready",
            "turned", "turned_hi", "turned_lo", "scored", "scores_ready", "scores_turned", "peaked", "peak_turned",
            "weighed", "probs_turned", "probs_hi", "probs_lo", "inverted", "gain_made", "attended", "mixed",
            "stats3_made", "moments3_made", "spread3_made", "mean3_turned", "istd3_made", "offset3_made",
            "x3n_ready", "largest_made", "largest_kept", "moments3_kept")}
        passed = consts["passed"]
        LEAD = 2

        def rounds(eng, iteration):
            def at(j):
                iteration(j, j, score=j < BATCHES, turn=j + 1 < BATCHES, fetch=j + 2 < BATCHES,
                          mix=1 <= j <= BATCHES, measure=j >= LEAD)

            for j in range(LEAD):
                at(j)
            step = 2 * BUFFERS
            with eng.Fori(0, (BATCHES - 2 - LEAD) // step) as i:
                for k in range(step):
                    iteration(i * step + LEAD + k, LEAD + k, score=True, turn=True, fetch=True, mix=True, measure=True)
            for j in range(BATCHES - 2, BATCHES + LEAD):
                at(j)

        block = ctx.enter_context(nc.Block())

        @block.sync
        def _(sp):
            def load_keys(b):
                sp.dma_start(keys[:].bitcast(F32), t["fold_pairs"][b]).then_inc(S["keys_loaded"], 16)

            def load_bias(b):
                sp.dma_start(key_bias[0:KEYS], t["fold_biases"][b]).then_inc(S["bias_loaded"], 16)

            load_keys(0)
            load_bias(0)

            def iteration(j, k, score, turn, fetch, mix, measure):
                if turn:
                    wait_apart(sp, S["scored"], j + 1, passed)
                    load_keys(j + 1)
                    wait_apart(sp, S["scores_ready"], j + 1, passed)
                    load_bias(j + 1)
                if score:
                    wait_apart(sp, S["attended"], TILES * j, passed)
                    sp.dma_start(values[0:KEYS].bitcast(F32), t["v1_pairs"][j]).then_inc(S["values_loaded"], 16)

            rounds(sp, iteration)

        @block.gpsimd
        def _(pool):
            def gather(b, k):
                wait_apart(pool, S["gathered"], 16 * TILES * b, passed)
                pool.tensor_copy(place[k % 2][:], keep["places"][:, bass.ds(TILES * b, TILES)]).then_inc(S["placed"], 1)
                wait(pool, S["mixed"], max(TILES * (b - 2), 0) if isinstance(b, int) else TILES * (b - 2))
                wait_apart(pool, S["placed"], b + 1, passed)
                for i in range(TILES):
                    pool.indirect_dma_start(x[k % BUFFERS][:, i, :], None, t["results"],
                                            bass.IndirectOffsetOnAxis(ap=place[k % 2][:, i:i + 1], axis=0)
                                            ).then_inc(S["gathered"], 16)

            def scale_of(b, moments, spread, istd, offset, names):
                moments_made, spread_made, mean_turned, istd_made, offset_made = [S[n] for n in names]
                wait_apart(pool, moments_made, TILES * (b + 1), passed)
                pool.tensor_scalar(spread[:], moments[:, :, 1], EPS, None, ALU.add).then_inc(spread_made, 1)
                pool.tensor_scalar(offset[:], moments[:, :, 0], -1.0, None, ALU.mult).then_inc(mean_turned, 1)
                pool.wait_ge(spread_made, b + 1)
                pool.tensor_tensor(istd[:], spread[:], half[:], ALU.pow).then_inc(istd_made, 1)
                pool.wait_ge(mean_turned, b + 1)
                pool.wait_ge(istd_made, b + 1)
                pool.tensor_tensor(offset[:], offset[:], istd[:], ALU.mult).then_inc(offset_made, 1)

            def normalize(b, k):
                scale_of(b, moments, spread, istd, offset,
                         ("moments_made", "spread_made", "mean_turned", "istd_made", "offset_made"))
                wait(pool, S["turned"], TILES * b)
                wait_apart(pool, S["offset_made"], b + 1, passed)
                for i in range(TILES):
                    pool.tensor_scalar(xn[:, i, :], x[k % BUFFERS][:, i, :], istd[:, i:i + 1], offset[:, i:i + 1],
                                       ALU.mult, ALU.add).then_inc(S["xn_ready"], 1)

            pool.memset(half[:], -0.5).then_inc(S["filled"], 1)
            pool.wait_ge(S["filled"], 1)
            gather(0, 0)
            gather(1, 1)
            normalize(0, 0)
            normalize(1, 1)

            def iteration(j, k, score, turn, fetch, mix, measure):
                if fetch:
                    gather(j + 2, k + 2)
                if mix:
                    if not (isinstance(j, int) and j < LEAD):
                        wait_apart(pool, S["x3n_ready"], TILES * (j - 2), passed)
                        wait_apart(pool, S["moments3_kept"], 2 * (j - 2), passed)
                    scale_of(j - 1, moments3, spread3, istd3[(k - 1) % 2], offset3[(k - 1) % 2],
                             ("moments3_made", "spread3_made", "mean3_turned", "istd3_made", "offset3_made"))
                if fetch:
                    normalize(j + 2, k + 2)

            rounds(pool, iteration)

        @block.tensor
        def _(pe):
            def turn_x(b):
                for i in range(TILES):
                    n = TILES * b + i
                    pe.wait_ge(S["xn_ready"], n + 1)
                    if not (isinstance(n, int) and n < 2):
                        pe.wait_ge(S["turned_lo"], n - 1)
                    for c in range(CHUNKS):
                        last = pe.transpose(turns[:, i % 2, c, :], xn[:, i, c * P:(c + 1) * P], consts["ident"][:])
                    last.then_inc(S["turned"], 1)

            turn_x(0)

            def iteration(j, k, score, turn, fetch, mix, measure):
                if score:
                    pe.wait_ge(S["turned_lo"], TILES * (j + 1))
                    pe.wait_ge(S["keys_loaded"], 16 * (j + 1))
                    wait(pe, S["scores_ready"], j)
                    for c in range(CHUNKS):
                        last = three_pass(pe, score_bank[0:KEYS, :], [keys[:, h, c, :] for h in range(2)],
                                          [h[:, c, :] for h in x_t], c == 0, c == CHUNKS - 1)
                    last.then_inc(S["scored"], 1)
                if turn:
                    turn_x(j + 1)
                if score:
                    pe.wait_ge(S["scores_ready"], j + 1)
                    wait(pe, S["weighed"], TILES * j)
                    for i in range(TILES):
                        last = pe.transpose(score_turns[:, i, 0:KEYS], scores[0:KEYS, i * P:(i + 1) * P],
                                            consts["ident"][0:KEYS, 0:KEYS])
                    last.then_inc(S["scores_turned"], 1)
                if mix:
                    pe.wait_ge(S["probs_lo"], j)
                    pe.wait_ge(S["values_loaded"], 16 * j)
                    for i in range(TILES):
                        n = TILES * (j - 1) + i
                        if not (isinstance(n, int) and n < 2):
                            pe.wait_ge(S["mixed"], n - 1)
                        three_pass(pe, sums[:, i % 2, :], [h[0:KEYS, i * P:(i + 1) * P] for h in probs_t],
                                   [values[0:KEYS, h, :] for h in range(2)]).then_inc(S["attended"], 1)
                if score:
                    pe.wait_ge(S["weighed"], TILES * (j + 1))
                    for i in range(TILES):
                        last = pe.transpose(prob_turns[0:KEYS, i, :], probs[:, i, :], consts["ident"][:])
                    last.then_inc(S["probs_turned"], 1)

            rounds(pe, iteration)

        @block.scalar
        def _(act):
            def turn_hi(b):
                for i in range(TILES):
                    act.wait_ge(S["turned"], TILES * b + i + 1)
                    act.activation(x_t[0][:, :, i * P:(i + 1) * P], turns[:, i % 2], ACT.Copy).then_inc(S["turned_hi"], 1)

            turn_hi(0)

            def iteration(j, k, score, turn, fetch, mix, measure):
                if score:
                    act.wait_ge(S["bias_loaded"], 16 * (j + 1))
                    wait(act, S["scores_turned"], j)
                    act.wait_ge(S["scored"], j + 1)
                    act.activation(scores[0:KEYS, :], score_bank[0:KEYS, :], ACT.Identity, bias=key_bias[0:KEYS, :],
                                   scale=D ** -0.5).then_inc(S["scores_ready"], 1)
                if turn:
                    turn_hi(j + 1)
                if score:
                    act.wait_ge(S["peak_turned"], j + 1)
                    wait(act, S["probs_turned"], j)
                    wait(act, S["inverted"], j)
                    for i in range(TILES):
                        act.activation(probs[:, i, :], score_turns[:, i, 0:KEYS], ACT.Exp, bias=minus_peak[:, i:i + 1],
                                       accum_out=total[:, i:i + 1]).then_inc(S["weighed"], 1)
                if measure:
                    for i in range(TILES):
                        n = TILES * (j - 2) + i
                        if not (isinstance(n, int) and n < 2):
                            act.wait_ge(S["largest_made"], n - min(i, 1))
                        wait_apart(act, S["offset3_made"], j - 1, passed)
                        act.activation(x3n[i % 2][:], x3[:, bass.ds(n, 1), :].squeeze(1), ACT.Identity,
                                       bias=offset3[k % 2][:, i:i + 1], scale=istd3[k % 2][:, i:i + 1]
                                       ).then_inc(S["x3n_ready"], 1)
                if score:
                    act.wait_ge(S["probs_turned"], j + 1)
                    wait(act, S["attended"], TILES * j)
                    act.activation(probs_t[0][0:KEYS, :], prob_turns[0:KEYS].rearrange("p i n -> p (i n)"), ACT.Copy
                                   ).then_inc(S["probs_hi"], 1)

            rounds(act, iteration)

        @block.vector
        def _(dve):
            def tile_stats(b, k):
                dve.wait_ge(S["gathered"], 16 * TILES * (b + 1))
                wait(dve, S["mean_turned"], b)
                wait(dve, S["spread_made"], b)
                for i in range(TILES):
                    dve.bn_stats(stats[:, i, :], x[k % BUFFERS][:, i, :]).then_inc(S["stats_made"], 1)
                for i in range(TILES):
                    wait_apart(dve, S["stats_made"], TILES * b + i + 1, passed)
                    dve.bn_aggr(moments[:, i, :], stats[:, i, :]).then_inc(S["moments_made"], 1)

            def turn_lo(b):
                for i in range(TILES):
                    dve.wait_ge(S["turned_hi"], TILES * b + i + 1)
                    hi, lo = [h[:, :, i * P:(i + 1) * P] for h in x_t]
                    dve.tensor_tensor(lo, turns[:, i % 2], hi.bitcast(F32), ALU.subtract).then_inc(S["turned_lo"], 1)

            tile_stats(0, 0)
            turn_lo(0)
            tile_stats(1, 1)

            def iteration(j, k, score, turn, fetch, mix, measure):
                if turn:
                    turn_lo(j + 1)
                if score:
                    dve.wait_ge(S["scores_turned"], j + 1)
                    dve.tensor_reduce(peak[:], score_turns[:, :, 0:KEYS], AX_X, ALU.max).then_inc(S["peaked"], 1)
                    dve.wait_ge(S["peaked"], j + 1)
                    dve.tensor_scalar(minus_peak[:], peak[:], -1.0, None, ALU.mult).then_inc(S["peak_turned"], 1)
                if mix:
                    wait(dve, S["spread3_made"], j - 1)
                    wait(dve, S["mean3_turned"], j - 1)
                    for i in range(TILES):
                        n = TILES * (j - 1) + i
                        dve.wait_ge(S["gain_made"], j)
                        dve.wait_ge(S["attended"], n + 1)
                        out = x3[:, bass.ds(n, 1), :].squeeze(1)
                        dve.scalar_tensor_tensor(out, sums[:, i % 2, :], gain[:, i:i + 1],
                                                 x[(k - 1) % BUFFERS][:, i, :], ALU.mult, ALU.add).then_inc(S["mixed"], 1)
                    for i in range(TILES):
                        n = TILES * (j - 1) + i
                        wait_apart(dve, S["mixed"], n + 1, passed)
                        dve.bn_stats(stats3[:, i, :], x3[:, bass.ds(n, 1), :].squeeze(1)).then_inc(S["stats3_made"], 1)
                if measure:
                    wait(dve, S["largest_kept"], j - 2 + 1)
                    for i in range(TILES):
                        dve.wait_ge(S["x3n_ready"], TILES * (j - 2) + i + 1)
                        dve.tensor_reduce(largest[:, i:i + 1], x3n[i % 2][:], AX_X, ALU.max, apply_absolute_value=True
                                          ).then_inc(S["largest_made"], 1)
                    wait_apart(dve, S["offset3_made"], j - 1, passed)
                    dve.tensor_copy(keep["istd3"][:, bass.ds(TILES * (j - 2), TILES)], istd3[k % 2][:]
                                    ).then_inc(S["moments3_kept"], 1)
                    dve.tensor_copy(keep["offset3"][:, bass.ds(TILES * (j - 2), TILES)], offset3[k % 2][:]
                                    ).then_inc(S["moments3_kept"], 1)
                if mix:
                    for i in range(TILES):
                        n = TILES * (j - 1) + i
                        wait_apart(dve, S["stats3_made"], n + 1, passed)
                        dve.bn_aggr(moments3[:, i, :], stats3[:, i, :]).then_inc(S["moments3_made"], 1)
                if measure:
                    dve.wait_ge(S["largest_made"], TILES * (j - 1))
                    dve.tensor_tensor(keep["largest"][:], keep["largest"][:], largest[:], ALU.max
                                      ).then_inc(S["largest_kept"], 1)
                if score:
                    dve.wait_ge(S["weighed"], TILES * (j + 1))
                    wait(dve, S["mixed"], TILES * j)
                    dve.reciprocal(share[:], total[:]).then_inc(S["inverted"], 1)
                    dve.wait_ge(S["inverted"], j + 1)
                    dve.tensor_scalar(gain[:], share[:], consts["gates"][:, 1:2], None, ALU.mult).then_inc(S["gain_made"], 1)
                    dve.wait_ge(S["probs_hi"], j + 1)
                    dve.tensor_tensor(probs_t[1][0:KEYS, :], prob_turns[0:KEYS].rearrange("p i n -> p (i n)"),
                                      probs_t[0][0:KEYS, :].bitcast(F32), ALU.subtract).then_inc(S["probs_lo"], 1)
                if fetch:
                    tile_stats(j + 2, k + 2)

            dve.memset(keep["largest"][:], 0.0).then_inc(S["largest_kept"], 1)
            rounds(dve, iteration)


def quantized_layer(nc, t, consts, keep, x3):
    with ExitStack() as ctx:
        mem = Memory(nc, ctx, "quantized_")
        COUNT = BATCHES * TILES
        ROUND = 4
        bias_row = mem.sbuf("bias_row", [P, D])
        top, largest, unit, per_unit, gain = [mem.sbuf(n, [P, 1]) for n in ("top", "largest", "unit", "per_unit", "gain")]
        scale, offset = mem.sbuf("scale", [P, COUNT]), mem.sbuf("offset", [P, COUNT])
        scaled = [mem.sbuf(f"scaled{i}", [P, D]) for i in range(2)]
        whole = [mem.sbuf(f"whole{i}", [P, D], BF16) for i in range(2)]
        whole_t = [mem.sbuf(f"whole_t{i}", [P, CHUNKS, P], BF16) for i in range(2)]
        turns = mem.psum("turns", [P, 2, 2 * D], BF16)
        sums = mem.psum("sums", [P, 2, D])
        S = {n: mem.sem(n) for n in ("row_loaded", "row_scaled", "step", "reduced", "scaled", "rounded", "turned", "turned_kept",
                                     "summed", "biased", "mixed", "stored")}
        passed = consts["passed"]

        def tiles_in_turn(eng, tile):
            with eng.Fori(0, COUNT // ROUND - 1) as i:
                for k in range(ROUND):
                    tile(i * ROUND + k, k, ROUND)
            for k in range(ROUND):
                tile(COUNT - ROUND + k, k, ROUND - 1 - k)

        def row(n):
            return x3[:, bass.ds(n, 1), :].squeeze(1)

        block = ctx.enter_context(nc.Block())

        @block.sync
        def _(sp):
            sp.dma_start(bias_row[:], t["L1_ffn_bias"].partition_broadcast(P)).then_inc(S["row_loaded"], 16)
            out = t["out"].rearrange("b (i p) d -> (b i) p d", p=P)

            def tile(n, k, left):
                wait_apart(sp, S["mixed"], n + 1, passed)
                sp.dma_start(out[bass.ds(n, 1)].squeeze(0), row(n)).then_inc(S["stored"], 16)

            tiles_in_turn(sp, tile)
            sp.wait_ge(S["stored"], 16 * COUNT)

        @block.gpsimd
        def _(pool):
            pool.wait_ge(S["step"], 1)
            pool.partition_all_reduce(largest[:], top[:], P, bass.bass_isa.ReduceOp.max).then_inc(S["reduced"], 1)
            pool.wait_ge(S["row_scaled"], 1)

            def tile(n, k, left):
                wait_apart(pool, S["scaled"], n + 1, passed)
                pool.tensor_tensor(row(n), row(n), bias_row[:], ALU.add).then_inc(S["biased"], 1)

            tiles_in_turn(pool, tile)

        @block.vector
        def _(dve):
            dve.tensor_reduce(top[:], keep["largest"][:], AX_X, ALU.max).then_inc(S["step"], 1)
            dve.wait_ge(S["row_loaded"], 16)
            dve.tensor_scalar(bias_row[:], bias_row[:], consts["gates"][:, 3:4], None, ALU.mult).then_inc(S["row_scaled"], 1)
            dve.wait_ge(S["reduced"], 1)
            dve.tensor_scalar(unit[:], largest[:], 1 / 127.0, None, ALU.mult).then_inc(S["step"], 1)
            dve.wait_ge(S["step"], 2)
            dve.reciprocal(per_unit[:], unit[:]).then_inc(S["step"], 1)
            dve.tensor_scalar(gain[:], unit[:], keep["w_scale"][:], consts["gates"][:, 3:4], ALU.mult, ALU.mult
                              ).then_inc(S["step"], 1)
            dve.wait_ge(S["step"], 4)
            dve.tensor_scalar(scale[:], keep["istd3"][:], per_unit[:], None, ALU.mult).then_inc(S["step"], 1)
            dve.tensor_scalar(offset[:], keep["offset3"][:], per_unit[:], None, ALU.mult).then_inc(S["step"], 1)
            dve.wait_ge(S["step"], 6)

            def scale_tile(n, k):
                wait(dve, S["rounded"], n - 1 if not isinstance(n, int) else max(n - 1, 0))
                dve.tensor_scalar(scaled[k % 2][:], row(n), scale[:, bass.ds(n, 1)], offset[:, bass.ds(n, 1)],
                                  ALU.mult, ALU.add).then_inc(S["scaled"], 1)

            def round_tile(n, k):
                wait(dve, S["turned"], n - 1 if not isinstance(n, int) else max(n - 1, 0))
                dve.wait_ge(S["scaled"], n + 1)
                dve.tensor_scalar(whole[k % 2][:], scaled[k % 2][:], ROUNDER, ROUNDER, ALU.add, ALU.subtract
                                  ).then_inc(S["rounded"], 1)

            for n in range(2):
                scale_tile(n, n)
                round_tile(n, n)

            def tile(n, k, left):
                if left > 1:
                    scale_tile(n + 2, k + 2)
                dve.wait_ge(S["biased"], n + 1)
                dve.wait_ge(S["summed"], n + 1)
                dve.scalar_tensor_tensor(row(n), sums[:, k % 2, :], gain[:], row(n), ALU.mult, ALU.add
                                         ).then_inc(S["mixed"], 1)
                if left > 1:
                    round_tile(n + 2, k + 2)

            tiles_in_turn(dve, tile)

        @block.tensor
        def _(pe):
            def turn(n, k):
                pe.wait_ge(S["rounded"], n + 1)
                wait(pe, S["turned_kept"], n - 1 if not isinstance(n, int) else max(n - 1, 0))
                for c in range(CHUNKS):
                    last = pe.transpose(turns[:, k % 2, c * P:(c + 1) * P], whole[k % 2][:, c * P:(c + 1) * P],
                                        consts["ident_half"][:])
                last.then_inc(S["turned"], 1)

            turn(0, 0)

            def tile(n, k, left):
                if left:
                    turn(n + 1, k + 1)
                pe.wait_ge(S["turned_kept"], n + 1)
                wait(pe, S["mixed"], n if not isinstance(n, int) and k < 2 else max(n - 1, 0) if isinstance(n, int) else n - 1)
                for c in range(CHUNKS):
                    last = pe.matmul(sums[:, k % 2, :], whole_t[k % 2][:, c, :], keep["ternary_t"][:, c, :],
                                     start=c == 0, stop=c == CHUNKS - 1)
                last.then_inc(S["summed"], 1)

            tiles_in_turn(pe, tile)

        @block.scalar
        def _(act):
            def tile(n, k, left):
                act.wait_ge(S["turned"], n + 1)
                wait(act, S["summed"], n if not isinstance(n, int) and k < 2 else max(n - 1, 0) if isinstance(n, int) else n - 1)
                act.activation(whole_t[k % 2][:], turns[:, k % 2, 0:D].rearrange("p (c n) -> p c n", n=P), ACT.Copy
                               ).then_inc(S["turned_kept"], 1)

            tiles_in_turn(act, tile)


def flamingo(nc, t):
    with ExitStack() as ctx:
        mem = Memory(nc, ctx)
        t.update(scratch(nc))
        consts = constants(nc, mem, t)
        keep = {"counts": mem.sbuf("counts", [P, EXPERTS]), "places": mem.sbuf("places", [P, BATCHES * TILES], U32),
                "w_scale": mem.sbuf("w_scale", [P, 1]), "ternary_t": mem.sbuf("ternary_t", [P, CHUNKS, D], BF16),
                "istd3": mem.sbuf("istd3", [P, BATCHES * TILES]), "offset3": mem.sbuf("offset3", [P, BATCHES * TILES]),
                "largest": mem.sbuf("largest", [P, TILES])}
        quantize_weights(nc, t, consts, keep)
        with ExitStack() as first:
            weights = Memory(nc, first)
            hold = {n: [weights.sbuf(f"{n}_{h}", [P, CHUNKS, D], F32R) for h in ("hi", "lo")] for n in ("wq", "wo", "wg")}
            prepare(nc, hold, t, consts)
            attend_and_route(nc, hold, t, consts, keep)
        run_experts(nc, t, consts, keep)
        x3 = mem.sbuf("x3", [P, BATCHES * TILES, D])
        attend_context(nc, t, consts, keep, x3)
        quantized_layer(nc, t, consts, keep, x3)


_INS = ['x', 'ctx_1024', 'g_xattn', 'g_ffn', 'L0_xattn_Wq', 'L0_xattn_bq', 'L0_xattn_Wkv', 'L0_xattn_bkv',
        'L0_xattn_Wo', 'L0_xattn_bo', 'L0_ffn_Wg', 'L0_ffn_bg', 'L0_ffn_We', 'L0_ffn_be', 'L1_xattn_Wq',
        'L1_xattn_bq', 'L1_ffn_weight', 'L1_ffn_bias']


def kernel(**inputs):
    import numpy as _np
    import concourse.bacc as _bacc
    from concourse import mybir as _mybir
    from concourse.bass_utils import run_bass_kernel_spmd as _run

    nc = _bacc.Bacc("TRN2", target_bir_lowering=False, num_devices=1)
    arrays, tensors = {}, {}
    for name in _INS:
        a = _np.ascontiguousarray(inputs[name])
        arrays[f"in_{name}"] = a
        tensors[name] = nc.dram_tensor(f"in_{name}", a.shape, _mybir.dt.from_np(a.dtype), kind="ExternalInput").ap()
    tensors["out"] = nc.dram_tensor("out_x", (BATCHES, SEQ, D), F32, kind="ExternalOutput").ap()
    flamingo(nc, tensors)
    return _run(nc, [arrays], core_ids=[0]).results[0]["out_x"]
```

```python
from contextlib import ExitStack

import concourse.bass as bass
from concourse import mybir

F32 = mybir.dt.float32
F32R = mybir.dt.float32r
BF16 = mybir.dt.bfloat16
U32 = mybir.dt.uint32
I32 = mybir.dt.int32
ALU = mybir.AluOpType
ACT = mybir.ActivationFunctionType
AX_X = mybir.AxisListType.X

P = 128
BATCHES, SEQ, D = 16, 512, 512
KEYS = 120
TILES = SEQ // P
CHUNKS = D // P
HEADS = 16
HEAD = D // HEADS
GROUP = P // HEAD
GROUPS = HEADS // GROUP
EXPERTS = 8
REGION = BATCHES * SEQ + P
ROW = D + 3
EPS = 1e-5


class Memory:

    def __init__(self, nc, ctx, phase=""):
        self.nc, self.ctx, self.phase, self.sems = nc, ctx, phase, []

    def sbuf(self, name, shape, dtype=F32):
        return self.ctx.enter_context(self.nc.sbuf_tensor(self.phase + name, shape, dtype))

    def psum(self, name, shape, dtype=F32):
        return self.ctx.enter_context(self.nc.psum_tensor(self.phase + name, shape, dtype))

    def sem(self, name):
        self.sems.append(self.nc.alloc_semaphore(name=self.phase + name))
        return self.sems[-1]

    def clear_semaphores(self):
        self.nc.clear_and_free_semaphores(self.sems)
        self.nc.all_engine_barrier()


def wait(eng, sem, n):
    if not isinstance(n, int) or n > 0:
        eng.wait_ge(sem, n)


def wait_apart(eng, sem, n, passed):
    wait(eng, sem, n)
    if not isinstance(n, int):
        eng.sem_inc(passed, 1)


def three_pass(pe, out, left, right, first=True, last=True, k=P):
    (left_hi, left_lo), (right_hi, right_lo) = left, right
    pe.matmul(out, left_lo, right_hi, start=first, stop=False)
    pe.matmul(out, left_hi, right_lo, start=False, stop=False)
    return pe.matmul(out, left_hi, right_hi, start=False, stop=last)


def prepare(nc, hold, t, consts):
    with ExitStack() as ctx:
        mem = Memory(nc, ctx, "prepare_")
        raw = [mem.sbuf(f"raw_weight{i}", [P, CHUNKS, D]) for i in range(3)]
        wk, wv, w1, w1t = [[mem.sbuf(f"{n}_{h}", [P, CHUNKS, D], F32R) for h in ("hi", "lo")]
                           for n in ("wk", "wv", "w1", "w1t")]
        bk_row = mem.sbuf("bk_row", [P, D])
        bv_row = mem.sbuf("bv_row", [P, D])
        b1_row = mem.sbuf("b1_row", [P, D])
        context = mem.sbuf("context", [P, D])
        context_t = [mem.sbuf(f"context_t_{h}", [P, CHUNKS, KEYS], F32R) for h in ("hi", "lo")]
        k0 = mem.sbuf("k0", [P, D])
        v0 = mem.sbuf("v0", [P, D])
        k1 = mem.sbuf("k1", [P, D])
        v1 = mem.sbuf("v1", [P, 2, D], F32R)
        k0_t = mem.sbuf("k0_t", [P, 2, CHUNKS, KEYS], F32R)
        k1_t = mem.sbuf("k1_t", [P, 2, CHUNKS, KEYS], F32R)
        fold = mem.sbuf("fold", [P, D])
        fold_t = mem.sbuf("fold_t", [P, 2, CHUNKS, KEYS], F32R)
        fold_bias = mem.sbuf("fold_bias", [P, 1])
        product = mem.sbuf("product", [P, D])

        k1_bank, k0_bank, v0_bank, fold_bank = [mem.psum(n, [P, D]) for n in (
            "k1_bank", "k0_bank", "v0_bank", "fold_bank")]
        fold_t_bank, k1_t_bank, context_t_bank, k0_t_bank = [mem.psum(n, [P, CHUNKS, P]) for n in (
            "fold_t_bank", "k1_t_bank", "context_t_bank", "k0_t_bank")]

        sum_banks = (k1_bank, k0_bank, v0_bank, fold_bank)
        raw_loaded = [mem.sem(f"raw_loaded{i}") for i in range(3)]
        rows_loaded = mem.sem("rows_loaded")
        weight_hi, weight_lo = mem.sem("weight_hi"), mem.sem("weight_lo")
        w1_turned, w1t_hi, w1t_lo = mem.sem("w1_turned"), mem.sem("w1t_hi"), mem.sem("w1t_lo")
        context_loaded, context_turned = mem.sem("context_loaded"), mem.sem("context_turned")
        context_hi, context_lo = mem.sem("context_hi"), mem.sem("context_lo")
        k1_summed, k1_ready, k1_turned = mem.sem("k1_summed"), mem.sem("k1_ready"), mem.sem("k1_turned")
        k1_hi, k1_lo, v1_hi, v1_lo = [mem.sem(n) for n in ("k1_hi", "k1_lo", "v1_hi", "v1_lo")]
        k0_summed, k0_ready, k0_turned = mem.sem("k0_summed"), mem.sem("k0_ready"), mem.sem("k0_turned")
        k0_hi, k0_lo = mem.sem("k0_hi"), mem.sem("k0_lo")
        v0_summed, v0_ready = mem.sem("v0_summed"), mem.sem("v0_ready")
        fold_summed, fold_ready, fold_turned = [mem.sem(n) for n in ("fold_summed", "fold_ready", "fold_turned")]
        fold_hi, fold_lo, bias_ready = mem.sem("fold_hi"), mem.sem("fold_lo"), mem.sem("bias_ready")
        k0_stored, v0_stored, v1_stored, fold_stored, bias_stored = [mem.sem(n) for n in (
            "k0_stored", "v0_stored", "v1_stored", "fold_stored", "bias_stored")]

        def rows(w):
            return w.rearrange("(c p) n -> p c n", p=P)

        def chunks(tile):
            return tile.rearrange("p (c n) -> p c n", c=CHUNKS)

        weights = [(rows(t["L0_xattn_Wkv"][:, 0:D]), wk), (rows(t["L0_xattn_Wkv"][:, D:2 * D]), wv),
                   (rows(t["L1_xattn_Wq"]), w1), (rows(t["L0_xattn_Wq"]), hold["wq"]),
                   (rows(t["L0_xattn_Wo"]), hold["wo"]), (rows(t["L0_ffn_Wg"]), hold["wg"])]
        W1 = 2

        ctx.callback(mem.clear_semaphores)
        block = ctx.enter_context(nc.Block())

        @block.sync
        def _(sp):
            sp.dma_start(context[0:KEYS, :], t["ctx_1024"][0]).then_inc(context_loaded, 16)
            for n, (src, _) in enumerate(weights):
                if n >= 3:
                    sp.wait_ge(weight_lo, n - 2)
                if n == 3 + W1:
                    sp.wait_ge(w1_turned, CHUNKS)
                sp.dma_start(raw[n % 3][:], src).then_inc(raw_loaded[n % 3], 16)
                if n == 1:
                    for row, src in ((bk_row, t["L0_xattn_bkv"][0:D]), (bv_row, t["L0_xattn_bkv"][D:2 * D]),
                                     (b1_row, t["L1_xattn_bq"])):
                        sp.dma_start(row[:], src.partition_broadcast(P)).then_inc(rows_loaded, 16)

            def stores(b, last):
                if not last:
                    sp.wait_ge(context_turned, b + 1)
                    sp.dma_start(context[0:KEYS, :], t["ctx_1024"][b + 1]).then_inc(context_loaded, 16)
                sp.wait_ge(v1_lo, b + 1)
                sp.dma_start(t["v1_pairs"][b], v1[0:KEYS].bitcast(F32)).then_inc(v1_stored, 16)
                sp.wait_ge(bias_ready, b + 1)
                sp.dma_start(t["fold_biases"][b], fold_bias[0:KEYS]).then_inc(bias_stored, 16)
                sp.wait_ge(v0_ready, b + 1)
                sp.dma_start(t["v0_rows"][b], v0[0:KEYS]).then_inc(v0_stored, 16)
                sp.wait_ge(k0_lo, b + 1)
                sp.dma_start(t["k0_pairs"][b], k0_t[:].bitcast(F32)).then_inc(k0_stored, 16)
                sp.wait_ge(fold_lo, b + 1)
                sp.dma_start(t["fold_pairs"][b], fold_t[:].bitcast(F32)).then_inc(fold_stored, 16)

            stores(0, False)
            with sp.Fori(1, BATCHES - 1) as b:
                stores(b, False)
            stores(BATCHES - 1, True)
            for s in (k0_stored, v0_stored, v1_stored, fold_stored, bias_stored):
                sp.wait_ge(s, 16 * BATCHES)

        @block.tensor
        def _(pe):
            def turn(bank, source, done):
                for c in range(CHUNKS):
                    last = pe.transpose(bank[:, c, 0:KEYS], source[0:KEYS, c * P:(c + 1) * P],
                                        consts["ident"][0:KEYS, 0:KEYS])
                last.then_inc(done, 1)

            def project(bank, left, right, done):
                for c in range(CHUNKS):
                    last = three_pass(pe, bank[0:KEYS, :], [x[:, c, :] for x in left],
                                      [x[:, c, :] for x in right], c == 0, c == CHUNKS - 1)
                last.then_inc(done, 1)

            def turn_context(b):
                pe.wait_ge(context_loaded, 16 * (b + 1))
                turn(context_t_bank, context, context_turned)

            pe.wait_ge(consts["ready"], consts["made"])
            pe.wait_ge(raw_loaded[W1], 16)
            for j, bank in enumerate(sum_banks):
                for c in range(CHUNKS):
                    last = pe.transpose(bank[:, c * P:(c + 1) * P], raw[W1][:, c, j * P:(j + 1) * P],
                                        consts["ident"][:])
                last.then_inc(w1_turned, 1)
            turn_context(0)
            pe.wait_ge(weight_lo, W1 + 1)
            pe.wait_ge(w1t_lo, CHUNKS)

            def batch(b, last):
                pe.wait_ge(context_lo, b + 1)
                wait(pe, k1_ready, b)
                project(k1_bank, context_t, w1, k1_summed)
                wait(pe, k0_ready, b)
                project(k0_bank, context_t, wk, k0_summed)
                pe.wait_ge(k1_ready, b + 1)
                wait(pe, k1_lo, b)
                turn(k1_t_bank, k1, k1_turned)
                wait(pe, v0_ready, b)
                project(v0_bank, context_t, wv, v0_summed)
                if not last:
                    turn_context(b + 1)
                pe.wait_ge(k1_lo, b + 1)
                wait(pe, fold_ready, b)
                project(fold_bank, [k1_t[:, h] for h in range(2)], w1t, fold_summed)
                pe.wait_ge(k0_ready, b + 1)
                wait(pe, k0_lo, b)
                turn(k0_t_bank, k0, k0_turned)
                pe.wait_ge(fold_ready, b + 1)
                wait(pe, fold_lo, b)
                turn(fold_t_bank, fold, fold_turned)

            batch(0, False)
            with pe.Fori(1, BATCHES - 1) as b:
                batch(b, False)
            batch(BATCHES - 1, True)

        @block.scalar
        def _(act):
            def high(out, bank, turned, n, done):
                act.wait_ge(turned, n)
                act.activation(out, bank, ACT.Copy).then_inc(done, 1)

            for n, (_, (hi, _)) in enumerate(weights):
                act.wait_ge(raw_loaded[n % 3], 16 * (n // 3 + 1))
                act.activation(hi[:], raw[n % 3][:], ACT.Copy).then_inc(weight_hi, 1)
                if n == W1:
                    for j, bank in enumerate(sum_banks):
                        high(w1t[0][:, j, :], bank[:], w1_turned, j + 1, w1t_hi)
                    high(context_t[0][:], context_t_bank[:, :, 0:KEYS], context_turned, 1, context_hi)

            def batch(b, last):
                act.wait_ge(k1_ready, b + 1)
                wait(act, v1_stored, 16 * b)
                act.activation(v1[0:KEYS, 0], k1[0:KEYS, :], ACT.Copy).then_inc(v1_hi, 1)
                high(k1_t[:, 0], k1_t_bank[:, :, 0:KEYS], k1_turned, b + 1, k1_hi)
                if not last:
                    high(context_t[0][:], context_t_bank[:, :, 0:KEYS], context_turned, b + 2, context_hi)
                wait(act, fold_turned, b)
                act.wait_ge(fold_summed, b + 1)
                act.activation(fold[0:KEYS, :], fold_bank[0:KEYS, :], ACT.Copy).then_inc(fold_ready, 1)
                wait(act, k0_stored, 16 * b)
                high(k0_t[:, 0], k0_t_bank[:, :, 0:KEYS], k0_turned, b + 1, k0_hi)
                wait(act, fold_stored, 16 * b)
                high(fold_t[:, 0], fold_t_bank[:, :, 0:KEYS], fold_turned, b + 1, fold_hi)

            batch(0, False)
            with act.Fori(1, BATCHES - 1) as b:
                batch(b, False)
            batch(BATCHES - 1, True)

        @block.vector
        def _(dve):
            def low(out, whole, hi, high_done, n, done):
                dve.wait_ge(high_done, n)
                dve.tensor_tensor(out, whole, hi.bitcast(F32), ALU.subtract).then_inc(done, 1)

            for n, (_, (hi, lo)) in enumerate(weights):
                low(lo[:], raw[n % 3][:], hi[:], weight_hi, n + 1, weight_lo)
                if n == W1:
                    for j, bank in enumerate(sum_banks):
                        low(w1t[1][:, j, :], bank[:], w1t[0][:, j, :], w1t_hi, j + 1, w1t_lo)
                    low(context_t[1][:], context_t_bank[:, :, 0:KEYS], context_t[0][:], context_hi, 1, context_lo)
            dve.wait_ge(rows_loaded, 16 * 3)

            def batch(b, last):
                wait(dve, k1_turned, b)
                wait(dve, v1_lo, b)
                dve.wait_ge(k1_summed, b + 1)
                dve.tensor_tensor(k1[0:KEYS], k1_bank[0:KEYS], b1_row[0:KEYS], ALU.add).then_inc(k1_ready, 1)
                wait(dve, k0_turned, b)
                dve.wait_ge(k0_summed, b + 1)
                dve.tensor_tensor(k0[0:KEYS], k0_bank[0:KEYS], bk_row[0:KEYS], ALU.add).then_inc(k0_ready, 1)
                dve.wait_ge(k1_ready, b + 1)
                wait(dve, bias_stored, 16 * b)
                dve.scalar_tensor_tensor(product[0:KEYS], k1[0:KEYS], D ** -0.5, b1_row[0:KEYS], ALU.mult,
                                         ALU.mult, accum_out=fold_bias[0:KEYS, :]).then_inc(bias_ready, 1)
                low(v1[0:KEYS, 1], k1[0:KEYS], v1[0:KEYS, 0], v1_hi, b + 1, v1_lo)
                low(k1_t[:, 1], k1_t_bank[:, :, 0:KEYS], k1_t[:, 0], k1_hi, b + 1, k1_lo)
                wait(dve, v0_stored, 16 * b)
                dve.wait_ge(v0_summed, b + 1)
                dve.tensor_tensor(v0[0:KEYS], v0_bank[0:KEYS], bv_row[0:KEYS], ALU.add).then_inc(v0_ready, 1)
                if not last:
                    low(context_t[1][:], context_t_bank[:, :, 0:KEYS], context_t[0][:], context_hi, b + 2,
                        context_lo)
                low(k0_t[:, 1], k0_t_bank[:, :, 0:KEYS], k0_t[:, 0], k0_hi, b + 1, k0_lo)
                low(fold_t[:, 1], fold_t_bank[:, :, 0:KEYS], fold_t[:, 0], fold_hi, b + 1, fold_lo)

            batch(0, False)
            with dve.Fori(1, BATCHES - 1) as b:
                batch(b, False)
            batch(BATCHES - 1, True)


def constants(nc, mem, t):
    c = {"ident": mem.sbuf("ident", [P, P]), "ident_half": mem.sbuf("ident_half", [P, P], BF16),
         "before": mem.sbuf("before", [P, P], BF16), "ones": mem.sbuf("ones", [P, P], BF16),
         "numbers": mem.sbuf("numbers", [P, EXPERTS]), "own": mem.sbuf("own", [P, EXPERTS]),
         "gates": mem.sbuf("gates", [P, 4])}
    c["ready"], filled, c["made"] = mem.sem("constants_ready"), mem.sem("constants_filled"), 6
    gates_loaded = mem.sem("gates_loaded")
    c["passed"] = mem.sem("passed")
    count = mem.sbuf("count", [P, EXPERTS], I32)
    count_own = mem.sbuf("count_own", [P, EXPERTS], I32)
    with nc.Block() as block:
        @block.gpsimd
        def _(pool):
            pool.memset(c["ident"][:], 0.0).then_inc(filled, 1)
            pool.memset(c["ident_half"][:], 0.0).then_inc(filled, 1)
            pool.memset(c["ones"][:], 1.0).then_inc(filled, 1)
            pool.iota(count[:], [[1, EXPERTS]], base=0, channel_multiplier=0).then_inc(filled, 1)
            pool.iota(count_own[:], [[REGION, EXPERTS]], base=0, channel_multiplier=1).then_inc(filled, 1)
            pool.wait_ge(filled, 5)
            pool.tensor_copy(c["numbers"][:], count[:]).then_inc(c["ready"], 1)
            pool.tensor_copy(c["own"][:], count_own[:]).then_inc(c["ready"], 1)
            for out, source, keep, fill in ((c["ident"], c["ident"], ALU.not_equal, 1.0),
                                            (c["ident_half"], c["ident_half"], ALU.not_equal, 1.0),
                                            (c["before"], c["ones"], ALU.is_gt, 0.0)):
                pool.affine_select(out=out[:], in_=source[:], compare_op=keep, fill=fill, base=0,
                                   pattern=[[1, P]], channel_multiplier=-1).then_inc(c["ready"], 1)

        @block.sync
        def _(sp):
            sp.dma_start(c["gates"][:, 0:2], t["g_xattn"].partition_broadcast(P)).then_inc(gates_loaded, 16)
            sp.dma_start(c["gates"][:, 2:4], t["g_ffn"].partition_broadcast(P)).then_inc(gates_loaded, 16)

        @block.scalar
        def _(act):
            act.wait_ge(gates_loaded, 32)
            act.activation(c["gates"][:], c["gates"][:], ACT.Tanh).then_inc(c["ready"], 1)
            act.wait_ge(c["ready"], 6)
    return c


def scratch(nc):
    def table(name, shape, dtype=F32):
        return nc.dram_tensor(name, shape, dtype).ap()

    return {"k0_pairs": table("k0_pairs", [BATCHES, P, 2, CHUNKS, KEYS]),
            "fold_pairs": table("fold_pairs", [BATCHES, P, 2, CHUNKS, KEYS]),
            "v0_rows": table("v0_rows", [BATCHES, KEYS, D]),
            "v1_pairs": table("v1_pairs", [BATCHES, KEYS, 2, D]),
            "fold_biases": table("fold_biases", [BATCHES, KEYS, 1]),
            "routed": table("routed", [(EXPERTS * REGION + EXPERTS * P), ROW]),
            "results": table("results", [(BATCHES * TILES + EXPERTS) * P, D])}


class Uses:

    def __init__(self, start, names):
        self.start, self.index = start, {name: k for k, name in enumerate(names)}

    def __getitem__(self, name):
        k = self.index[name]
        return self.start + k, k % 2


def attend_and_route(nc, hold, t, consts, keep):
    with ExitStack() as ctx:
        mem = Memory(nc, ctx, "attend_")
        wq, wo, wg = hold["wq"], hold["wo"], hold["wg"]
        bq_cols, bo_row, bg_row = mem.sbuf("bq_cols", [P, CHUNKS]), mem.sbuf("bo_row", [P, D]), mem.sbuf("bg_row", [P, D])
        x = mem.sbuf("x", [P, 2, TILES, D])
        stats, moments = mem.sbuf("stats", [P, TILES, 6]), mem.sbuf("moments", [P, TILES, 2])
        spread, istd, offset = [mem.sbuf(n, [P, TILES]) for n in ("spread", "istd", "offset")]
        half = mem.sbuf("half", [P, TILES])
        xn = mem.sbuf("xn", [P, TILES, D])
        x_t = [mem.sbuf(f"x_t_{h}", [P, CHUNKS, SEQ], F32R) for h in ("hi", "lo")]
        q = [mem.sbuf(f"q_{h}", [P, 2, SEQ], F32R) for h in ("hi", "lo")]
        q_stack = mem.sbuf("q_stack", [P, 2, GROUP, SEQ], F32R)
        k_stack = mem.sbuf("k_stack", [P, GROUPS, GROUP, KEYS], F32R)
        peak, shift, total, share = [mem.sbuf(n, [P, 2, GROUP]) for n in ("peak", "shift", "total", "share")]
        weights = mem.sbuf("weights", [P, 2, GROUP, SEQ])
        v = mem.sbuf("v", [P, D])
        v_shared = mem.sbuf("v_shared", [P, 2, GROUP, HEAD])
        out_t = [mem.sbuf(f"out_t_{h}", [P, GROUPS, SEQ], F32R) for h in ("hi", "lo")]
        x1 = mem.sbuf("x1", [P, TILES, ROW])
        stats1, moments1 = mem.sbuf("stats1", [P, TILES, 6]), mem.sbuf("moments1", [P, TILES, 2])
        spread1, minus_mean1 = mem.sbuf("spread1", [P, TILES]), mem.sbuf("minus_mean1", [P, TILES])
        xn1 = mem.sbuf("xn1", [P, TILES, D])
        x1_t = [mem.sbuf(f"x1_t_{h}", [P, 2, CHUNKS, P], F32R) for h in ("hi", "lo")]
        logits = mem.sbuf("logits", [P, 2, D])
        best, minus_best = mem.sbuf("best", [P, TILES, 8]), mem.sbuf("minus_best", [P, TILES])
        best_at = mem.sbuf("best_at", [P, TILES, 8], U32)
        mass, chance = mem.sbuf("mass", [P, TILES]), mem.sbuf("chance", [P, TILES])
        expert_u, expert = mem.sbuf("expert_u", [P, TILES], U32), mem.sbuf("expert", [P, TILES])
        one_hot = mem.sbuf("one_hot", [P, TILES, EXPERTS], BF16)
        rank, rank_own = mem.sbuf("rank", [P, TILES, EXPERTS]), mem.sbuf("rank_own", [P, TILES, EXPERTS])
        rank_sum = mem.sbuf("rank_sum", [P, TILES])
        place = mem.sbuf("place", [P, TILES], U32)

        score = mem.psum("score", [P, GROUP, SEQ])
        sums = mem.psum("sums", [P, 2, D])
        turns = mem.psum("turns", [P, 2, CHUNKS, P])

        S = {n: mem.sem(n) for n in (
            "rows_loaded", "row_scaled", "x_loaded", "k_loaded", "v_loaded", "filled", "stats_made",
            "moments_made", "spread_made", "istd_made", "mean_turned", "offset_made", "xn_ready",
            "x_biased", "sum_ready", "sum_done", "turn_ready", "turn_done", "x_hi", "q_hi", "q_stacked0",
            "q_stacked1", "scored", "peaked", "shifted", "weighed", "inverted", "v_ready", "out_hi",
            "stats1_made", "moments1_made", "spread1_made", "mean1_turned", "istd1_made", "offset1_made",
            "xn1_ready", "x1_hi", "best_made", "best_turned", "best_found", "massed", "expert_read",
            "expert_made", "one_hot_made", "chance_made", "rank_picked", "rank_summed", "placed",
            "place_kept", "counted", "scattered")}
        q_stacked = (S["q_stacked0"], S["q_stacked1"])
        STACK = 16 * 3 * GROUP

        def uses_of_sums(b, route, attend, prefetch):
            names = [("query", 2), ("gate", 0), ("query", 3), ("gate", 1), ("gate", 2), ("gate", 3),
                     ("query", 0), ("ranks", 0), ("counts", 0), ("query", 1)] + [("back", i) for i in range(TILES)]
            there = {"gate": route, "ranks": route, "counts": route, "back": attend}
            here = [n for n in names if there.get(n[0], prefetch if n[1] < 2 else attend)]
            FIRST, EACH = 2, len(names)
            ROUTED = TILES + 2
            if isinstance(b, int) and b == 0:
                return Uses(FIRST, here)
            return Uses(EACH * b + FIRST - ROUTED - (2 if isinstance(b, int) and b == BATCHES else 0), here)

        def uses_of_turns(b, route, attend, prefetch):
            names = [("routed", 0), ("routed", 1), ("weigh", 0), ("routed", 2), ("routed", 3), ("weigh", 1),
                     ("x", 0), ("x", 1), ("x", 2), ("x", 3), ("weigh", 2), ("weigh", 3)]
            there = {"routed": route, "weigh": attend, "x": prefetch}
            here = [n for n in names if there[n[0]]]
            if isinstance(b, int) and b == 0:
                return Uses(TILES, here)
            return Uses(len(names) * b - (TILES if isinstance(b, int) and b == BATCHES else 0), here)

        FIRST_SUMS = Uses(0, [("query", 0), ("query", 1)])
        FIRST_TURNS = Uses(0, [("x", i) for i in range(TILES)])

        def iterations(eng, iteration):
            def at(b, odd, route=True, attend=True, prefetch=True):
                there = route, attend, prefetch
                iteration(b, odd, uses_of_sums(b, *there), uses_of_turns(b, *there), *there)

            FIRST = 3
            for b in range(FIRST):
                at(b, b % 2, route=b > 0)
            with eng.Fori(0, (BATCHES - 1 - FIRST) // 2) as pair:
                for k in range(2):
                    at(2 * pair + FIRST + k, (FIRST + k) % 2)
            at(BATCHES - 1, 1, prefetch=False)
            at(BATCHES, 0, attend=False, prefetch=False)

        passed = consts["passed"]
        ctx.callback(mem.clear_semaphores)
        block = ctx.enter_context(nc.Block())

        @block.sync
        def _(sp):
            def load_x(b, odd, start=0):
                wait(sp, S["sum_done"], start)
                sp.dma_start(x[:, odd], t["x"][b].rearrange("(t p) d -> p t d", p=P)).then_inc(S["x_loaded"], 16)

            def load_keys(b):
                pairs = t["k0_pairs"][b].rearrange("(g d) h m n -> g d h m n", d=HEAD)
                wait(sp, S["scored"], HEADS * b)
                for block_of, part in enumerate((0, 0, 1)):
                    for g in range(GROUP):
                        sp.dma_start(k_stack[HEAD * block_of:HEAD * (block_of + 1), :, g, :].bitcast(F32),
                                     pairs[g, :, part]).then_inc(S["k_loaded"], 16)

            def load_values(b):
                wait(sp, S["v_ready"], GROUPS * b)
                sp.dma_start(v[0:KEYS], t["v0_rows"][b]).then_inc(S["v_loaded"], 16)

            def stack(b, m, uses):
                wait_apart(sp, S["scored"], HEADS * b + GROUP * (m - 1), passed)
                sp.wait_ge(S["sum_done"], uses["query", m][0] + 1)
                for g in range(GROUP):
                    for block_of, part in enumerate((0, 1, 0)):
                        sp.dma_start(q_stack[HEAD * block_of:HEAD * (block_of + 1), m % 2, g, :].bitcast(F32),
                                     q[part][HEAD * g:HEAD * (g + 1), m % 2, :].bitcast(F32)
                                     ).then_inc(q_stacked[m % 2], 16)

            load_x(0, 0)
            for to, source in ((bo_row, "L0_xattn_bo"), (bg_row, "L0_ffn_bg")):
                sp.dma_start(to[:], t[source].partition_broadcast(P)).then_inc(S["rows_loaded"], 16)
            sp.dma_start(bq_cols[:], t["L0_xattn_bq"].rearrange("(c p) -> p c", p=P),
                         allow_slow_non_contiguous=True).then_inc(S["rows_loaded"], 16)
            load_keys(0)
            load_values(0)
            for m in range(2):
                stack(0, m, FIRST_SUMS)

            def iteration(b, odd, s, r, route, attend, prefetch):
                if prefetch:
                    load_x(b + 1, 1 - odd, s.start)
                if attend:
                    stack(b, 2, s)
                    stack(b, 3, s)
                if prefetch:
                    stack(b + 1, 0, s)
                    load_keys(b + 1)
                    stack(b + 1, 1, s)
                    load_values(b + 1)

            iterations(sp, iteration)

        @block.tensor
        def _(pe):
            def turn(use, source):
                n, bank = use
                wait(pe, S["turn_done"], n - 1)
                for c in range(CHUNKS):
                    last = pe.transpose(turns[:, bank, c, :], source[:, c * P:(c + 1) * P], consts["ident"][:])
                last.then_inc(S["turn_ready"], 1)
                return n + 1

            def project(use, left, right):
                n, bank = use
                wait(pe, S["sum_done"], n - 1)
                for c in range(CHUNKS):
                    last = three_pass(pe, sums[:, bank, :], left(c), right(c), c == 0, c == CHUNKS - 1)
                last.then_inc(S["sum_ready"], 1)

            def turn_x(uses, b, i):
                pe.wait_ge(S["xn_ready"], TILES * b + i + 1)
                return turn(uses["x", i], xn[:, i])

            def turn_routed(uses, b, i):
                pe.wait_ge(S["xn1_ready"], TILES * b + i + 1)
                return turn(uses["routed", i], xn1[:, i])

            def gate(uses, i, turned):
                pe.wait_ge(S["turn_done"], turned)
                project(uses["gate", i], lambda c: [h[:, i % 2, c, :] for h in x1_t], lambda c: [h[:, c, :] for h in wg])

            def query(uses, m):
                project(uses["query", m], lambda c: [h[:, c, m * P:(m + 1) * P] for h in wq], lambda c: [h[:, c, :] for h in x_t])

            def scores(b, m):
                pe.wait_ge(q_stacked[m % 2], STACK * (2 * b + m // 2 + 1))
                pe.wait_ge(S["k_loaded"], 16 * 3 * GROUP * (b + 1))
                for g in range(GROUP):
                    wait(pe, S["weighed"], HEADS * b + GROUP * (m - 1) + g + 1)
                    pe.matmul(score[0:KEYS, g, :], k_stack[0:3 * HEAD, m, g, :], q_stack[0:3 * HEAD, m % 2, g, :],
                              start=True, stop=True).then_inc(S["scored"], 1)

            def weigh(uses, b, m):
                n, bank = uses["weigh", m]
                wait(pe, S["turn_done"], n - 1)
                pe.wait_ge(S["v_ready"], GROUPS * b + m + 1)
                for g in range(GROUP):
                    last = pe.matmul(turns[HEAD * g:HEAD * (g + 1), bank].rearrange("p c n -> p (c n)"),
                                     v_shared[0:KEYS, m % 2, g, :], weights[0:KEYS, m % 2, g, :], start=True, stop=True,
                                     tile_position=(0, HEAD * g))
                last.then_inc(S["turn_ready"], 1)
                return n + 1

            def back(uses, i, turned):
                pe.wait_ge(S["turn_done"], turned)
                project(uses["back", i], lambda c: [h[:, c, i * P:(i + 1) * P] for h in out_t], lambda c: [h[:, c, :] for h in wo])

            def ranks(uses, b):
                n, bank = uses["ranks", 0]
                wait(pe, S["sum_done"], n - 1)
                pe.wait_ge(S["one_hot_made"], b + 1)
                out = sums[:, bank, 0:TILES * EXPERTS].rearrange("p (i e) -> p i e", e=EXPERTS)
                last = pe.matmul(out, consts["before"][:], one_hot[:], start=True, stop=False)
                for i in range(TILES - 1):
                    rest = TILES - 1 - i
                    last = pe.matmul(out[:, i + 1:TILES, :], consts["ones"][:],
                                     one_hot[:, i:i + 1, :].broadcast_to([P, rest, EXPERTS]), start=False,
                                     stop=i == TILES - 2)
                last.then_inc(S["sum_ready"], 1)
                n, bank = uses["counts", 0]
                wait(pe, S["sum_done"], n - 1)
                for i in range(TILES):
                    last = pe.matmul(sums[:, bank, 0:EXPERTS], consts["ones"][:], one_hot[:, i, :],
                                     start=i == 0, stop=i == TILES - 1)
                last.then_inc(S["sum_ready"], 1)

            for i in range(TILES):
                turned_x = turn_x(FIRST_TURNS, 0, i)
            pe.wait_ge(S["turn_done"], turned_x)
            for m in range(2):
                query(FIRST_SUMS, m)

            def iteration(b, odd, s, r, route, attend, prefetch):
                p, turned = b - 1, {}
                if attend:
                    scores(b, 0)
                    query(s, 2)
                if route:
                    turned[0] = turn_routed(r, p, 0)
                    turned[1] = turn_routed(r, p, 1)
                    gate(s, 0, turned[0])
                if attend:
                    scores(b, 1)
                    weigh(r, b, 0)
                    query(s, 3)
                if route:
                    turned[2] = turn_routed(r, p, 2)
                    gate(s, 1, turned[1])
                    turned[3] = turn_routed(r, p, 3)
                if attend:
                    scores(b, 2)
                    weigh(r, b, 1)
                if prefetch:
                    turn_x(r, b + 1, 0)
                if route:
                    gate(s, 2, turned[2])
                if prefetch:
                    for i in range(1, TILES):
                        turned_x = turn_x(r, b + 1, i)
                if route:
                    gate(s, 3, turned[3])
                if attend:
                    scores(b, 3)
                    weigh(r, b, 2)
                if prefetch:
                    pe.wait_ge(S["turn_done"], turned_x)
                    query(s, 0)
                if route:
                    ranks(s, p)
                if attend:
                    turned_out = weigh(r, b, 3)
                if prefetch:
                    query(s, 1)
                if attend:
                    for i in range(TILES):
                        back(s, i, turned_out)

            iterations(pe, iteration)

        @block.scalar
        def _(act):
            def turned_hi(use, out, done):
                n, bank = use
                act.wait_ge(S["turn_ready"], n + 1)
                act.activation(out, turns[:, bank], ACT.Copy).then_inc(S[done], 1)

            def x_hi(uses, i):
                turned_hi(uses["x", i], x_t[0][:, :, i * P:(i + 1) * P], "x_hi")

            def routed_hi(uses, i):
                turned_hi(uses["routed", i], x1_t[0][:, i % 2], "x1_hi")

            def query_hi(uses, b, m):
                n, bank = uses["query", m]
                act.wait_ge(S["sum_ready"], n + 1)
                wait(act, q_stacked[m % 2], STACK * (2 * b + m // 2))
                act.activation(q[0][:, m % 2, :], sums[:, bank, :], ACT.Identity,
                               bias=bq_cols[:, m:m + 1]).then_inc(S["q_hi"], 1)

            def weights_of(b, m):
                act.wait_ge(S["shifted"], GROUPS * b + m + 1)
                for g in range(GROUP):
                    act.activation(weights[0:KEYS, m % 2, g, :], score[0:KEYS, g, :], ACT.Exp,
                                   bias=shift[0:KEYS, m % 2, g:g + 1], scale=HEAD ** -0.5,
                                   accum_out=total[0:KEYS, m % 2, g:g + 1]).then_inc(S["weighed"], 1)

            def out_hi(uses, m):
                n, bank = uses["weigh", m]
                act.wait_ge(S["turn_ready"], n + 1)
                act.activation(out_t[0][:, m, :], turns[:, bank].rearrange("p c n -> p (c n)"), ACT.Copy
                               ).then_inc(S["out_hi"], 1)

            def gate_mass(b, i):
                act.wait_ge(S["best_turned"], TILES * b + i + 1)
                act.wait_ge(S["best_found"], TILES * b + i + 1)
                act.activation(logits[:, i % 2, :], logits[:, i % 2, :], ACT.Exp, bias=minus_best[:, i:i + 1],
                               accum_out=mass[:, i:i + 1]).then_inc(S["massed"], 1)

            act.wait_ge(S["rows_loaded"], 16 * 3)
            for i in range(TILES):
                x_hi(FIRST_TURNS, i)
            for m in range(2):
                query_hi(FIRST_SUMS, 0, m)

            def iteration(b, odd, s, r, route, attend, prefetch):
                p = b - 1
                if attend:
                    query_hi(s, b, 2)
                if route:
                    routed_hi(r, 0)
                    routed_hi(r, 1)
                if attend:
                    weights_of(b, 0)
                    out_hi(r, 0)
                    query_hi(s, b, 3)
                    weights_of(b, 1)
                if route:
                    routed_hi(r, 2)
                    routed_hi(r, 3)
                    gate_mass(p, 0)
                if attend:
                    out_hi(r, 1)
                if prefetch:
                    x_hi(r, 0)
                if attend:
                    weights_of(b, 2)
                if prefetch:
                    for i in range(1, TILES):
                        x_hi(r, i)
                if route:
                    gate_mass(p, 1)
                    gate_mass(p, 2)
                if attend:
                    out_hi(r, 2)
                if prefetch:
                    query_hi(s, b + 1, 0)
                if route:
                    gate_mass(p, 3)
                if attend:
                    weights_of(b, 3)
                    out_hi(r, 3)
                if prefetch:
                    query_hi(s, b + 1, 1)

            iterations(act, iteration)

        @block.vector
        def _(dve):
            def turned_lo(use, hi, lo, hi_done, n_hi):
                _, bank = use
                dve.wait_ge(S[hi_done], n_hi)
                dve.tensor_tensor(lo, turns[:, bank], hi.bitcast(F32), ALU.subtract
                                  ).then_inc(S["turn_done"], 1)

            def x_lo(uses, b, i):
                hi, lo = [h[:, :, i * P:(i + 1) * P] for h in x_t]
                turned_lo(uses["x", i], hi, lo, "x_hi", TILES * b + i + 1)

            def routed_lo(uses, b, i):
                hi, lo = [h[:, i % 2] for h in x1_t]
                turned_lo(uses["routed", i], hi, lo, "x1_hi", TILES * b + i + 1)

            def query_lo(uses, b, m):
                n, bank = uses["query", m]
                dve.wait_ge(S["q_hi"], GROUPS * b + m + 1)
                dve.scalar_tensor_tensor(q[1][:, m % 2, :], sums[:, bank, :], bq_cols[:, m:m + 1],
                                         q[0][:, m % 2, :].bitcast(F32), ALU.add, ALU.subtract
                                         ).then_inc(S["sum_done"], 1)

            def out_lo(uses, b, m):
                n, bank = uses["weigh", m]
                dve.wait_ge(S["out_hi"], GROUPS * b + m + 1)
                dve.tensor_tensor(out_t[1][:, m, :], turns[:, bank].rearrange("p c n -> p (c n)"),
                                  out_t[0][:, m, :].bitcast(F32), ALU.subtract
                                  ).then_inc(S["turn_done"], 1)

            def peaks(b, m):
                n = GROUPS * b + m + 1
                dve.wait_ge(S["scored"], GROUP * n)
                dve.tensor_reduce(peak[0:KEYS, m % 2, :], score[0:KEYS], AX_X, ALU.max).then_inc(S["peaked"], 1)
                dve.wait_ge(S["peaked"], n)
                dve.tensor_scalar(shift[0:KEYS, m % 2, :], peak[0:KEYS, m % 2, :], -(HEAD ** -0.5), None, ALU.mult
                                  ).then_inc(S["shifted"], 1)

            def share_values(b, m):
                n = GROUPS * b + m + 1
                dve.wait_ge(S["weighed"], GROUP * n)
                dve.reciprocal(share[0:KEYS, m % 2, :], total[0:KEYS, m % 2, :]).then_inc(S["inverted"], 1)
                dve.wait_ge(S["v_loaded"], 16 * (b + 1))
                dve.wait_ge(S["inverted"], n)
                dve.tensor_tensor(v_shared[0:KEYS, m % 2], v[0:KEYS, m * P:(m + 1) * P].rearrange("p (g d) -> p g d", d=HEAD),
                                  share[0:KEYS, m % 2, :].unsqueeze(2).broadcast_to([KEYS, GROUP, HEAD]), ALU.mult
                                  ).then_inc(S["v_ready"], 1)

            def tile_stats(b, odd, i):
                if i == 0:
                    dve.wait_ge(S["x_loaded"], 16 * (b + 1))
                    wait(dve, S["xn_ready"], TILES * b)
                dve.bn_stats(stats[:, i, :], x[:, odd, i, :]).then_inc(S["stats_made"], 1)

            def batch_moments(b):
                for i in range(TILES):
                    wait_apart(dve, S["stats_made"], TILES * b + i + 1, passed)
                    dve.bn_aggr(moments[:, i, :], stats[:, i, :]).then_inc(S["moments_made"], 1)

            def gate_logits(uses, b, i):
                n, bank = uses["gate", i]
                dve.wait_ge(S["sum_ready"], n + 1)
                wait(dve, S["massed"], TILES * b + max(i - 1, 0))
                dve.tensor_tensor(logits[:, i % 2, :], sums[:, bank, :], bg_row[:], ALU.add
                                  ).then_inc(S["sum_done"], 1)
                return n + 1

            def gate_best(b, i, logits_at):
                n = TILES * b + i + 1
                wait_apart(dve, S["sum_done"], logits_at, passed)
                dve.max(best[:, i, :], logits[:, i % 2, :]).then_inc(S["best_made"], 1)
                dve.wait_ge(S["best_made"], n)
                dve.tensor_scalar(minus_best[:, i:i + 1], best[:, i, 0:1], -1.0, None, ALU.mult
                                  ).then_inc(S["best_turned"], 1)
                dve.max_index(best_at[:, i, :], best[:, i, :], logits[:, i % 2, :]).then_inc(S["best_found"], 1)

            def choose(b):
                dve.wait_ge(S["best_found"], TILES * (b + 1))
                dve.tensor_scalar(expert_u[:], best_at[:, :, 0], EXPERTS - 1, None, ALU.bitwise_and
                                  ).then_inc(S["expert_read"], 1)
                dve.wait_ge(S["expert_read"], b + 1)
                dve.tensor_copy(expert[:], expert_u[:]).then_inc(S["expert_made"], 1)
                dve.wait_ge(S["expert_made"], b + 1)
                dve.tensor_tensor(one_hot[:], consts["numbers"][:].unsqueeze(1).broadcast_to([P, TILES, EXPERTS]),
                                  expert[:].unsqueeze(2).broadcast_to([P, TILES, EXPERTS]), ALU.is_equal
                                  ).then_inc(S["one_hot_made"], 1)

            def place_rows(uses, b):
                n, bank = uses["ranks", 0]
                dve.wait_ge(S["sum_ready"], n + 1)
                dve.wait_ge(S["sum_done"], uses.start)
                dve.tensor_tensor(rank[:], sums[:, bank, 0:TILES * EXPERTS].rearrange("p (i e) -> p i e", e=EXPERTS),
                                  keep["counts"][:].unsqueeze(1).broadcast_to([P, TILES, EXPERTS]), ALU.add
                                  ).then_inc(S["sum_done"], 1)
                dve.wait_ge(S["sum_done"], n + 1)
                n, bank = uses["counts", 0]
                dve.wait_ge(S["sum_ready"], n + 1)
                dve.tensor_tensor(keep["counts"][:], keep["counts"][:], sums[:, bank, 0:EXPERTS], ALU.add
                                  ).then_inc(S["sum_done"], 1)
                dve.tensor_tensor(rank_own[:], rank[:], one_hot[:], ALU.mult).then_inc(S["rank_picked"], 1)
                dve.wait_ge(S["rank_picked"], b + 1)
                dve.tensor_reduce(rank_sum[:], rank_own[:], AX_X, ALU.add).then_inc(S["rank_summed"], 1)
                dve.wait_ge(S["rank_summed"], b + 1)
                wait(dve, S["scattered"], 16 * TILES * b)
                dve.scalar_tensor_tensor(place[:], expert[:], float(REGION), rank_sum[:], ALU.mult, ALU.add
                                         ).then_inc(S["placed"], 1)
                dve.wait_ge(S["placed"], b + 1)
                dve.tensor_copy(keep["places"][:, bass.ds(TILES * b, TILES)], place[:]).then_inc(S["place_kept"], 1)

            def chances(b):
                dve.wait_ge(S["massed"], TILES * (b + 1))
                dve.reciprocal(chance[:], mass[:]).then_inc(S["chance_made"], 1)
                dve.wait_ge(S["chance_made"], 2 * b + 1)
                dve.tensor_scalar(x1[:, :, D + 2], chance[:], consts["gates"][:, 2:3], None, ALU.mult
                                  ).then_inc(S["chance_made"], 1)

            def add_up(uses, b, odd, i):
                n, bank = uses["back", i]
                dve.wait_ge(S["sum_ready"], n + 1)
                if i == 0:
                    wait(dve, S["scattered"], 16 * TILES * b)
                dve.wait_ge(S["x_biased"], TILES * b + i + 1)
                dve.scalar_tensor_tensor(x1[:, i, 0:D], sums[:, bank, :], consts["gates"][:, 0:1], x[:, odd, i, :],
                                         ALU.mult, ALU.add).then_inc(S["sum_done"], 1)
                if i == 0:
                    wait(dve, S["xn1_ready"], TILES * b)
                dve.wait_ge(S["sum_done"], n + 1)
                dve.bn_stats(stats1[:, i, :], x1[:, i, 0:D]).then_inc(S["stats1_made"], 1)
                wait_apart(dve, S["stats1_made"], TILES * b + i + 1, passed)
                dve.bn_aggr(moments1[:, i, :], stats1[:, i, :]).then_inc(S["moments1_made"], 1)

            dve.memset(keep["counts"][:], 0.0).then_inc(S["counted"], 1)
            dve.wait_ge(S["counted"], 1)
            dve.wait_ge(S["rows_loaded"], 16 * 3)
            dve.tensor_scalar(bo_row[:], bo_row[:], consts["gates"][:, 0:1], None, ALU.mult).then_inc(S["row_scaled"], 1)
            for i in range(TILES):
                tile_stats(0, 0, i)
            batch_moments(0)
            for i in range(TILES):
                x_lo(FIRST_TURNS, 0, i)
            for m in range(2):
                query_lo(FIRST_SUMS, 0, m)

            def iteration(b, odd, s, r, route, attend, prefetch):
                p = b - 1
                if attend:
                    peaks(b, 0)
                    query_lo(s, b, 2)
                if route:
                    routed_lo(r, p, 0)
                    routed_lo(r, p, 1)
                if attend:
                    share_values(b, 0)
                if route:
                    logits_at = gate_logits(s, p, 0)
                if attend:
                    peaks(b, 1)
                    out_lo(r, b, 0)
                if prefetch:
                    for i in range(TILES):
                        tile_stats(b + 1, 1 - odd, i)
                    batch_moments(b + 1)
                if route:
                    gate_best(p, 0, logits_at)
                if attend:
                    query_lo(s, b, 3)
                if route:
                    routed_lo(r, p, 2)
                    logits_at = gate_logits(s, p, 1)
                    routed_lo(r, p, 3)
                if attend:
                    share_values(b, 1)
                if route:
                    gate_best(p, 1, logits_at)
                if attend:
                    peaks(b, 2)
                    out_lo(r, b, 1)
                if prefetch:
                    x_lo(r, b + 1, 0)
                if route:
                    logits_at = gate_logits(s, p, 2)
                if prefetch:
                    for i in range(1, TILES):
                        x_lo(r, b + 1, i)
                if route:
                    gate_best(p, 2, logits_at)
                if attend:
                    share_values(b, 2)
                if route:
                    logits_at = gate_logits(s, p, 3)
                    gate_best(p, 3, logits_at)
                    choose(p)
                if attend:
                    peaks(b, 3)
                    out_lo(r, b, 2)
                if prefetch:
                    query_lo(s, b + 1, 0)
                if route:
                    place_rows(s, p)
                    chances(p)
                if attend:
                    share_values(b, 3)
                    out_lo(r, b, 3)
                if prefetch:
                    query_lo(s, b + 1, 1)
                if attend:
                    for i in range(TILES):
                        add_up(s, b, odd, i)

            iterations(dve, iteration)
            dve.wait_ge(S["place_kept"], BATCHES)

        @block.gpsimd
        def _(pool):
            pool.memset(half[:], -0.5).then_inc(S["filled"], 1)
            pool.wait_ge(S["filled"], 1)

            def normalize(b, odd):
                wait_apart(pool, S["moments_made"], TILES * (b + 1), passed)
                pool.tensor_scalar(spread[:], moments[:, :, 1], EPS, None, ALU.add).then_inc(S["spread_made"], 1)
                pool.tensor_scalar(offset[:], moments[:, :, 0], -1.0, None, ALU.mult).then_inc(S["mean_turned"], 1)
                pool.wait_ge(S["spread_made"], b + 1)
                pool.tensor_tensor(istd[:], spread[:], half[:], ALU.pow).then_inc(S["istd_made"], 1)
                pool.wait_ge(S["mean_turned"], b + 1)
                pool.wait_ge(S["istd_made"], b + 1)
                pool.tensor_tensor(offset[:], offset[:], istd[:], ALU.mult).then_inc(S["offset_made"], 1)
                wait_apart(pool, S["offset_made"], b + 1, passed)
                wait_apart(pool, S["x_hi"], TILES * b, passed)
                for i in range(TILES):
                    pool.tensor_scalar(xn[:, i, :], x[:, odd, i, :], istd[:, i:i + 1], offset[:, i:i + 1],
                                       ALU.mult, ALU.add).then_inc(S["xn_ready"], 1)
                pool.wait_ge(S["row_scaled"], 1)

            def add_bias(b, odd):
                for i in range(TILES):
                    pool.wait_ge(S["xn_ready"], TILES * b + i + 1)
                    pool.tensor_tensor(x[:, odd, i, :], x[:, odd, i, :], bo_row[:], ALU.add
                                       ).then_inc(S["x_biased"], 1)

            def normalize_routed(b, i):
                n = TILES * b + i + 1
                wait_apart(pool, S["moments1_made"], n, passed)
                pool.tensor_scalar(spread1[:, i:i + 1], moments1[:, i, 1:2], EPS, None, ALU.add).then_inc(S["spread1_made"], 1)
                pool.tensor_scalar(minus_mean1[:, i:i + 1], moments1[:, i, 0:1], -1.0, None, ALU.mult).then_inc(S["mean1_turned"], 1)
                pool.wait_ge(S["spread1_made"], n)
                pool.tensor_tensor(x1[:, i, D:D + 1], spread1[:, i:i + 1], half[:, 0:1], ALU.pow).then_inc(S["istd1_made"], 1)
                pool.wait_ge(S["mean1_turned"], n)
                pool.wait_ge(S["istd1_made"], n)
                pool.tensor_tensor(x1[:, i, D + 1:D + 2], minus_mean1[:, i:i + 1], x1[:, i, D:D + 1], ALU.mult
                                   ).then_inc(S["offset1_made"], 1)
                wait_apart(pool, S["offset1_made"], n, passed)
                pool.tensor_scalar(xn1[:, i, :], x1[:, i, 0:D], x1[:, i, D:D + 1], x1[:, i, D + 1:D + 2],
                                   ALU.mult, ALU.add).then_inc(S["xn1_ready"], 1)

            def scatter(b):
                pool.wait_ge(S["placed"], b + 1)
                wait_apart(pool, S["chance_made"], 2 * (b + 1), passed)
                for i in range(TILES):
                    pool.indirect_dma_start(t["routed"], bass.IndirectOffsetOnAxis(ap=place[:, i:i + 1], axis=0),
                                            x1[:, i, :], None).then_inc(S["scattered"], 16)

            normalize(0, 0)
            add_bias(0, 0)

            def iteration(b, odd, s, r, route, attend, prefetch):
                if prefetch:
                    normalize(b + 1, 1 - odd)
                    add_bias(b + 1, 1 - odd)
                if route:
                    scatter(b - 1)
                if attend:
                    for i in range(TILES):
                        normalize_routed(b, i)

            iterations(pool, iteration)
            pool.wait_ge(S["scattered"], 16 * TILES * BATCHES)


PLACES = BATCHES * TILES
SLOTS = BATCHES * TILES + EXPERTS


def run_experts(nc, t, consts, keep):
    with ExitStack() as ctx:
        mem = Memory(nc, ctx, "experts_")
        AHEAD, BUFFERS = 3, 4
        padded, padded_tiles = mem.sbuf("padded", [P, EXPERTS], I32), mem.sbuf("padded_tiles", [P, EXPERTS], I32)
        tiles, ends, stride = [mem.sbuf(n, [P, EXPERTS]) for n in ("tiles", "ends", "stride")]
        slot_i, slot = mem.sbuf("slot_i", [P, SLOTS], I32), mem.sbuf("slot", [P, SLOTS])
        past, past_rows = mem.sbuf("past", [P, SLOTS, EXPERTS]), mem.sbuf("past_rows", [P, SLOTS, EXPERTS])
        expert, row = mem.sbuf("expert", [P, SLOTS]), mem.sbuf("row", [P, SLOTS])
        expert_of, row_of = mem.sbuf("expert_of", [P, SLOTS], I32), mem.sbuf("row_of", [P, SLOTS], I32)
        routed_at, moved_by = mem.sbuf("routed_at", [P, PLACES]), mem.sbuf("moved_by", [P, PLACES])
        moves = mem.sbuf("moves", [P, PLACES, EXPERTS - 1])
        pad_at, zeros = mem.sbuf("pad_at", [P, EXPERTS], U32), mem.sbuf("zeros", [P, ROW])

        raw = [mem.sbuf(f"raw{i}", [P, CHUNKS, D]) for i in range(2)]
        w = [mem.sbuf(f"w_{h}", [P, EXPERTS, CHUNKS, D], F32R) for h in ("hi", "lo")]
        be_rows = mem.sbuf("be_rows", [P, EXPERTS, D])
        x = [mem.sbuf(f"x{i}", [P, ROW]) for i in range(BUFFERS)]
        xn = [mem.sbuf(f"xn{i}", [P, D]) for i in range(2)]
        x_t = [[mem.sbuf(f"x_t{i}_{h}", [P, CHUNKS, P], F32R) for h in ("hi", "lo")] for i in range(2)]
        before, after = [[mem.sbuf(f"{n}{i}", [P, D]) for i in range(2)] for n in ("before", "after")]
        turns, sums = mem.psum("turns", [P, 2, CHUNKS, P]), mem.psum("sums", [P, 2, D])

        planned, slots_made, zeros_made, pads_placed, pads_written = [mem.sem(n) for n in (
            "planned", "slots_made", "zeros_made", "pads_placed", "pads_written")]
        raw_loaded = [mem.sem(f"raw_loaded{i}") for i in range(2)]
        rows_loaded, weight_hi, weight_lo = mem.sem("rows_loaded"), mem.sem("weight_hi"), mem.sem("weight_lo")
        loaded = [mem.sem(f"loaded{i}") for i in range(BUFFERS)]
        stored = [mem.sem(f"stored{i}") for i in range(BUFFERS)]
        normalized, turned, turned_hi, turned_lo = [mem.sem(n) for n in (
            "normalized", "turned", "turned_hi", "turned_lo")]
        summed, biased, clipped, mixed = [mem.sem(n) for n in ("summed", "biased", "clipped", "mixed")]
        PLAN = 12
        moved = mem.sem("moved")

        passed = consts["passed"]
        ctx.callback(mem.clear_semaphores)
        block = ctx.enter_context(nc.Block())

        def tiles_in_turn(eng, tile):
            rounds = SLOTS // BUFFERS
            for k in range(BUFFERS):
                tile(0, k, BUFFERS)
            with eng.Fori(1, rounds - 1) as i:
                for k in range(BUFFERS):
                    tile(i, k, BUFFERS)
            for k in range(BUFFERS):
                tile(rounds - 1, k, BUFFERS - 1 - k)

        def expert_weights(e):
            return t["L0_ffn_We"][e].rearrange("(c p) n -> p c n", p=P)

        @block.gpsimd
        def _(pool):
            pool.iota(slot_i[:], [[1, SLOTS]], base=0, channel_multiplier=0).then_inc(slots_made, 1)
            pool.memset(zeros[:], 0.0).then_inc(zeros_made, 1)
            for e in range(2):
                pool.dma_start(raw[e][:], expert_weights(e)).then_inc(raw_loaded[e], 16)
            pool.wait_ge(zeros_made, 1)
            for e in range(EXPERTS):
                pool.dma_start(t["routed"][EXPERTS * REGION + e * P:EXPERTS * REGION + (e + 1) * P, :], zeros[:]
                               ).then_inc(pads_written, 16)
            pool.wait_ge(pads_placed, 1)
            for e in range(EXPERTS):
                pool.indirect_dma_start(t["routed"], bass.IndirectOffsetOnAxis(ap=pad_at[:, e:e + 1], axis=0),
                                        zeros[:], None).then_inc(pads_written, 16)
            for e in range(2, EXPERTS):
                pool.wait_ge(weight_lo, e - 1)
                pool.dma_start(raw[e % 2][:], expert_weights(e)).then_inc(raw_loaded[e % 2], 16)

        @block.sync
        def _(sp):
            def place_of(n):
                at = sp.value_load(row_of[0:1, bass.ds(n, 1)], min_val=0, max_val=EXPERTS * (REGION + P) - P)
                return t["routed"][bass.ds(at, P), :]

            def load(n, k):
                sp.dma_start(x[k][:], place_of(n)).then_inc(loaded[k], 16)

            def tile(i, k, left):
                n = i * BUFFERS + k
                if left >= AHEAD:
                    wait_apart(sp, stored[k - 1], 16 * (i + (k > 0)), passed)
                    load(n + AHEAD, (k + AHEAD) % BUFFERS)
                wait_apart(sp, mixed, n + 1, passed)
                sp.dma_start(results[bass.ds(n, 1)].squeeze(0), x[k][:, 0:D]).then_inc(stored[k], 16)

            results = t["results"].rearrange("(n p) d -> n p d", p=P)
            for e in range(EXPERTS):
                sp.dma_start(be_rows[:, e, :], t["L0_ffn_be"][e].partition_broadcast(P)).then_inc(rows_loaded, 16)
            sp.wait_ge(planned, PLAN)
            sp.wait_ge(pads_written, 16 * 2 * EXPERTS)
            for n in range(AHEAD):
                load(n, n)
            tiles_in_turn(sp, tile)
            for k in range(BUFFERS):
                sp.wait_ge(stored[k], 16 * SLOTS // BUFFERS)

        @block.vector
        def _(dve):
            def step(ins, n):
                ins.then_inc(planned, 1)
                dve.wait_ge(planned, n)

            def wide(small):
                return small.unsqueeze(1).broadcast_to([P, SLOTS, EXPERTS])

            counts = keep["counts"]
            dve.tensor_tensor(pad_at[:], consts["own"][:], counts[:], ALU.add).then_inc(pads_placed, 1)
            step(dve.tensor_scalar(padded[:], counts[:], float(P - 1), None, ALU.add), 1)
            step(dve.tensor_scalar(padded_tiles[:], padded[:], P.bit_length() - 1, None, ALU.arith_shift_right), 2)
            step(dve.tensor_copy(tiles[:], padded_tiles[:]), 3)
            dve.tensor_scalar(stride[:], tiles[:], -float(P), float(REGION), ALU.mult, ALU.add).then_inc(planned, 1)
            dve.wait_ge(planned, 4)
            step(dve.tensor_tensor_scan(ends[:], tiles[:], tiles[:], 0.0, ALU.add, ALU.bypass), 5)
            dve.wait_ge(slots_made, 1)
            step(dve.tensor_copy(slot[:], slot_i[:]), 6)
            step(dve.tensor_tensor(past[:], slot[:].unsqueeze(2).broadcast_to([P, SLOTS, EXPERTS]), wide(ends[:]),
                                   ALU.is_ge), 7)
            step(dve.tensor_reduce(expert[:], past[:], AX_X, ALU.add), 8)
            step(dve.tensor_tensor(past_rows[:], past[:], wide(stride[:]), ALU.mult), 9)
            step(dve.tensor_reduce(row[:], past_rows[:], AX_X, ALU.add), 10)
            dve.tensor_scalar(expert_of[:], expert[:], float(EXPERTS - 1), None, ALU.min).then_inc(planned, 1)
            dve.scalar_tensor_tensor(row_of[:], slot[:], float(P), row[:], ALU.mult, ALU.add).then_inc(planned, 1)

            dve.tensor_copy(routed_at[:], keep["places"][:]).then_inc(moved, 1)
            dve.wait_ge(moved, 1)
            for e in range(EXPERTS - 1):
                dve.tensor_scalar(moves[:, :, e], routed_at[:], float((e + 1) * REGION), stride[:, e:e + 1],
                                  ALU.is_ge, ALU.mult).then_inc(moved, 1)
            dve.wait_ge(moved, EXPERTS)
            dve.tensor_reduce(moved_by[:], moves[:], AX_X, ALU.add).then_inc(moved, 1)
            dve.wait_ge(moved, EXPERTS + 1)
            dve.tensor_tensor(keep["places"][:], routed_at[:], moved_by[:], ALU.subtract).then_inc(moved, 1)
            dve.wait_ge(moved, EXPERTS + 2)

            for e in range(EXPERTS):
                dve.wait_ge(weight_hi, e + 1)
                dve.tensor_tensor(w[1][:, e], raw[e % 2][:], w[0][:, e].bitcast(F32), ALU.subtract
                                  ).then_inc(weight_lo, 1)
            dve.wait_ge(rows_loaded, 16 * EXPERTS)

            def turn_lo(n, k):
                dve.wait_ge(turned_hi, n + 1)
                hi, lo = x_t[k % 2]
                dve.tensor_tensor(lo[:], turns[:, k % 2], hi[:].bitcast(F32), ALU.subtract).then_inc(turned_lo, 1)

            turn_lo(0, 0)

            def tile(i, k, left):
                n = i * BUFFERS + k
                if left:
                    turn_lo(n + 1, k + 1)
                e = dve.value_load(expert_of[0:1, bass.ds(n, 1)], min_val=0, max_val=EXPERTS - 1)
                dve.wait_ge(summed, n + 1)
                wait(dve, clipped, n - 1)
                dve.tensor_tensor(before[k % 2][:], sums[:, k % 2, :], be_rows[:, bass.ds(e, 1), :].squeeze(1), ALU.add
                                  ).then_inc(biased, 1)
                dve.wait_ge(clipped, n + 1)
                dve.scalar_tensor_tensor(x[k][:, 0:D], after[k % 2][:], x[k][:, D + 2:D + 3], x[k][:, 0:D],
                                         ALU.mult, ALU.add).then_inc(mixed, 1)

            tiles_in_turn(dve, tile)

        @block.scalar
        def _(act):
            for e in range(EXPERTS):
                act.wait_ge(raw_loaded[e % 2], 16 * (e // 2 + 1))
                act.activation(w[0][:, e], raw[e % 2][:], ACT.Copy).then_inc(weight_hi, 1)

            def normalize(loads, n, k):
                act.wait_ge(loaded[k], 16 * loads)
                act.activation(xn[k % 2][:], x[k][:, 0:D], ACT.Identity, bias=x[k][:, D + 1:D + 2],
                               scale=x[k][:, D:D + 1]).then_inc(normalized, 1)

            def turn_hi(n, k):
                act.wait_ge(turned, n + 1)
                act.activation(x_t[k % 2][0][:], turns[:, k % 2], ACT.Copy).then_inc(turned_hi, 1)

            normalize(1, 0, 0)
            normalize(1, 1, 1)
            turn_hi(0, 0)

            def tile(i, k, left):
                n = i * BUFFERS + k
                if left:
                    turn_hi(n + 1, k + 1)
                if left > 1:
                    normalize(i + 1 + (k + 2) // BUFFERS, n + 2, (k + 2) % BUFFERS)
                act.wait_ge(biased, n + 1)
                wait(act, mixed, n - 1)
                act.activation(after[k % 2][:], before[k % 2][:], ACT.Relu).then_inc(clipped, 1)

            tiles_in_turn(act, tile)

        @block.tensor
        def _(pe):
            def turn(n, k):
                pe.wait_ge(normalized, n + 1)
                for c in range(CHUNKS):
                    last = pe.transpose(turns[:, k % 2, c, :], xn[k % 2][:, c * P:(c + 1) * P], consts["ident"][:])
                last.then_inc(turned, 1)

            pe.wait_ge(planned, PLAN)
            turn(0, 0)
            pe.wait_ge(weight_lo, EXPERTS)

            def tile(i, k, left):
                n = i * BUFFERS + k
                if left:
                    turn(n + 1, k + 1)
                e = pe.value_load(expert_of[0:1, bass.ds(n, 1)], min_val=0, max_val=EXPERTS - 1)
                pe.wait_ge(turned_lo, n + 1)
                wait(pe, biased, n - 1)
                for c in range(CHUNKS):
                    last = three_pass(pe, sums[:, k % 2, :], [h[:, c, :] for h in x_t[k % 2]],
                                      [h[:, bass.ds(e, 1), c, :].squeeze(1) for h in w], c == 0, c == CHUNKS - 1)
                last.then_inc(summed, 1)

            tiles_in_turn(pe, tile)


WEIGHT_COUNT = float(D * D)
ROUNDER = 1.5 * 2 ** 23


def quantize_weights(nc, t, consts, keep):
    with ExitStack() as ctx:
        mem = Memory(nc, ctx, "quantize_")
        w = mem.sbuf("w", [P, CHUNKS, D])
        above, below = mem.sbuf("above", [P, CHUNKS, D]), mem.sbuf("below", [P, CHUNKS, D])
        ternary = mem.sbuf("ternary", [P, CHUNKS, D], BF16)
        magnitude, total, threshold = [mem.sbuf(n, [P, 1]) for n in ("magnitude", "total", "threshold")]
        turns = mem.psum("turns", [P, CHUNKS, 2 * D], BF16)
        loaded, magnitudes_summed, totalled, thresholds_made, compared, made, turned, kept = [mem.sem(n) for n in (
            "loaded", "magnitudes_summed", "totalled", "thresholds_made", "compared", "made", "turned", "kept")]
        ctx.callback(mem.clear_semaphores)
        with nc.Block() as block:
            @block.sync
            def _(sp):
                sp.dma_start(w[:], t["L1_ffn_weight"].rearrange("(c p) k -> p c k", p=P)).then_inc(loaded, 16)

            @block.gpsimd
            def _(pool):
                pool.wait_ge(magnitudes_summed, 1)
                pool.partition_all_reduce(total[:], magnitude[:], P, bass.bass_isa.ReduceOp.add).then_inc(totalled, 1)

            @block.vector
            def _(dve):
                dve.wait_ge(loaded, 16)
                dve.tensor_reduce(magnitude[:], w[:], mybir.AxisListType.XY, ALU.add, apply_absolute_value=True
                                  ).then_inc(magnitudes_summed, 1)
                dve.wait_ge(totalled, 1)
                dve.tensor_scalar(keep["w_scale"][:], total[:], 1 / WEIGHT_COUNT, None, ALU.mult).then_inc(thresholds_made, 1)
                dve.tensor_scalar(threshold[:], total[:], 0.5 / WEIGHT_COUNT, None, ALU.mult).then_inc(thresholds_made, 1)
                dve.wait_ge(thresholds_made, 2)
                dve.tensor_scalar(above[:], w[:], threshold[:], None, ALU.is_gt).then_inc(compared, 1)
                dve.tensor_scalar(below[:], w[:], -1.0, threshold[:], ALU.mult, ALU.is_gt).then_inc(compared, 1)
                dve.wait_ge(compared, 2)
                dve.tensor_tensor(ternary[:], above[:], below[:], ALU.subtract).then_inc(made, 1)

            @block.tensor
            def _(pe):
                pe.wait_ge(made, 1)
                pe.wait_ge(consts["ready"], consts["made"])
                for c in range(CHUNKS):
                    for o in range(CHUNKS):
                        last = pe.transpose(turns[:, c, o * P:(o + 1) * P], ternary[:, o, c * P:(c + 1) * P],
                                            consts["ident_half"][:])
                    last.then_inc(turned, 1)

            @block.scalar
            def _(act):
                for c in range(CHUNKS):
                    act.wait_ge(turned, c + 1)
                    act.activation(keep["ternary_t"][:, c, :], turns[:, c, 0:D], ACT.Copy).then_inc(kept, 1)
                act.wait_ge(kept, CHUNKS)


def attend_context(nc, t, consts, keep, x3):
    with ExitStack() as ctx:
        mem = Memory(nc, ctx, "context_")
        BUFFERS = 3
        place = [mem.sbuf(f"place{i}", [P, TILES], U32) for i in range(2)]
        x = [mem.sbuf(f"x{i}", [P, TILES, D]) for i in range(BUFFERS)]
        stats, moments = mem.sbuf("stats", [P, TILES, 6]), mem.sbuf("moments", [P, TILES, 2])
        stats3, moments3 = mem.sbuf("stats3", [P, TILES, 6]), mem.sbuf("moments3", [P, TILES, 2])
        spread, istd, offset, half = [mem.sbuf(n, [P, TILES]) for n in ("spread", "istd", "offset", "half")]
        spread3 = mem.sbuf("spread3", [P, TILES])
        istd3, offset3 = [[mem.sbuf(f"{n}{i}", [P, TILES]) for i in range(2)] for n in ("istd3_", "offset3_")]
        xn = mem.sbuf("xn", [P, TILES, D])
        x_t = [mem.sbuf(f"x_t_{h}", [P, CHUNKS, SEQ], F32R) for h in ("hi", "lo")]
        keys = mem.sbuf("keys", [P, 2, CHUNKS, KEYS], F32R)
        key_bias = mem.sbuf("key_bias", [P, 1])
        values = mem.sbuf("values", [P, 2, D], F32R)
        scores = mem.sbuf("scores", [P, SEQ])
        peak, minus_peak = mem.sbuf("peak", [P, TILES]), mem.sbuf("minus_peak", [P, TILES])
        probs = mem.sbuf("probs", [P, TILES, KEYS])
        total = mem.sbuf("total", [P, TILES])
        share, gain = mem.sbuf("share", [P, TILES]), mem.sbuf("gain", [P, TILES])
        probs_t = [mem.sbuf(f"probs_t_{h}", [P, SEQ], F32R) for h in ("hi", "lo")]
        x3n = [mem.sbuf(f"x3n{i}", [P, D]) for i in range(2)]
        largest = mem.sbuf("largest", [P, TILES])

        score_bank, score_turns, prob_turns = mem.psum("score_bank", [P, SEQ]), mem.psum("score_turns", [P, TILES, P]), \
            mem.psum("prob_turns", [P, TILES, P])
        turns, sums = mem.psum("turns", [P, 2, CHUNKS, P]), mem.psum("sums", [P, 2, D])

        S = {n: mem.sem(n) for n in (
            "filled", "placed", "gathered", "keys_loaded", "bias_loaded", "values_loaded",
            "stats_made", "moments_made", "spread_made", "mean_turned", "istd_made", "offset_made", "xn_ready",
            "turned", "turned_hi", "turned_lo", "scored", "scores_ready", "scores_turned", "peaked", "peak_turned",
            "weighed", "probs_turned", "probs_hi", "probs_lo", "inverted", "gain_made", "attended", "mixed",
            "stats3_made", "moments3_made", "spread3_made", "mean3_turned", "istd3_made", "offset3_made",
            "x3n_ready", "largest_made", "largest_kept", "moments3_kept")}
        passed = consts["passed"]
        LEAD = 2
        START = 1

        def rounds(eng, iteration):
            def at(j):
                iteration(j, j, score=j < BATCHES, turn=j + 1 < BATCHES, fetch=j + 2 < BATCHES,
                          mix=1 <= j <= BATCHES, measure=j >= LEAD)

            for j in range(LEAD):
                at(j)
            step = 2 * BUFFERS
            with eng.Fori(0, (BATCHES - 2 - LEAD) // step) as i:
                for k in range(step):
                    iteration(i * step + LEAD + k, LEAD + k, score=True, turn=True, fetch=True, mix=True, measure=True)
            for j in range(BATCHES - 2, BATCHES + LEAD):
                at(j)

        block = ctx.enter_context(nc.Block())

        @block.sync
        def _(sp):
            def load_keys(b):
                sp.dma_start(keys[:].bitcast(F32), t["fold_pairs"][b]).then_inc(S["keys_loaded"], 16)

            def load_bias(b):
                sp.dma_start(key_bias[0:KEYS], t["fold_biases"][b]).then_inc(S["bias_loaded"], 16)

            load_keys(0)
            load_bias(0)

            def iteration(j, k, score, turn, fetch, mix, measure):
                if turn:
                    wait_apart(sp, S["scored"], j + 1, passed)
                    load_keys(j + 1)
                    wait_apart(sp, S["scores_ready"], j + 1, passed)
                    load_bias(j + 1)
                if score:
                    wait_apart(sp, S["attended"], TILES * j, passed)
                    sp.dma_start(values[0:KEYS].bitcast(F32), t["v1_pairs"][j]).then_inc(S["values_loaded"], 16)

            rounds(sp, iteration)

        @block.gpsimd
        def _(pool):
            def gather(b, k):
                wait_apart(pool, S["gathered"], 16 * TILES * b, passed)
                pool.tensor_copy(place[k % 2][:], keep["places"][:, bass.ds(TILES * b, TILES)]).then_inc(S["placed"], 1)
                wait(pool, S["mixed"], max(TILES * (b - 2), 0) if isinstance(b, int) else TILES * (b - 2))
                wait_apart(pool, S["placed"], b + 1, passed)
                for i in range(TILES):
                    pool.indirect_dma_start(x[k % BUFFERS][:, i, :], None, t["results"],
                                            bass.IndirectOffsetOnAxis(ap=place[k % 2][:, i:i + 1], axis=0)
                                            ).then_inc(S["gathered"], 16)

            def scale_of(b, moments, spread, istd, offset, names):
                moments_made, spread_made, mean_turned, istd_made, offset_made = [S[n] for n in names]
                wait_apart(pool, moments_made, TILES * (b + 1), passed)
                pool.tensor_scalar(spread[:], moments[:, :, 1], EPS, None, ALU.add).then_inc(spread_made, 1)
                pool.tensor_scalar(offset[:], moments[:, :, 0], -1.0, None, ALU.mult).then_inc(mean_turned, 1)
                pool.wait_ge(spread_made, b + 1)
                pool.tensor_tensor(istd[:], spread[:], half[:], ALU.pow).then_inc(istd_made, 1)
                pool.wait_ge(mean_turned, b + 1)
                pool.wait_ge(istd_made, b + 1)
                pool.tensor_tensor(offset[:], offset[:], istd[:], ALU.mult).then_inc(offset_made, 1)

            def normalize(b, k):
                scale_of(b, moments, spread, istd, offset,
                         ("moments_made", "spread_made", "mean_turned", "istd_made", "offset_made"))
                wait(pool, S["turned"], TILES * b)
                wait_apart(pool, S["offset_made"], b + 1, passed)
                for i in range(TILES):
                    pool.tensor_scalar(xn[:, i, :], x[k % BUFFERS][:, i, :], istd[:, i:i + 1], offset[:, i:i + 1],
                                       ALU.mult, ALU.add).then_inc(S["xn_ready"], 1)

            pool.memset(half[:], -0.5).then_inc(S["filled"], 1)
            pool.wait_ge(S["filled"], 1)
            gather(0, 0)
            gather(1, 1)
            normalize(0, 0)
            normalize(1, 1)

            def iteration(j, k, score, turn, fetch, mix, measure):
                if fetch:
                    gather(j + 2, k + 2)
                if mix:
                    if not (isinstance(j, int) and j < LEAD):
                        wait_apart(pool, S["x3n_ready"], START + TILES * (j - 2), passed)
                        wait_apart(pool, S["moments3_kept"], START + 2 * (j - 2), passed)
                    scale_of(j - 1, moments3, spread3, istd3[(k - 1) % 2], offset3[(k - 1) % 2],
                             ("moments3_made", "spread3_made", "mean3_turned", "istd3_made", "offset3_made"))
                if fetch:
                    normalize(j + 2, k + 2)

            rounds(pool, iteration)

        @block.tensor
        def _(pe):
            def turn_x(b):
                for i in range(TILES):
                    n = TILES * b + i
                    pe.wait_ge(S["xn_ready"], n + 1)
                    if not (isinstance(n, int) and n < 2):
                        pe.wait_ge(S["turned_lo"], n - 1)
                    for c in range(CHUNKS):
                        last = pe.transpose(turns[:, i % 2, c, :], xn[:, i, c * P:(c + 1) * P], consts["ident"][:])
                    last.then_inc(S["turned"], 1)

            turn_x(0)

            def iteration(j, k, score, turn, fetch, mix, measure):
                if score:
                    pe.wait_ge(S["turned_lo"], TILES * (j + 1))
                    pe.wait_ge(S["keys_loaded"], 16 * (j + 1))
                    wait(pe, S["scores_ready"], j)
                    for c in range(CHUNKS):
                        last = three_pass(pe, score_bank[0:KEYS, :], [keys[:, h, c, :] for h in range(2)],
                                          [h[:, c, :] for h in x_t], c == 0, c == CHUNKS - 1)
                    last.then_inc(S["scored"], 1)
                if turn:
                    turn_x(j + 1)
                if score:
                    pe.wait_ge(S["scores_ready"], j + 1)
                    wait(pe, S["weighed"], TILES * j)
                    for i in range(TILES):
                        last = pe.transpose(score_turns[:, i, 0:KEYS], scores[0:KEYS, i * P:(i + 1) * P],
                                            consts["ident"][0:KEYS, 0:KEYS])
                    last.then_inc(S["scores_turned"], 1)
                if mix:
                    pe.wait_ge(S["probs_lo"], j)
                    pe.wait_ge(S["values_loaded"], 16 * j)
                    for i in range(TILES):
                        n = TILES * (j - 1) + i
                        if not (isinstance(n, int) and n < 2):
                            pe.wait_ge(S["mixed"], n - 1)
                        three_pass(pe, sums[:, i % 2, :], [h[0:KEYS, i * P:(i + 1) * P] for h in probs_t],
                                   [values[0:KEYS, h, :] for h in range(2)]).then_inc(S["attended"], 1)
                if score:
                    pe.wait_ge(S["weighed"], TILES * (j + 1))
                    for i in range(TILES):
                        last = pe.transpose(prob_turns[0:KEYS, i, :], probs[:, i, :], consts["ident"][:])
                    last.then_inc(S["probs_turned"], 1)

            rounds(pe, iteration)

        @block.scalar
        def _(act):
            def turn_hi(b):
                for i in range(TILES):
                    act.wait_ge(S["turned"], TILES * b + i + 1)
                    act.activation(x_t[0][:, :, i * P:(i + 1) * P], turns[:, i % 2], ACT.Copy).then_inc(S["turned_hi"], 1)

            act.sem_inc(S["x3n_ready"], START)
            turn_hi(0)

            def iteration(j, k, score, turn, fetch, mix, measure):
                if score:
                    act.wait_ge(S["bias_loaded"], 16 * (j + 1))
                    wait(act, S["scores_turned"], j)
                    act.wait_ge(S["scored"], j + 1)
                    act.activation(scores[0:KEYS, :], score_bank[0:KEYS, :], ACT.Identity, bias=key_bias[0:KEYS, :],
                                   scale=D ** -0.5).then_inc(S["scores_ready"], 1)
                if turn:
                    turn_hi(j + 1)
                if score:
                    act.wait_ge(S["peak_turned"], j + 1)
                    wait(act, S["probs_turned"], j)
                    wait(act, S["inverted"], j)
                    for i in range(TILES):
                        act.activation(probs[:, i, :], score_turns[:, i, 0:KEYS], ACT.Exp, bias=minus_peak[:, i:i + 1],
                                       accum_out=total[:, i:i + 1]).then_inc(S["weighed"], 1)
                if measure:
                    for i in range(TILES):
                        n = TILES * (j - 2) + i
                        if not (isinstance(n, int) and n < 2):
                            act.wait_ge(S["largest_made"], START + n - min(i, 1))
                        wait_apart(act, S["offset3_made"], j - 1, passed)
                        act.activation(x3n[i % 2][:], x3[:, bass.ds(n, 1), :].squeeze(1), ACT.Identity,
                                       bias=offset3[k % 2][:, i:i + 1], scale=istd3[k % 2][:, i:i + 1]
                                       ).then_inc(S["x3n_ready"], 1)
                if score:
                    act.wait_ge(S["probs_turned"], j + 1)
                    wait(act, S["attended"], TILES * j)
                    act.activation(probs_t[0][0:KEYS, :], prob_turns[0:KEYS].rearrange("p i n -> p (i n)"), ACT.Copy
                                   ).then_inc(S["probs_hi"], 1)

            rounds(act, iteration)

        @block.vector
        def _(dve):
            def tile_stats(b, k):
                dve.wait_ge(S["gathered"], 16 * TILES * (b + 1))
                wait(dve, S["mean_turned"], b)
                wait(dve, S["spread_made"], b)
                for i in range(TILES):
                    dve.bn_stats(stats[:, i, :], x[k % BUFFERS][:, i, :]).then_inc(S["stats_made"], 1)
                for i in range(TILES):
                    wait_apart(dve, S["stats_made"], TILES * b + i + 1, passed)
                    dve.bn_aggr(moments[:, i, :], stats[:, i, :]).then_inc(S["moments_made"], 1)

            def turn_lo(b):
                for i in range(TILES):
                    dve.wait_ge(S["turned_hi"], TILES * b + i + 1)
                    hi, lo = [h[:, :, i * P:(i + 1) * P] for h in x_t]
                    dve.tensor_tensor(lo, turns[:, i % 2], hi.bitcast(F32), ALU.subtract).then_inc(S["turned_lo"], 1)

            dve.sem_inc(S["moments3_kept"], START)
            dve.sem_inc(S["largest_made"], START)
            tile_stats(0, 0)
            turn_lo(0)
            tile_stats(1, 1)

            def iteration(j, k, score, turn, fetch, mix, measure):
                if turn:
                    turn_lo(j + 1)
                if score:
                    dve.wait_ge(S["scores_turned"], j + 1)
                    dve.tensor_reduce(peak[:], score_turns[:, :, 0:KEYS], AX_X, ALU.max).then_inc(S["peaked"], 1)
                    dve.wait_ge(S["peaked"], j + 1)
                    dve.tensor_scalar(minus_peak[:], peak[:], -1.0, None, ALU.mult).then_inc(S["peak_turned"], 1)
                if mix:
                    wait(dve, S["spread3_made"], j - 1)
                    wait(dve, S["mean3_turned"], j - 1)
                    for i in range(TILES):
                        n = TILES * (j - 1) + i
                        dve.wait_ge(S["gain_made"], j)
                        dve.wait_ge(S["attended"], n + 1)
                        out = x3[:, bass.ds(n, 1), :].squeeze(1)
                        dve.scalar_tensor_tensor(out, sums[:, i % 2, :], gain[:, i:i + 1],
                                                 x[(k - 1) % BUFFERS][:, i, :], ALU.mult, ALU.add).then_inc(S["mixed"], 1)
                    for i in range(TILES):
                        n = TILES * (j - 1) + i
                        wait_apart(dve, S["mixed"], n + 1, passed)
                        dve.bn_stats(stats3[:, i, :], x3[:, bass.ds(n, 1), :].squeeze(1)).then_inc(S["stats3_made"], 1)
                if measure:
                    wait(dve, S["largest_kept"], j - 2 + 1)
                    for i in range(TILES):
                        dve.wait_ge(S["x3n_ready"], START + TILES * (j - 2) + i + 1)
                        dve.tensor_reduce(largest[:, i:i + 1], x3n[i % 2][:], AX_X, ALU.max, apply_absolute_value=True
                                          ).then_inc(S["largest_made"], 1)
                    wait_apart(dve, S["offset3_made"], j - 1, passed)
                    dve.tensor_copy(keep["istd3"][:, bass.ds(TILES * (j - 2), TILES)], istd3[k % 2][:]
                                    ).then_inc(S["moments3_kept"], 1)
                    dve.tensor_copy(keep["offset3"][:, bass.ds(TILES * (j - 2), TILES)], offset3[k % 2][:]
                                    ).then_inc(S["moments3_kept"], 1)
                if mix:
                    for i in range(TILES):
                        n = TILES * (j - 1) + i
                        wait_apart(dve, S["stats3_made"], n + 1, passed)
                        dve.bn_aggr(moments3[:, i, :], stats3[:, i, :]).then_inc(S["moments3_made"], 1)
                if measure:
                    dve.wait_ge(S["largest_made"], START + TILES * (j - 1))
                    dve.tensor_tensor(keep["largest"][:], keep["largest"][:], largest[:], ALU.max
                                      ).then_inc(S["largest_kept"], 1)
                if score:
                    dve.wait_ge(S["weighed"], TILES * (j + 1))
                    wait(dve, S["mixed"], TILES * j)
                    dve.reciprocal(share[:], total[:]).then_inc(S["inverted"], 1)
                    dve.wait_ge(S["inverted"], j + 1)
                    dve.tensor_scalar(gain[:], share[:], consts["gates"][:, 1:2], None, ALU.mult).then_inc(S["gain_made"], 1)
                    dve.wait_ge(S["probs_hi"], j + 1)
                    dve.tensor_tensor(probs_t[1][0:KEYS, :], prob_turns[0:KEYS].rearrange("p i n -> p (i n)"),
                                      probs_t[0][0:KEYS, :].bitcast(F32), ALU.subtract).then_inc(S["probs_lo"], 1)
                if fetch:
                    tile_stats(j + 2, k + 2)

            dve.memset(keep["largest"][:], 0.0).then_inc(S["largest_kept"], 1)
            rounds(dve, iteration)


def quantized_layer(nc, t, consts, keep, x3):
    with ExitStack() as ctx:
        mem = Memory(nc, ctx, "quantized_")
        COUNT = BATCHES * TILES
        ROUND = 4
        bias_row = mem.sbuf("bias_row", [P, D])
        top, largest, unit, per_unit, gain = [mem.sbuf(n, [P, 1]) for n in ("top", "largest", "unit", "per_unit", "gain")]
        scale, offset = mem.sbuf("scale", [P, COUNT]), mem.sbuf("offset", [P, COUNT])
        scaled = [mem.sbuf(f"scaled{i}", [P, D]) for i in range(2)]
        whole = [mem.sbuf(f"whole{i}", [P, D], BF16) for i in range(2)]
        whole_t = [mem.sbuf(f"whole_t{i}", [P, CHUNKS, P], BF16) for i in range(2)]
        turns = mem.psum("turns", [P, 2, 2 * D], BF16)
        sums = mem.psum("sums", [P, 2, D])
        S = {n: mem.sem(n) for n in ("row_loaded", "row_scaled", "step", "reduced", "scaled", "rounded", "turned", "turned_kept",
                                     "summed", "biased", "mixed", "stored")}
        passed = consts["passed"]

        def tiles_in_turn(eng, tile):
            for k in range(ROUND):
                tile(k, k, ROUND)
            with eng.Fori(1, COUNT // ROUND - 1) as i:
                for k in range(ROUND):
                    tile(i * ROUND + k, k, ROUND)
            for k in range(ROUND):
                tile(COUNT - ROUND + k, k, ROUND - 1 - k)

        def row(n):
            return x3[:, bass.ds(n, 1), :].squeeze(1)

        block = ctx.enter_context(nc.Block())

        @block.sync
        def _(sp):
            sp.dma_start(bias_row[:], t["L1_ffn_bias"].partition_broadcast(P)).then_inc(S["row_loaded"], 16)
            out = t["out"].rearrange("b (i p) d -> (b i) p d", p=P)

            def tile(n, k, left):
                wait_apart(sp, S["mixed"], n + 1, passed)
                sp.dma_start(out[bass.ds(n, 1)].squeeze(0), row(n)).then_inc(S["stored"], 16)

            tiles_in_turn(sp, tile)
            sp.wait_ge(S["stored"], 16 * COUNT)

        @block.gpsimd
        def _(pool):
            pool.wait_ge(S["step"], 1)
            pool.partition_all_reduce(largest[:], top[:], P, bass.bass_isa.ReduceOp.max).then_inc(S["reduced"], 1)
            pool.wait_ge(S["row_scaled"], 1)

            def tile(n, k, left):
                wait_apart(pool, S["scaled"], n + 1, passed)
                pool.tensor_tensor(row(n), row(n), bias_row[:], ALU.add).then_inc(S["biased"], 1)

            tiles_in_turn(pool, tile)

        @block.vector
        def _(dve):
            dve.tensor_reduce(top[:], keep["largest"][:], AX_X, ALU.max).then_inc(S["step"], 1)
            dve.wait_ge(S["row_loaded"], 16)
            dve.tensor_scalar(bias_row[:], bias_row[:], consts["gates"][:, 3:4], None, ALU.mult).then_inc(S["row_scaled"], 1)
            dve.wait_ge(S["reduced"], 1)
            dve.tensor_scalar(unit[:], largest[:], 1 / 127.0, None, ALU.mult).then_inc(S["step"], 1)
            dve.wait_ge(S["step"], 2)
            dve.reciprocal(per_unit[:], unit[:]).then_inc(S["step"], 1)
            dve.tensor_scalar(gain[:], unit[:], keep["w_scale"][:], consts["gates"][:, 3:4], ALU.mult, ALU.mult
                              ).then_inc(S["step"], 1)
            dve.wait_ge(S["step"], 4)
            dve.tensor_scalar(scale[:], keep["istd3"][:], per_unit[:], None, ALU.mult).then_inc(S["step"], 1)
            dve.tensor_scalar(offset[:], keep["offset3"][:], per_unit[:], None, ALU.mult).then_inc(S["step"], 1)
            dve.wait_ge(S["step"], 6)

            def scale_tile(n, k):
                wait(dve, S["rounded"], n - 1)
                dve.tensor_scalar(scaled[k % 2][:], row(n), scale[:, bass.ds(n, 1)], offset[:, bass.ds(n, 1)],
                                  ALU.mult, ALU.add).then_inc(S["scaled"], 1)

            def round_tile(n, k):
                wait(dve, S["turned"], n - 1)
                dve.wait_ge(S["scaled"], n + 1)
                dve.tensor_scalar(whole[k % 2][:], scaled[k % 2][:], ROUNDER, ROUNDER, ALU.add, ALU.subtract
                                  ).then_inc(S["rounded"], 1)

            for n in range(2):
                scale_tile(n, n)
                round_tile(n, n)

            def tile(n, k, left):
                if left > 1:
                    scale_tile(n + 2, k + 2)
                dve.wait_ge(S["biased"], n + 1)
                dve.wait_ge(S["summed"], n + 1)
                dve.scalar_tensor_tensor(row(n), sums[:, k % 2, :], gain[:], row(n), ALU.mult, ALU.add
                                         ).then_inc(S["mixed"], 1)
                if left > 1:
                    round_tile(n + 2, k + 2)

            tiles_in_turn(dve, tile)

        @block.tensor
        def _(pe):
            def turn(n, k):
                pe.wait_ge(S["rounded"], n + 1)
                wait(pe, S["turned_kept"], n - 1)
                for c in range(CHUNKS):
                    last = pe.transpose(turns[:, k % 2, c * P:(c + 1) * P], whole[k % 2][:, c * P:(c + 1) * P],
                                        consts["ident_half"][:])
                last.then_inc(S["turned"], 1)

            turn(0, 0)

            def tile(n, k, left):
                if left:
                    turn(n + 1, k + 1)
                pe.wait_ge(S["turned_kept"], n + 1)
                wait(pe, S["mixed"], n - 1)
                for c in range(CHUNKS):
                    last = pe.matmul(sums[:, k % 2, :], whole_t[k % 2][:, c, :], keep["ternary_t"][:, c, :],
                                     start=c == 0, stop=c == CHUNKS - 1)
                last.then_inc(S["summed"], 1)

            tiles_in_turn(pe, tile)

        @block.scalar
        def _(act):
            def tile(n, k, left):
                act.wait_ge(S["turned"], n + 1)
                wait(act, S["summed"], n - 1)
                act.activation(whole_t[k % 2][:], turns[:, k % 2, 0:D].rearrange("p (c n) -> p c n", n=P), ACT.Copy
                               ).then_inc(S["turned_kept"], 1)

            tiles_in_turn(act, tile)


def flamingo(nc, t):
    with ExitStack() as ctx:
        mem = Memory(nc, ctx)
        t.update(scratch(nc))
        consts = constants(nc, mem, t)
        keep = {"counts": mem.sbuf("counts", [P, EXPERTS]), "places": mem.sbuf("places", [P, BATCHES * TILES], U32),
                "w_scale": mem.sbuf("w_scale", [P, 1]), "ternary_t": mem.sbuf("ternary_t", [P, CHUNKS, D], BF16),
                "istd3": mem.sbuf("istd3", [P, BATCHES * TILES]), "offset3": mem.sbuf("offset3", [P, BATCHES * TILES]),
                "largest": mem.sbuf("largest", [P, TILES])}
        quantize_weights(nc, t, consts, keep)
        with ExitStack() as first:
            weights = Memory(nc, first)
            hold = {n: [weights.sbuf(f"{n}_{h}", [P, CHUNKS, D], F32R) for h in ("hi", "lo")] for n in ("wq", "wo", "wg")}
            prepare(nc, hold, t, consts)
            attend_and_route(nc, hold, t, consts, keep)
        run_experts(nc, t, consts, keep)
        x3 = mem.sbuf("x3", [P, BATCHES * TILES, D])
        attend_context(nc, t, consts, keep, x3)
        quantized_layer(nc, t, consts, keep, x3)


_INS = ['x', 'ctx_1024', 'g_xattn', 'g_ffn', 'L0_xattn_Wq', 'L0_xattn_bq', 'L0_xattn_Wkv', 'L0_xattn_bkv',
        'L0_xattn_Wo', 'L0_xattn_bo', 'L0_ffn_Wg', 'L0_ffn_bg', 'L0_ffn_We', 'L0_ffn_be', 'L1_xattn_Wq',
        'L1_xattn_bq', 'L1_ffn_weight', 'L1_ffn_bias']


def kernel(**inputs):
    import numpy as _np
    import concourse.bacc as _bacc
    from concourse import mybir as _mybir
    from concourse.bass_utils import run_bass_kernel_spmd as _run

    nc = _bacc.Bacc("TRN2", target_bir_lowering=False, num_devices=1)
    arrays, tensors = {}, {}
    for name in _INS:
        a = _np.ascontiguousarray(inputs[name])
        arrays[f"in_{name}"] = a
        tensors[name] = nc.dram_tensor(f"in_{name}", a.shape, _mybir.dt.from_np(a.dtype), kind="ExternalInput").ap()
    tensors["out"] = nc.dram_tensor("out_x", (BATCHES, SEQ, D), F32, kind="ExternalOutput").ap()
    flamingo(nc, tensors)
    return _run(nc, [arrays], core_ids=[0]).results[0]["out_x"]
```

```python
from contextlib import ExitStack

import concourse.bass as bass
from concourse import mybir

F32 = mybir.dt.float32
F32R = mybir.dt.float32r
BF16 = mybir.dt.bfloat16
U32 = mybir.dt.uint32
I32 = mybir.dt.int32
ALU = mybir.AluOpType
ACT = mybir.ActivationFunctionType
AX_X = mybir.AxisListType.X

P = 128
BATCHES, SEQ, D = 16, 512, 512
KEYS = 120
TILES = SEQ // P
CHUNKS = D // P
HEADS = 16
HEAD = D // HEADS
GROUP = P // HEAD
GROUPS = HEADS // GROUP
EXPERTS = 8
REGION = BATCHES * SEQ + P
ROW = D + 4
RESULT = D + 2
SLOTS = BATCHES * TILES + EXPERTS
RESULTS_AT = SLOTS * P
EPS = 1e-5


class Memory:

    def __init__(self, nc, ctx, phase=""):
        self.nc, self.ctx, self.phase, self.sems = nc, ctx, phase, []

    def sbuf(self, name, shape, dtype=F32):
        return self.ctx.enter_context(self.nc.sbuf_tensor(self.phase + name, shape, dtype))

    def psum(self, name, shape, dtype=F32):
        return self.ctx.enter_context(self.nc.psum_tensor(self.phase + name, shape, dtype))

    def sem(self, name):
        self.sems.append(self.nc.alloc_semaphore(name=self.phase + name))
        return self.sems[-1]

    def clear_semaphores(self):
        self.nc.clear_and_free_semaphores(self.sems)
        self.nc.all_engine_barrier()


def wait(eng, sem, n):
    if not isinstance(n, int) or n > 0:
        eng.wait_ge(sem, n)


def wait_apart(eng, sem, n, passed):
    wait(eng, sem, n)
    if not isinstance(n, int):
        eng.sem_inc(passed, 1)


def three_pass(pe, out, left, right, first=True, last=True, k=P):
    (left_hi, left_lo), (right_hi, right_lo) = left, right
    pe.matmul(out, left_lo, right_hi, start=first, stop=False)
    pe.matmul(out, left_hi, right_lo, start=False, stop=False)
    return pe.matmul(out, left_hi, right_hi, start=False, stop=last)


def weight_sources(t):
    def rows(w):
        return w.rearrange("(c p) n -> p c n", p=P)

    return [rows(w) for w in (t["L0_xattn_Wkv"][:, 0:D], t["L0_xattn_Wkv"][:, D:2 * D], t["L1_xattn_Wq"],
                              t["L0_xattn_Wq"], t["L0_xattn_Wo"], t["L0_ffn_Wg"])]


def prepare(nc, hold, t, consts, keep, staging):
    with ExitStack() as ctx:
        mem = Memory(nc, ctx, "prepare_")
        raw, raw_loaded = staging
        wk, wv, w1, w1t = [[mem.sbuf(f"{n}_{h}", [P, CHUNKS, D], F32R) for h in ("hi", "lo")]
                           for n in ("wk", "wv", "w1", "w1t")]
        bk_row = mem.sbuf("bk_row", [P, D])
        bv_row = mem.sbuf("bv_row", [P, D])
        b1_row = mem.sbuf("b1_row", [P, D])
        context = mem.sbuf("context", [P, D])
        context_t = [mem.sbuf(f"context_t_{h}", [P, CHUNKS, KEYS], F32R) for h in ("hi", "lo")]
        k0 = mem.sbuf("k0", [P, D])
        v0 = mem.sbuf("v0", [P, D])
        k1 = mem.sbuf("k1", [P, D])
        v1 = mem.sbuf("v1", [P, 2, D], F32R)
        k0_t = mem.sbuf("k0_t", [P, 2, CHUNKS, KEYS], F32R)
        k1_t = mem.sbuf("k1_t", [P, 2, CHUNKS, KEYS], F32R)
        fold = mem.sbuf("fold", [P, D])
        fold_t = mem.sbuf("fold_t", [P, 2, CHUNKS, KEYS], F32R)
        fold_bias = mem.sbuf("fold_bias", [P, 1])
        product = mem.sbuf("product", [P, D])
        x = mem.sbuf("x", [P, TILES, D])
        stats, moments = mem.sbuf("stats", [P, TILES, 6]), mem.sbuf("moments", [P, TILES, 2])
        spread, minus_mean, istd, half = [mem.sbuf(n, [P, TILES]) for n in ("spread", "minus_mean", "istd", "half")]

        k1_bank, k0_bank, v0_bank, fold_bank = [mem.psum(n, [P, D]) for n in (
            "k1_bank", "k0_bank", "v0_bank", "fold_bank")]
        fold_t_bank, k1_t_bank, context_t_bank, k0_t_bank = [mem.psum(n, [P, CHUNKS, P]) for n in (
            "fold_t_bank", "k1_t_bank", "context_t_bank", "k0_t_bank")]

        sum_banks = (k1_bank, k0_bank, v0_bank, fold_bank)
        rows_loaded = mem.sem("rows_loaded")
        x_loaded, stats_made, moments_made, filled = [mem.sem(n) for n in (
            "x_loaded", "stats_made", "moments_made", "filled")]
        spread_made, mean_turned, istd_made, scales_made = [mem.sem(n) for n in (
            "spread_made", "mean_turned", "istd_made", "scales_made")]
        passed = consts["passed"]
        weight_hi, weight_lo = mem.sem("weight_hi"), mem.sem("weight_lo")
        w1_turned, w1t_hi, w1t_lo = mem.sem("w1_turned"), mem.sem("w1t_hi"), mem.sem("w1t_lo")
        context_loaded, context_turned = mem.sem("context_loaded"), mem.sem("context_turned")
        context_hi, context_lo = mem.sem("context_hi"), mem.sem("context_lo")
        k1_summed, k1_ready, k1_turned = mem.sem("k1_summed"), mem.sem("k1_ready"), mem.sem("k1_turned")
        k1_hi, k1_lo, v1_hi, v1_lo = [mem.sem(n) for n in ("k1_hi", "k1_lo", "v1_hi", "v1_lo")]
        k0_summed, k0_ready, k0_turned = mem.sem("k0_summed"), mem.sem("k0_ready"), mem.sem("k0_turned")
        k0_hi, k0_lo = mem.sem("k0_hi"), mem.sem("k0_lo")
        v0_summed, v0_ready = mem.sem("v0_summed"), mem.sem("v0_ready")
        fold_summed, fold_ready, fold_turned = [mem.sem(n) for n in ("fold_summed", "fold_ready", "fold_turned")]
        fold_hi, fold_lo, bias_ready = mem.sem("fold_hi"), mem.sem("fold_lo"), mem.sem("bias_ready")
        k0_stored, v0_stored, v1_stored, fold_stored, bias_stored = [mem.sem(n) for n in (
            "k0_stored", "v0_stored", "v1_stored", "fold_stored", "bias_stored")]

        STAGED = len(raw)
        weights = list(zip(weight_sources(t), (wk, wv, w1, hold["wq"], hold["wo"], hold["wg"])))
        W1 = 2

        ctx.callback(mem.clear_semaphores)
        block = ctx.enter_context(nc.Block())

        @block.sync
        def _(sp):
            sp.dma_start(context[0:KEYS, :], t["ctx_1024"][0]).then_inc(context_loaded, 16)
            for row, src in ((bk_row, t["L0_xattn_bkv"][0:D]), (bv_row, t["L0_xattn_bkv"][D:2 * D]),
                             (b1_row, t["L1_xattn_bq"])):
                sp.dma_start(row[:], src.partition_broadcast(P)).then_inc(rows_loaded, 16)
            for n, (src, _) in enumerate(weights):
                if n < STAGED:
                    continue
                sp.wait_ge(weight_lo, n - STAGED + 1)
                if n == STAGED + W1:
                    sp.wait_ge(w1_turned, CHUNKS)
                sp.dma_start(raw[n % STAGED][:], src).then_inc(raw_loaded[n % STAGED], 16)

            def stores(b, last):
                if not last:
                    sp.wait_ge(context_turned, b + 1)
                    sp.dma_start(context[0:KEYS, :], t["ctx_1024"][b + 1]).then_inc(context_loaded, 16)
                wait_apart(sp, stats_made, TILES * b, passed)
                sp.dma_start(x[:], t["x"][b].rearrange("(i p) d -> p i d", p=P)).then_inc(x_loaded, 16)
                sp.wait_ge(v1_lo, b + 1)
                sp.dma_start(t["v1_pairs"][b], v1[0:KEYS].bitcast(F32)).then_inc(v1_stored, 16)
                sp.wait_ge(bias_ready, b + 1)
                sp.dma_start(t["fold_biases"][b], fold_bias[0:KEYS]).then_inc(bias_stored, 16)
                sp.wait_ge(v0_ready, b + 1)
                sp.dma_start(t["v0_rows"][b], v0[0:KEYS]).then_inc(v0_stored, 16)
                sp.wait_ge(k0_lo, b + 1)
                for g in range(GROUP):
                    sp.dma_start(t["k0_pairs"][b, :, :, :, g, :], k0_t[HEAD * g:HEAD * (g + 1)].bitcast(F32)
                                 ).then_inc(k0_stored, 16)
                sp.wait_ge(fold_lo, b + 1)
                sp.dma_start(t["fold_pairs"][b], fold_t[:].bitcast(F32)).then_inc(fold_stored, 16)

            stores(0, False)
            with sp.Fori(1, BATCHES - 1) as b:
                stores(b, False)
            stores(BATCHES - 1, True)
            sp.wait_ge(k0_stored, 16 * GROUP * BATCHES)
            for s in (v0_stored, v1_stored, fold_stored, bias_stored):
                sp.wait_ge(s, 16 * BATCHES)

        @block.tensor
        def _(pe):
            def turn(bank, source, done):
                for c in range(CHUNKS):
                    last = pe.transpose(bank[:, c, 0:KEYS], source[0:KEYS, c * P:(c + 1) * P],
                                        consts["ident"][0:KEYS, 0:KEYS])
                last.then_inc(done, 1)

            def project(bank, left, right, done):
                for c in range(CHUNKS):
                    last = three_pass(pe, bank[0:KEYS, :], [x[:, c, :] for x in left],
                                      [x[:, c, :] for x in right], c == 0, c == CHUNKS - 1)
                last.then_inc(done, 1)

            def turn_context(b):
                pe.wait_ge(context_loaded, 16 * (b + 1))
                turn(context_t_bank, context, context_turned)

            pe.wait_ge(consts["ready"], consts["made"])
            pe.wait_ge(raw_loaded[W1], 16)
            for j, bank in enumerate(sum_banks):
                for c in range(CHUNKS):
                    last = pe.transpose(bank[:, c * P:(c + 1) * P], raw[W1][:, c, j * P:(j + 1) * P],
                                        consts["ident"][:])
                last.then_inc(w1_turned, 1)
            turn_context(0)
            pe.wait_ge(weight_lo, W1 + 1)
            pe.wait_ge(w1t_lo, CHUNKS)

            def batch(b, last):
                pe.wait_ge(context_lo, b + 1)
                wait(pe, k1_ready, b)
                project(k1_bank, context_t, w1, k1_summed)
                wait(pe, k0_ready, b)
                project(k0_bank, context_t, wk, k0_summed)
                pe.wait_ge(k1_ready, b + 1)
                wait(pe, k1_lo, b)
                turn(k1_t_bank, k1, k1_turned)
                wait(pe, v0_ready, b)
                project(v0_bank, context_t, wv, v0_summed)
                if not last:
                    turn_context(b + 1)
                pe.wait_ge(k1_lo, b + 1)
                wait(pe, fold_ready, b)
                project(fold_bank, [k1_t[:, h] for h in range(2)], w1t, fold_summed)
                pe.wait_ge(k0_ready, b + 1)
                wait(pe, k0_lo, b)
                turn(k0_t_bank, k0, k0_turned)
                pe.wait_ge(fold_ready, b + 1)
                wait(pe, fold_lo, b)
                turn(fold_t_bank, fold, fold_turned)

            batch(0, False)
            with pe.Fori(1, BATCHES - 1) as b:
                batch(b, False)
            batch(BATCHES - 1, True)

        @block.gpsimd
        def _(pool):
            pool.memset(half[:], -0.5).then_inc(filled, 1)
            pool.wait_ge(filled, 1)

            def batch(b):
                wait_apart(pool, moments_made, TILES * (b + 1), passed)
                pool.tensor_scalar(spread[:], moments[:, :, 1], EPS, None, ALU.add).then_inc(spread_made, 1)
                wait_apart(pool, scales_made, 2 * b, passed)
                pool.tensor_scalar(minus_mean[:], moments[:, :, 0], -1.0, None, ALU.mult).then_inc(mean_turned, 1)
                pool.wait_ge(spread_made, b + 1)
                pool.tensor_tensor(istd[:], spread[:], half[:], ALU.pow).then_inc(istd_made, 1)
                wait_apart(pool, mean_turned, b + 1, passed)
                wait_apart(pool, istd_made, b + 1, passed)
                at = bass.ds(TILES * b, TILES)
                pool.tensor_copy(keep["x_scales"][:, at, 0], istd[:]).then_inc(scales_made, 1)
                pool.tensor_tensor(keep["x_scales"][:, at, 1], minus_mean[:], istd[:], ALU.mult).then_inc(scales_made, 1)

            batch(0)
            with pool.Fori(1, BATCHES) as b:
                batch(b)
            pool.wait_ge(scales_made, 2 * BATCHES)

        @block.scalar
        def _(act):
            def high(out, bank, turned, n, done):
                act.wait_ge(turned, n)
                act.activation(out, bank, ACT.Copy).then_inc(done, 1)

            for n, (_, (hi, _)) in enumerate(weights):
                act.wait_ge(raw_loaded[n % STAGED], 16 * (n // STAGED + 1))
                act.activation(hi[:], raw[n % STAGED][:], ACT.Copy).then_inc(weight_hi, 1)
                if n == W1:
                    for j, bank in enumerate(sum_banks):
                        high(w1t[0][:, j, :], bank[:], w1_turned, j + 1, w1t_hi)
                    high(context_t[0][:], context_t_bank[:, :, 0:KEYS], context_turned, 1, context_hi)

            def batch(b, last):
                act.wait_ge(k1_ready, b + 1)
                wait(act, v1_stored, 16 * b)
                act.activation(v1[0:KEYS, 0], k1[0:KEYS, :], ACT.Copy).then_inc(v1_hi, 1)
                high(k1_t[:, 0], k1_t_bank[:, :, 0:KEYS], k1_turned, b + 1, k1_hi)
                if not last:
                    high(context_t[0][:], context_t_bank[:, :, 0:KEYS], context_turned, b + 2, context_hi)
                wait(act, fold_turned, b)
                act.wait_ge(fold_summed, b + 1)
                act.activation(fold[0:KEYS, :], fold_bank[0:KEYS, :], ACT.Copy).then_inc(fold_ready, 1)
                wait(act, k0_stored, 16 * GROUP * b)
                high(k0_t[:, 0], k0_t_bank[:, :, 0:KEYS], k0_turned, b + 1, k0_hi)
                wait(act, fold_stored, 16 * b)
                high(fold_t[:, 0], fold_t_bank[:, :, 0:KEYS], fold_turned, b + 1, fold_hi)

            batch(0, False)
            with act.Fori(1, BATCHES - 1) as b:
                batch(b, False)
            batch(BATCHES - 1, True)

        @block.vector
        def _(dve):
            def low(out, whole, hi, high_done, n, done):
                dve.wait_ge(high_done, n)
                dve.tensor_tensor(out, whole, hi.bitcast(F32), ALU.subtract).then_inc(done, 1)

            for n, (_, (hi, lo)) in enumerate(weights):
                low(lo[:], raw[n % STAGED][:], hi[:], weight_hi, n + 1, weight_lo)
                if n == W1:
                    for j, bank in enumerate(sum_banks):
                        low(w1t[1][:, j, :], bank[:], w1t[0][:, j, :], w1t_hi, j + 1, w1t_lo)
                    low(context_t[1][:], context_t_bank[:, :, 0:KEYS], context_t[0][:], context_hi, 1, context_lo)
            dve.wait_ge(rows_loaded, 16 * 3)

            def measure(i):
                dve.bn_stats(stats[:, i, :], x[:, i, :]).then_inc(stats_made, 1)

            def batch(b, last):
                wait(dve, k1_turned, b)
                wait(dve, v1_lo, b)
                dve.wait_ge(k1_summed, b + 1)
                dve.tensor_tensor(k1[0:KEYS], k1_bank[0:KEYS], b1_row[0:KEYS], ALU.add).then_inc(k1_ready, 1)
                wait(dve, k0_turned, b)
                dve.wait_ge(k0_summed, b + 1)
                dve.tensor_tensor(k0[0:KEYS], k0_bank[0:KEYS], bk_row[0:KEYS], ALU.add).then_inc(k0_ready, 1)
                dve.wait_ge(k1_ready, b + 1)
                wait(dve, bias_stored, 16 * b)
                dve.scalar_tensor_tensor(product[0:KEYS], k1[0:KEYS], D ** -0.5, b1_row[0:KEYS], ALU.mult,
                                         ALU.mult, accum_out=fold_bias[0:KEYS, :]).then_inc(bias_ready, 1)
                low(v1[0:KEYS, 1], k1[0:KEYS], v1[0:KEYS, 0], v1_hi, b + 1, v1_lo)
                low(k1_t[:, 1], k1_t_bank[:, :, 0:KEYS], k1_t[:, 0], k1_hi, b + 1, k1_lo)
                wait(dve, v0_stored, 16 * b)
                dve.wait_ge(v0_summed, b + 1)
                dve.tensor_tensor(v0[0:KEYS], v0_bank[0:KEYS], bv_row[0:KEYS], ALU.add).then_inc(v0_ready, 1)
                dve.wait_ge(x_loaded, 16 * (b + 1))
                measure(0)
                if not last:
                    low(context_t[1][:], context_t_bank[:, :, 0:KEYS], context_t[0][:], context_hi, b + 2,
                        context_lo)
                measure(1)
                low(k0_t[:, 1], k0_t_bank[:, :, 0:KEYS], k0_t[:, 0], k0_hi, b + 1, k0_lo)
                measure(2)
                measure(3)
                low(fold_t[:, 1], fold_t_bank[:, :, 0:KEYS], fold_t[:, 0], fold_hi, b + 1, fold_lo)
                wait_apart(dve, spread_made, b, passed)
                wait_apart(dve, mean_turned, b, passed)
                for i in range(TILES):
                    wait_apart(dve, stats_made, TILES * b + i + 1, passed)
                    dve.bn_aggr(moments[:, i, :], stats[:, i, :]).then_inc(moments_made, 1)

            batch(0, False)
            with dve.Fori(1, BATCHES - 1) as b:
                batch(b, False)
            batch(BATCHES - 1, True)


def constants(nc, mem, t):
    c = {"ident": mem.sbuf("ident", [P, P]), "ident_half": mem.sbuf("ident_half", [P, P], BF16),
         "before": mem.sbuf("before", [P, P], BF16), "ones": mem.sbuf("ones", [P, P], BF16),
         "numbers": mem.sbuf("numbers", [P, EXPERTS]), "own": mem.sbuf("own", [P, EXPERTS]),
         "tokens": mem.sbuf("tokens", [P, BATCHES * TILES], I32), "gates": mem.sbuf("gates", [P, 4])}
    c["ready"], filled, c["made"] = mem.sem("constants_ready"), mem.sem("constants_filled"), 7
    gates_loaded = mem.sem("gates_loaded")
    c["passed"] = mem.sem("passed")
    count = mem.sbuf("count", [P, EXPERTS], I32)
    count_own = mem.sbuf("count_own", [P, EXPERTS], I32)
    with nc.Block() as block:
        @block.gpsimd
        def _(pool):
            pool.memset(c["ident"][:], 0.0).then_inc(filled, 1)
            pool.memset(c["ident_half"][:], 0.0).then_inc(filled, 1)
            pool.memset(c["ones"][:], 1.0).then_inc(filled, 1)
            pool.iota(count[:], [[1, EXPERTS]], base=0, channel_multiplier=0).then_inc(filled, 1)
            pool.iota(count_own[:], [[REGION, EXPERTS]], base=0, channel_multiplier=1).then_inc(filled, 1)
            pool.iota(c["tokens"][:], [[P, BATCHES * TILES]], base=RESULTS_AT, channel_multiplier=1).then_inc(c["ready"], 1)
            pool.wait_ge(filled, 5)
            pool.tensor_copy(c["numbers"][:], count[:]).then_inc(c["ready"], 1)
            pool.tensor_copy(c["own"][:], count_own[:]).then_inc(c["ready"], 1)
            for out, source, keep, fill in ((c["ident"], c["ident"], ALU.not_equal, 1.0),
                                            (c["ident_half"], c["ident_half"], ALU.not_equal, 1.0),
                                            (c["before"], c["ones"], ALU.is_gt, 0.0)):
                pool.affine_select(out=out[:], in_=source[:], compare_op=keep, fill=fill, base=0,
                                   pattern=[[1, P]], channel_multiplier=-1).then_inc(c["ready"], 1)

        @block.sync
        def _(sp):
            sp.dma_start(c["gates"][:, 0:2], t["g_xattn"].partition_broadcast(P)).then_inc(gates_loaded, 16)
            sp.dma_start(c["gates"][:, 2:4], t["g_ffn"].partition_broadcast(P)).then_inc(gates_loaded, 16)

        @block.scalar
        def _(act):
            act.wait_ge(gates_loaded, 32)
            act.activation(c["gates"][:], c["gates"][:], ACT.Tanh).then_inc(c["ready"], 1)
            act.wait_ge(c["ready"], c["made"])
    return c


def scratch(nc):
    def table(name, shape, dtype=F32):
        return nc.dram_tensor(name, shape, dtype).ap()

    return {"k0_pairs": table("k0_pairs", [BATCHES, HEAD, 2, GROUPS, GROUP, KEYS]),
            "fold_pairs": table("fold_pairs", [BATCHES, P, 2, CHUNKS, KEYS]),
            "v0_rows": table("v0_rows", [BATCHES, KEYS, D]),
            "v1_pairs": table("v1_pairs", [BATCHES, KEYS, 2, D]),
            "fold_biases": table("fold_biases", [BATCHES, KEYS, 1]),
            "routed": table("routed", [(EXPERTS * REGION + EXPERTS * P), ROW]),
            "results": table("results", [RESULTS_AT + BATCHES * SEQ, RESULT])}


class Uses:

    def __init__(self, start, names):
        self.start, self.index = start, {name: k for k, name in enumerate(names)}

    def __getitem__(self, name):
        k = self.index[name]
        return self.start + k, k % 2


def attend_and_route(nc, hold, t, consts, keep):
    with ExitStack() as ctx:
        mem = Memory(nc, ctx, "attend_")
        wq, wo, wg = hold["wq"], hold["wo"], hold["wg"]
        bq_cols, bo_row, bg_row = mem.sbuf("bq_cols", [P, CHUNKS]), mem.sbuf("bo_row", [P, D]), mem.sbuf("bg_row", [P, D])
        x = mem.sbuf("x", [P, 2, TILES, D])
        scales = mem.sbuf("scales", [P, TILES, 2])
        half = mem.sbuf("half", [P, TILES])
        xn = mem.sbuf("xn", [P, TILES, D])
        x_t = [mem.sbuf(f"x_t_{h}", [P, CHUNKS, SEQ], F32R) for h in ("hi", "lo")]
        q = [mem.sbuf(f"q_{h}", [P, 2, SEQ], F32R) for h in ("hi", "lo")]
        q_stack = mem.sbuf("q_stack", [P, 2, GROUP, SEQ], F32R)
        k_stack = mem.sbuf("k_stack", [P, GROUPS, GROUP, KEYS], F32R)
        peak, shift, total, share = [mem.sbuf(n, [P, 2, GROUP]) for n in ("peak", "shift", "total", "share")]
        weights = mem.sbuf("weights", [P, 2, GROUP, SEQ])
        v = mem.sbuf("v", [P, D])
        v_shared = mem.sbuf("v_shared", [P, 2, GROUP, HEAD])
        out_t = [mem.sbuf(f"out_t_{h}", [P, GROUPS, SEQ], F32R) for h in ("hi", "lo")]
        x1 = mem.sbuf("x1", [P, 2, TILES, ROW])
        stats1, moments1 = mem.sbuf("stats1", [P, TILES, 6]), mem.sbuf("moments1", [P, TILES, 2])
        spread1, minus_mean1 = mem.sbuf("spread1", [P, TILES]), mem.sbuf("minus_mean1", [P, TILES])
        xn1 = mem.sbuf("xn1", [P, TILES, D])
        x1_t = [mem.sbuf(f"x1_t_{h}", [P, 2, CHUNKS, P], F32R) for h in ("hi", "lo")]
        logits = mem.sbuf("logits", [P, 2, D])
        best, minus_best = mem.sbuf("best", [P, TILES, 8]), mem.sbuf("minus_best", [P, TILES])
        best_at = mem.sbuf("best_at", [P, TILES, 8], U32)
        mass, chance = mem.sbuf("mass", [P, TILES]), mem.sbuf("chance", [P, TILES])
        expert_u, expert = mem.sbuf("expert_u", [P, TILES], U32), mem.sbuf("expert", [P, TILES])
        one_hot = mem.sbuf("one_hot", [P, TILES, EXPERTS], BF16)
        rank, rank_own = mem.sbuf("rank", [P, TILES, EXPERTS]), mem.sbuf("rank_own", [P, TILES, EXPERTS])
        rank_sum = mem.sbuf("rank_sum", [P, TILES])
        place = mem.sbuf("place", [P, TILES], U32)

        score = mem.psum("score", [P, GROUP, SEQ])
        sums = mem.psum("sums", [P, 2, D])
        turns = mem.psum("turns", [P, 2, CHUNKS, P])

        S = {n: mem.sem(n) for n in (
            "rows_loaded", "row_scaled", "x_loaded", "k_loaded", "v_loaded", "filled", "scales_kept", "xn_ready",
            "x_biased", "sum_ready", "sum_done", "turn_ready", "turn_done", "x_hi", "q_hi", "q_stacked0",
            "q_stacked1", "scored", "peaked", "shifted", "weighed", "inverted", "v_ready", "out_hi",
            "stats1_made", "moments1_made", "spread1_made", "mean1_turned", "istd1_made", "offset1_made",
            "xn1_ready", "x1_hi", "best_made", "best_turned", "best_found", "massed", "expert_read",
            "expert_made", "one_hot_made", "chance_made", "token_kept", "rank_picked", "rank_summed", "placed",
            "counted", "scattered")}
        q_stacked = (S["q_stacked0"], S["q_stacked1"])
        STACK = 16 * 3 * GROUP

        def uses_of_sums(b, route, attend, prefetch):
            names = [("query", 2), ("gate", 0), ("query", 3), ("gate", 1), ("gate", 2), ("gate", 3),
                     ("query", 0), ("query", 1), ("back", 0), ("back", 1), ("back", 2), ("back", 3)]
            there = {"gate": route, "back": attend}
            here = [n for n in names if there.get(n[0], prefetch if n[1] < 2 else attend)]
            FIRST, EACH = 2, len(names)
            if isinstance(b, int) and b == 0:
                return Uses(FIRST, here)
            return Uses(EACH * b + FIRST - TILES - (2 if isinstance(b, int) and b == BATCHES else 0), here)

        def uses_of_turns(b, route, attend, prefetch):
            names = [("routed", 0), ("routed", 1), ("weigh", 0), ("routed", 2), ("routed", 3), ("weigh", 1),
                     ("x", 0), ("x", 1), ("x", 2), ("x", 3), ("weigh", 2), ("weigh", 3),
                     ("ranks", 0), ("counts", 0)]
            there = {"routed": route, "ranks": route, "counts": route, "weigh": attend, "x": prefetch}
            here = [n for n in names if there[n[0]]]
            if isinstance(b, int) and b == 0:
                return Uses(TILES, here)
            return Uses(len(names) * b - 2 - (TILES if isinstance(b, int) and b == BATCHES else 0), here)

        FIRST_SUMS = Uses(0, [("query", 0), ("query", 1)])
        FIRST_TURNS = Uses(0, [("x", i) for i in range(TILES)])

        def iterations(eng, iteration):
            def at(b, odd, route=True, attend=True, prefetch=True):
                there = route, attend, prefetch
                iteration(b, odd, uses_of_sums(b, *there), uses_of_turns(b, *there), *there)

            FIRST = 3
            for b in range(FIRST):
                at(b, b % 2, route=b > 0)
            with eng.Fori(0, (BATCHES - 1 - FIRST) // 2) as pair:
                for k in range(2):
                    at(2 * pair + FIRST + k, (FIRST + k) % 2)
            at(BATCHES - 1, 1, prefetch=False)
            at(BATCHES, 0, attend=False, prefetch=False)

        passed = consts["passed"]
        ctx.callback(mem.clear_semaphores)
        block = ctx.enter_context(nc.Block())

        @block.sync
        def _(sp):
            def load_x(b, odd, start=0):
                wait(sp, S["sum_done"], start)
                sp.dma_start(x[:, odd], t["x"][b].rearrange("(t p) d -> p t d", p=P)).then_inc(S["x_loaded"], 16)

            def load_keys(b):
                wait(sp, S["scored"], HEADS * b)
                for block_of, part in enumerate((0, 0, 1)):
                    sp.dma_start(k_stack[HEAD * block_of:HEAD * (block_of + 1)].bitcast(F32),
                                 t["k0_pairs"][b, :, part]).then_inc(S["k_loaded"], 16)

            def load_values(b):
                wait(sp, S["v_ready"], GROUPS * b)
                sp.dma_start(v[0:KEYS], t["v0_rows"][b]).then_inc(S["v_loaded"], 16)

            def stack(b, m, uses):
                wait_apart(sp, S["scored"], HEADS * b + GROUP * (m - 1), passed)
                sp.wait_ge(S["sum_done"], uses["query", m][0] + 1)
                for g in range(GROUP):
                    for block_of, part in enumerate((0, 1, 0)):
                        sp.dma_start(q_stack[HEAD * block_of:HEAD * (block_of + 1), m % 2, g, :].bitcast(F32),
                                     q[part][HEAD * g:HEAD * (g + 1), m % 2, :].bitcast(F32)
                                     ).then_inc(q_stacked[m % 2], 16)

            load_x(0, 0)
            for to, source in ((bo_row, "L0_xattn_bo"), (bg_row, "L0_ffn_bg")):
                sp.dma_start(to[:], t[source].partition_broadcast(P)).then_inc(S["rows_loaded"], 16)
            sp.dma_start(bq_cols[:], t["L0_xattn_bq"].rearrange("(c p) -> p c", p=P),
                         allow_slow_non_contiguous=True).then_inc(S["rows_loaded"], 16)
            load_keys(0)
            load_values(0)
            for m in range(2):
                stack(0, m, FIRST_SUMS)

            def iteration(b, odd, s, r, route, attend, prefetch):
                if prefetch:
                    load_x(b + 1, 1 - odd, s.start)
                if attend:
                    stack(b, 2, s)
                    stack(b, 3, s)
                if prefetch:
                    load_keys(b + 1)
                    stack(b + 1, 0, s)
                    stack(b + 1, 1, s)
                    load_values(b + 1)

            iterations(sp, iteration)

        @block.tensor
        def _(pe):
            def turn(use, source):
                n, bank = use
                wait(pe, S["turn_done"], n - 1)
                for c in range(CHUNKS):
                    last = pe.transpose(turns[:, bank, c, :], source[:, c * P:(c + 1) * P], consts["ident"][:])
                last.then_inc(S["turn_ready"], 1)
                return n + 1

            def project(use, left, right):
                n, bank = use
                wait(pe, S["sum_done"], n - 1)
                for c in range(CHUNKS):
                    last = three_pass(pe, sums[:, bank, :], left(c), right(c), c == 0, c == CHUNKS - 1)
                last.then_inc(S["sum_ready"], 1)

            def turn_x(uses, b, i):
                pe.wait_ge(S["xn_ready"], TILES * b + i + 1)
                return turn(uses["x", i], xn[:, i])

            def turn_routed(uses, b, i):
                pe.wait_ge(S["xn1_ready"], TILES * b + i + 1)
                return turn(uses["routed", i], xn1[:, i])

            def gate(uses, i, turned):
                pe.wait_ge(S["turn_done"], turned)
                project(uses["gate", i], lambda c: [h[:, i % 2, c, :] for h in x1_t], lambda c: [h[:, c, :] for h in wg])

            def query(uses, m):
                project(uses["query", m], lambda c: [h[:, c, m * P:(m + 1) * P] for h in wq], lambda c: [h[:, c, :] for h in x_t])

            def scores(b, m):
                pe.wait_ge(q_stacked[m % 2], STACK * (2 * b + m // 2 + 1))
                pe.wait_ge(S["k_loaded"], 16 * 3 * (b + 1))
                for g in range(GROUP):
                    wait(pe, S["weighed"], HEADS * b + GROUP * (m - 1) + g + 1)
                    pe.matmul(score[0:KEYS, g, :], k_stack[0:3 * HEAD, m, g, :], q_stack[0:3 * HEAD, m % 2, g, :],
                              start=True, stop=True).then_inc(S["scored"], 1)

            def weigh(uses, b, m):
                n, bank = uses["weigh", m]
                wait(pe, S["turn_done"], n - 1)
                pe.wait_ge(S["v_ready"], GROUPS * b + m + 1)
                for g in range(GROUP):
                    last = pe.matmul(turns[HEAD * g:HEAD * (g + 1), bank].rearrange("p c n -> p (c n)"),
                                     v_shared[0:KEYS, m % 2, g, :], weights[0:KEYS, m % 2, g, :], start=True, stop=True,
                                     tile_position=(0, HEAD * g))
                last.then_inc(S["turn_ready"], 1)
                return n + 1

            def back(uses, i, turned):
                pe.wait_ge(S["turn_done"], turned)
                project(uses["back", i], lambda c: [h[:, c, i * P:(i + 1) * P] for h in out_t], lambda c: [h[:, c, :] for h in wo])

            def ranks(uses, b):
                n, bank = uses["ranks", 0]
                wait(pe, S["turn_done"], n - 1)
                pe.wait_ge(S["one_hot_made"], b + 1)
                out = turns[:, bank, 0, 0:TILES * EXPERTS].rearrange("p (i e) -> p i e", e=EXPERTS)
                last = pe.matmul(out, consts["before"][:], one_hot[:], start=True, stop=False)
                for i in range(TILES - 1):
                    rest = TILES - 1 - i
                    last = pe.matmul(out[:, i + 1:TILES, :], consts["ones"][:],
                                     one_hot[:, i:i + 1, :].broadcast_to([P, rest, EXPERTS]), start=False,
                                     stop=i == TILES - 2)
                last.then_inc(S["turn_ready"], 1)
                n, bank = uses["counts", 0]
                wait(pe, S["turn_done"], n - 1)
                for i in range(TILES):
                    last = pe.matmul(turns[:, bank, 0, 0:EXPERTS], consts["ones"][:], one_hot[:, i, :],
                                     start=i == 0, stop=i == TILES - 1)
                last.then_inc(S["turn_ready"], 1)

            for i in range(TILES):
                turned_x = turn_x(FIRST_TURNS, 0, i)
            pe.wait_ge(S["turn_done"], turned_x)
            for m in range(2):
                query(FIRST_SUMS, m)

            def iteration(b, odd, s, r, route, attend, prefetch):
                p, turned = b - 1, {}
                if route:
                    turned[0] = turn_routed(r, p, 0)
                if attend:
                    scores(b, 0)
                    query(s, 2)
                if route:
                    turned[1] = turn_routed(r, p, 1)
                    gate(s, 0, turned[0])
                if attend:
                    scores(b, 1)
                    weigh(r, b, 0)
                    query(s, 3)
                if route:
                    turned[2] = turn_routed(r, p, 2)
                    gate(s, 1, turned[1])
                    turned[3] = turn_routed(r, p, 3)
                if attend:
                    scores(b, 2)
                    weigh(r, b, 1)
                if prefetch:
                    turn_x(r, b + 1, 0)
                if route:
                    gate(s, 2, turned[2])
                if prefetch:
                    turn_x(r, b + 1, 1)
                    turn_x(r, b + 1, 2)
                if route:
                    gate(s, 3, turned[3])
                if prefetch:
                    turned_x = turn_x(r, b + 1, 3)
                if attend:
                    scores(b, 3)
                    weigh(r, b, 2)
                if prefetch:
                    pe.wait_ge(S["turn_done"], turned_x)
                    query(s, 0)
                    query(s, 1)
                if attend:
                    turned_out = weigh(r, b, 3)
                    back(s, 0, turned_out)
                if route:
                    ranks(r, p)
                if attend:
                    for i in range(1, TILES):
                        back(s, i, turned_out)

            iterations(pe, iteration)

        @block.scalar
        def _(act):
            def turned_hi(use, out, done):
                n, bank = use
                act.wait_ge(S["turn_ready"], n + 1)
                act.activation(out, turns[:, bank], ACT.Copy).then_inc(S[done], 1)

            def x_hi(uses, i):
                turned_hi(uses["x", i], x_t[0][:, :, i * P:(i + 1) * P], "x_hi")

            def routed_hi(uses, i):
                turned_hi(uses["routed", i], x1_t[0][:, i % 2], "x1_hi")

            def query_hi(uses, b, m):
                n, bank = uses["query", m]
                act.wait_ge(S["sum_ready"], n + 1)
                wait(act, q_stacked[m % 2], STACK * (2 * b + m // 2))
                act.activation(q[0][:, m % 2, :], sums[:, bank, :], ACT.Identity,
                               bias=bq_cols[:, m:m + 1]).then_inc(S["q_hi"], 1)

            def weights_of(b, m):
                act.wait_ge(S["shifted"], GROUPS * b + m + 1)
                for g in range(GROUP):
                    act.activation(weights[0:KEYS, m % 2, g, :], score[0:KEYS, g, :], ACT.Exp,
                                   bias=shift[0:KEYS, m % 2, g:g + 1], scale=HEAD ** -0.5,
                                   accum_out=total[0:KEYS, m % 2, g:g + 1]).then_inc(S["weighed"], 1)

            def out_hi(uses, m):
                n, bank = uses["weigh", m]
                act.wait_ge(S["turn_ready"], n + 1)
                act.activation(out_t[0][:, m, :], turns[:, bank].rearrange("p c n -> p (c n)"), ACT.Copy
                               ).then_inc(S["out_hi"], 1)

            def gate_mass(b, i):
                act.wait_ge(S["best_turned"], TILES * b + i + 1)
                act.wait_ge(S["best_found"], TILES * b + i + 1)
                act.activation(logits[:, i % 2, :], logits[:, i % 2, :], ACT.Exp, bias=minus_best[:, i:i + 1],
                               accum_out=mass[:, i:i + 1]).then_inc(S["massed"], 1)

            act.wait_ge(S["rows_loaded"], 16 * 3)
            for i in range(TILES):
                x_hi(FIRST_TURNS, i)
            for m in range(2):
                query_hi(FIRST_SUMS, 0, m)

            def iteration(b, odd, s, r, route, attend, prefetch):
                p = b - 1
                if route:
                    routed_hi(r, 0)
                if attend:
                    query_hi(s, b, 2)
                    weights_of(b, 0)
                if route:
                    routed_hi(r, 1)
                if attend:
                    out_hi(r, 0)
                    weights_of(b, 1)
                    query_hi(s, b, 3)
                if route:
                    routed_hi(r, 2)
                    routed_hi(r, 3)
                    gate_mass(p, 0)
                if attend:
                    out_hi(r, 1)
                if prefetch:
                    x_hi(r, 0)
                if attend:
                    weights_of(b, 2)
                if prefetch:
                    x_hi(r, 1)
                    x_hi(r, 2)
                if route:
                    gate_mass(p, 1)
                if prefetch:
                    x_hi(r, 3)
                if attend:
                    out_hi(r, 2)
                    weights_of(b, 3)
                if prefetch:
                    query_hi(s, b + 1, 0)
                    query_hi(s, b + 1, 1)
                if attend:
                    out_hi(r, 3)
                if route:
                    gate_mass(p, 2)
                    gate_mass(p, 3)

            iterations(act, iteration)

        @block.vector
        def _(dve):
            def turned_lo(use, hi, lo, hi_done, n_hi):
                _, bank = use
                dve.wait_ge(S[hi_done], n_hi)
                dve.tensor_tensor(lo, turns[:, bank], hi.bitcast(F32), ALU.subtract
                                  ).then_inc(S["turn_done"], 1)

            def x_lo(uses, b, i):
                hi, lo = [h[:, :, i * P:(i + 1) * P] for h in x_t]
                turned_lo(uses["x", i], hi, lo, "x_hi", TILES * b + i + 1)

            def routed_lo(uses, b, i):
                hi, lo = [h[:, i % 2] for h in x1_t]
                turned_lo(uses["routed", i], hi, lo, "x1_hi", TILES * b + i + 1)

            def query_lo(uses, b, m):
                n, bank = uses["query", m]
                dve.wait_ge(S["q_hi"], GROUPS * b + m + 1)
                dve.scalar_tensor_tensor(q[1][:, m % 2, :], sums[:, bank, :], bq_cols[:, m:m + 1],
                                         q[0][:, m % 2, :].bitcast(F32), ALU.add, ALU.subtract
                                         ).then_inc(S["sum_done"], 1)

            def out_lo(uses, b, m):
                n, bank = uses["weigh", m]
                dve.wait_ge(S["out_hi"], GROUPS * b + m + 1)
                dve.tensor_tensor(out_t[1][:, m, :], turns[:, bank].rearrange("p c n -> p (c n)"),
                                  out_t[0][:, m, :].bitcast(F32), ALU.subtract
                                  ).then_inc(S["turn_done"], 1)

            def peaks(b, m):
                n = GROUPS * b + m + 1
                dve.wait_ge(S["scored"], GROUP * n)
                dve.tensor_reduce(peak[0:KEYS, m % 2, :], score[0:KEYS], AX_X, ALU.max).then_inc(S["peaked"], 1)
                dve.wait_ge(S["peaked"], n)
                dve.tensor_scalar(shift[0:KEYS, m % 2, :], peak[0:KEYS, m % 2, :], -(HEAD ** -0.5), None, ALU.mult
                                  ).then_inc(S["shifted"], 1)

            def share_values(b, m):
                n = GROUPS * b + m + 1
                dve.wait_ge(S["weighed"], GROUP * n)
                dve.reciprocal(share[0:KEYS, m % 2, :], total[0:KEYS, m % 2, :]).then_inc(S["inverted"], 1)
                dve.wait_ge(S["v_loaded"], 16 * (b + 1))
                dve.wait_ge(S["inverted"], n)
                dve.tensor_tensor(v_shared[0:KEYS, m % 2], v[0:KEYS, m * P:(m + 1) * P].rearrange("p (g d) -> p g d", d=HEAD),
                                  share[0:KEYS, m % 2, :].unsqueeze(2).broadcast_to([KEYS, GROUP, HEAD]), ALU.mult
                                  ).then_inc(S["v_ready"], 1)

            def keep_scales(b):
                wait_apart(dve, S["xn_ready"], TILES * b, passed)
                dve.tensor_copy(scales[:], keep["x_scales"][:, bass.ds(TILES * b, TILES), :]).then_inc(S["scales_kept"], 1)

            def gate_logits(uses, b, i):
                n, bank = uses["gate", i]
                dve.wait_ge(S["sum_ready"], n + 1)
                wait(dve, S["massed"], TILES * b + max(i - 1, 0))
                dve.tensor_tensor(logits[:, i % 2, :], sums[:, bank, :], bg_row[:], ALU.add
                                  ).then_inc(S["sum_done"], 1)
                return n + 1

            def gate_best(b, i, logits_at):
                n = TILES * b + i + 1
                wait_apart(dve, S["sum_done"], logits_at, passed)
                dve.max(best[:, i, :], logits[:, i % 2, :]).then_inc(S["best_made"], 1)
                dve.wait_ge(S["best_made"], n)
                dve.tensor_scalar(minus_best[:, i:i + 1], best[:, i, 0:1], -1.0, None, ALU.mult
                                  ).then_inc(S["best_turned"], 1)
                dve.max_index(best_at[:, i, :], best[:, i, :], logits[:, i % 2, :]).then_inc(S["best_found"], 1)

            def choose(b):
                dve.wait_ge(S["best_found"], TILES * (b + 1))
                dve.tensor_scalar(expert_u[:], best_at[:, :, 0], EXPERTS - 1, None, ALU.bitwise_and
                                  ).then_inc(S["expert_read"], 1)
                dve.wait_ge(S["expert_read"], b + 1)
                dve.tensor_copy(expert[:], expert_u[:]).then_inc(S["expert_made"], 1)
                dve.wait_ge(S["expert_made"], b + 1)
                dve.tensor_tensor(one_hot[:], consts["numbers"][:].unsqueeze(1).broadcast_to([P, TILES, EXPERTS]),
                                  expert[:].unsqueeze(2).broadcast_to([P, TILES, EXPERTS]), ALU.is_equal
                                  ).then_inc(S["one_hot_made"], 1)

            def place_rows(uses, b):
                n, bank = uses["ranks", 0]
                dve.wait_ge(S["turn_ready"], n + 1)
                dve.wait_ge(S["turn_done"], uses.start)
                dve.tensor_tensor(rank[:], turns[:, bank, 0, 0:TILES * EXPERTS].rearrange("p (i e) -> p i e", e=EXPERTS),
                                  keep["counts"][:].unsqueeze(1).broadcast_to([P, TILES, EXPERTS]), ALU.add
                                  ).then_inc(S["turn_done"], 1)
                dve.wait_ge(S["turn_done"], n + 1)
                n, bank = uses["counts", 0]
                dve.wait_ge(S["turn_ready"], n + 1)
                dve.tensor_tensor(keep["counts"][:], keep["counts"][:], turns[:, bank, 0, 0:EXPERTS], ALU.add
                                  ).then_inc(S["turn_done"], 1)
                dve.tensor_tensor(rank_own[:], rank[:], one_hot[:], ALU.mult).then_inc(S["rank_picked"], 1)
                dve.wait_ge(S["rank_picked"], b + 1)
                dve.tensor_reduce(rank_sum[:], rank_own[:], AX_X, ALU.add).then_inc(S["rank_summed"], 1)
                dve.wait_ge(S["rank_summed"], b + 1)
                wait(dve, S["scattered"], 16 * TILES * b)
                dve.scalar_tensor_tensor(place[:], expert[:], float(REGION), rank_sum[:], ALU.mult, ALU.add
                                         ).then_inc(S["placed"], 1)

            def chances(b, odd):
                dve.wait_ge(S["massed"], TILES * (b + 1))
                dve.reciprocal(chance[:], mass[:]).then_inc(S["chance_made"], 1)
                dve.tensor_copy(x1[:, odd, :, D + 3].bitcast(I32), consts["tokens"][:, bass.ds(TILES * b, TILES)]
                                ).then_inc(S["token_kept"], 1)
                dve.wait_ge(S["chance_made"], 2 * b + 1)
                dve.tensor_scalar(x1[:, odd, :, D + 2], chance[:], consts["gates"][:, 2:3], None, ALU.mult
                                  ).then_inc(S["chance_made"], 1)

            def add_up(uses, b, odd, i):
                n, bank = uses["back", i]
                dve.wait_ge(S["sum_ready"], n + 1)
                if i == 0:
                    wait(dve, S["scattered"], 16 * TILES * (b - 1))
                dve.wait_ge(S["x_biased"], TILES * b + i + 1)
                dve.scalar_tensor_tensor(x1[:, odd, i, 0:D], sums[:, bank, :], consts["gates"][:, 0:1], x[:, odd, i, :],
                                         ALU.mult, ALU.add).then_inc(S["sum_done"], 1)
                if i == 0:
                    wait(dve, S["xn1_ready"], TILES * b)
                dve.wait_ge(S["sum_done"], n + 1)
                dve.bn_stats(stats1[:, i, :], x1[:, odd, i, 0:D]).then_inc(S["stats1_made"], 1)
                wait_apart(dve, S["stats1_made"], TILES * b + i + 1, passed)
                dve.bn_aggr(moments1[:, i, :], stats1[:, i, :]).then_inc(S["moments1_made"], 1)

            dve.memset(keep["counts"][:], 0.0).then_inc(S["counted"], 1)
            dve.wait_ge(S["counted"], 1)
            dve.wait_ge(S["rows_loaded"], 16 * 3)
            dve.tensor_scalar(bo_row[:], bo_row[:], consts["gates"][:, 0:1], None, ALU.mult).then_inc(S["row_scaled"], 1)
            keep_scales(0)
            for i in range(TILES):
                x_lo(FIRST_TURNS, 0, i)
            for m in range(2):
                query_lo(FIRST_SUMS, 0, m)

            def iteration(b, odd, s, r, route, attend, prefetch):
                p = b - 1
                if route:
                    routed_lo(r, p, 0)
                if prefetch:
                    keep_scales(b + 1)
                if attend:
                    peaks(b, 0)
                    query_lo(s, b, 2)
                    share_values(b, 0)
                if route:
                    routed_lo(r, p, 1)
                if route:
                    logits_at = gate_logits(s, p, 0)
                if attend:
                    peaks(b, 1)
                    out_lo(r, b, 0)
                if attend:
                    share_values(b, 1)
                    query_lo(s, b, 3)
                if route:
                    routed_lo(r, p, 2)
                    next_at = gate_logits(s, p, 1)
                    routed_lo(r, p, 3)
                    gate_best(p, 0, logits_at)
                if attend:
                    peaks(b, 2)
                    out_lo(r, b, 1)
                if prefetch:
                    x_lo(r, b + 1, 0)
                if route:
                    gate_best(p, 1, next_at)
                    logits_at = gate_logits(s, p, 2)
                if prefetch:
                    x_lo(r, b + 1, 1)
                    x_lo(r, b + 1, 2)
                if attend:
                    share_values(b, 2)
                if prefetch:
                    x_lo(r, b + 1, 3)
                if attend:
                    peaks(b, 3)
                if route:
                    next_at = gate_logits(s, p, 3)
                if attend:
                    out_lo(r, b, 2)
                if route:
                    gate_best(p, 2, logits_at)
                if attend:
                    share_values(b, 3)
                if prefetch:
                    query_lo(s, b + 1, 0)
                    query_lo(s, b + 1, 1)
                if attend:
                    out_lo(r, b, 3)
                if route:
                    gate_best(p, 3, next_at)
                    choose(p)
                if attend:
                    add_up(s, b, odd, 0)
                if route:
                    place_rows(r, p)
                    chances(p, 1 - odd)
                if attend:
                    for i in range(1, TILES):
                        add_up(s, b, odd, i)

            iterations(dve, iteration)

        @block.gpsimd
        def _(pool):
            pool.memset(half[:], -0.5).then_inc(S["filled"], 1)
            pool.wait_ge(S["filled"], 1)

            def normalize(b, odd):
                wait_apart(pool, S["x_loaded"], 16 * (b + 1), passed)
                wait_apart(pool, S["scales_kept"], b + 1, passed)
                wait_apart(pool, S["x_hi"], TILES * b, passed)
                for i in range(TILES):
                    pool.tensor_scalar(xn[:, i, :], x[:, odd, i, :], scales[:, i, 0:1], scales[:, i, 1:2],
                                       ALU.mult, ALU.add).then_inc(S["xn_ready"], 1)
                pool.wait_ge(S["row_scaled"], 1)

            def add_bias(b, odd):
                for i in range(TILES):
                    pool.wait_ge(S["xn_ready"], TILES * b + i + 1)
                    pool.tensor_tensor(x[:, odd, i, :], x[:, odd, i, :], bo_row[:], ALU.add
                                       ).then_inc(S["x_biased"], 1)

            def normalize_routed(b, odd, i):
                n = TILES * b + i + 1
                wait_apart(pool, S["moments1_made"], n, passed)
                pool.tensor_scalar(spread1[:, i:i + 1], moments1[:, i, 1:2], EPS, None, ALU.add).then_inc(S["spread1_made"], 1)
                pool.tensor_scalar(minus_mean1[:, i:i + 1], moments1[:, i, 0:1], -1.0, None, ALU.mult).then_inc(S["mean1_turned"], 1)
                pool.wait_ge(S["spread1_made"], n)
                pool.tensor_tensor(x1[:, odd, i, D:D + 1], spread1[:, i:i + 1], half[:, 0:1], ALU.pow).then_inc(S["istd1_made"], 1)
                pool.wait_ge(S["mean1_turned"], n)
                pool.wait_ge(S["istd1_made"], n)
                pool.tensor_tensor(x1[:, odd, i, D + 1:D + 2], minus_mean1[:, i:i + 1], x1[:, odd, i, D:D + 1], ALU.mult
                                   ).then_inc(S["offset1_made"], 1)
                wait_apart(pool, S["offset1_made"], n, passed)
                pool.tensor_scalar(xn1[:, i, :], x1[:, odd, i, 0:D], x1[:, odd, i, D:D + 1], x1[:, odd, i, D + 1:D + 2],
                                   ALU.mult, ALU.add).then_inc(S["xn1_ready"], 1)

            def scatter(b, odd):
                pool.wait_ge(S["placed"], b + 1)
                wait_apart(pool, S["chance_made"], 2 * (b + 1), passed)
                wait_apart(pool, S["token_kept"], b + 1, passed)
                for i in range(TILES):
                    pool.indirect_dma_start(t["routed"], bass.IndirectOffsetOnAxis(ap=place[:, i:i + 1], axis=0),
                                            x1[:, odd, i, :], None).then_inc(S["scattered"], 16)

            normalize(0, 0)
            add_bias(0, 0)

            def iteration(b, odd, s, r, route, attend, prefetch):
                if prefetch:
                    normalize(b + 1, 1 - odd)
                    add_bias(b + 1, 1 - odd)
                if attend:
                    for i in range(TILES):
                        normalize_routed(b, odd, i)
                if route:
                    scatter(b - 1, 1 - odd)

            iterations(pool, iteration)
            pool.wait_ge(S["scattered"], 16 * TILES * BATCHES)


def run_experts(nc, t, consts, keep):
    with ExitStack() as ctx:
        mem = Memory(nc, ctx, "experts_")
        AHEAD, BUFFERS = 7, 8
        padded, padded_tiles = mem.sbuf("padded", [P, EXPERTS], I32), mem.sbuf("padded_tiles", [P, EXPERTS], I32)
        tiles, ends, stride = [mem.sbuf(n, [P, EXPERTS]) for n in ("tiles", "ends", "stride")]
        slot_i, slot = mem.sbuf("slot_i", [P, SLOTS], I32), mem.sbuf("slot", [P, SLOTS])
        past = mem.sbuf("past", [P, SLOTS, EXPERTS])
        expert, row = mem.sbuf("expert", [P, SLOTS]), mem.sbuf("row", [P, SLOTS])
        expert_of, row_of = mem.sbuf("expert_of", [P, SLOTS], I32), mem.sbuf("row_of", [P, SLOTS], I32)
        pad_at, pads = mem.sbuf("pad_at", [P, EXPERTS], U32), mem.sbuf("pads", [P, ROW])
        pad_row, to = mem.sbuf("pad_row", [P, SLOTS], I32), mem.sbuf("to", [P, BUFFERS], U32)

        raw = [mem.sbuf(f"raw{i}", [P, CHUNKS, D]) for i in range(2)]
        raw_loaded = [mem.sem(f"raw_loaded{i}") for i in range(2)]
        w = [mem.sbuf(f"w_{h}", [P, EXPERTS, CHUNKS, D], F32R) for h in ("hi", "lo")]
        be_rows = mem.sbuf("be_rows", [P, EXPERTS, D])
        x = [mem.sbuf(f"x{i}", [P, ROW]) for i in range(BUFFERS)]
        xn = [mem.sbuf(f"xn{i}", [P, D]) for i in range(2)]
        x_t = [[mem.sbuf(f"x_t{i}_{h}", [P, CHUNKS, P], F32R) for h in ("hi", "lo")] for i in range(2)]
        inner = [mem.sbuf(f"inner{i}", [P, D]) for i in range(2)]
        stats, moments = mem.sbuf("stats", [P, 6]), mem.sbuf("moments", [P, 2])
        spread, minus_mean, half = [mem.sbuf(n, [P, 1]) for n in ("spread", "minus_mean", "half")]
        turns, sums = mem.psum("turns", [P, 2, CHUNKS, P]), mem.psum("sums", [P, 2, D])

        planned, slots_made, zeros_made, pads_placed, pads_written = [mem.sem(n) for n in (
            "planned", "slots_made", "zeros_made", "pads_placed", "pads_written")]
        rows_loaded, weight_hi, weight_lo = mem.sem("rows_loaded"), mem.sem("weight_hi"), mem.sem("weight_lo")
        loaded = [mem.sem(f"loaded{i}") for i in range(BUFFERS)]
        stored = [mem.sem(f"stored{i}") for i in range(BUFFERS)]
        normalized, turned, turned_hi, turned_lo = [mem.sem(n) for n in (
            "normalized", "turned", "turned_hi", "turned_lo")]
        summed, biased, clipped, mixed = [mem.sem(n) for n in ("summed", "biased", "clipped", "mixed")]
        stats_made, measured, spread_made, mean_turned, istd_made, offset_made, to_made = [mem.sem(n) for n in (
            "stats_made", "measured", "spread_made", "mean_turned", "istd_made", "offset_made", "to_made")]
        PLAN = 12

        passed = consts["passed"]
        ctx.callback(mem.clear_semaphores)
        block = ctx.enter_context(nc.Block())

        def expert_weights(e):
            return t["L0_ffn_We"][e].rearrange("(c p) n -> p c n", p=P)

        def tiles_in_turn(eng, tile):
            rounds = SLOTS // BUFFERS
            for k in range(BUFFERS):
                tile(0, k, BUFFERS)
            with eng.Fori(1, rounds - 1) as i:
                for k in range(BUFFERS):
                    tile(i, k, BUFFERS)
            for k in range(BUFFERS):
                tile(rounds - 1, k, BUFFERS - 1 - k)

        @block.gpsimd
        def _(pool):
            pool.iota(slot_i[:], [[1, SLOTS]], base=0, channel_multiplier=0).then_inc(slots_made, 1)
            pool.iota(pad_row[:], [[P, SLOTS]], base=0, channel_multiplier=1).then_inc(zeros_made, 1)
            pool.memset(pads[:], 0.0).then_inc(zeros_made, 1)
            pool.memset(half[:], -0.5).then_inc(zeros_made, 1)
            pool.wait_ge(zeros_made, 3)
            for e in range(EXPERTS):
                pool.dma_start(t["routed"][EXPERTS * REGION + e * P:EXPERTS * REGION + (e + 1) * P, :], pads[:]
                               ).then_inc(pads_written, 16)
            pool.wait_ge(pads_placed, 1)
            for e in range(EXPERTS):
                pool.indirect_dma_start(t["routed"], bass.IndirectOffsetOnAxis(ap=pad_at[:, e:e + 1], axis=0),
                                        pads[:], None).then_inc(pads_written, 16)

            def tile(i, k, left):
                n = i * BUFFERS + k
                wait_apart(pool, measured, n + 1, passed)
                pool.tensor_scalar(spread[:], moments[:, 1:2], EPS, None, ALU.add).then_inc(spread_made, 1)
                pool.tensor_scalar(minus_mean[:], moments[:, 0:1], -1.0, None, ALU.mult).then_inc(mean_turned, 1)
                pool.wait_ge(spread_made, n + 1)
                pool.tensor_tensor(x[k][:, D:D + 1], spread[:], half[:], ALU.pow).then_inc(istd_made, 1)
                pool.wait_ge(mean_turned, n + 1)
                pool.wait_ge(istd_made, n + 1)
                pool.tensor_tensor(x[k][:, D + 1:D + 2], minus_mean[:], x[k][:, D:D + 1], ALU.mult).then_inc(offset_made, 1)
                pool.wait_ge(to_made, n + 1)
                wait_apart(pool, offset_made, n + 1, passed)
                pool.indirect_dma_start(t["results"], bass.IndirectOffsetOnAxis(
                    ap=to[:, k:k + 1], axis=0), x[k][:, 0:RESULT], None).then_inc(stored[k], 16)

            tiles_in_turn(pool, tile)
            for k in range(BUFFERS):
                pool.wait_ge(stored[k], 16 * SLOTS // BUFFERS)

        @block.sync
        def _(sp):
            def place_of(n):
                at = sp.value_load(row_of[0:1, bass.ds(n, 1)], min_val=0, max_val=EXPERTS * (REGION + P) - P)
                return t["routed"][bass.ds(at, P), :]

            def load(n, k):
                sp.dma_start(x[k][:], place_of(n)).then_inc(loaded[k], 16)

            def tile(i, k, left):
                if left >= AHEAD:
                    wait_apart(sp, stored[k - 1], 16 * (i + (k > 0)), passed)
                    load(i * BUFFERS + k + AHEAD, (k + AHEAD) % BUFFERS)

            for e in range(2):
                sp.dma_start(raw[e][:], expert_weights(e)).then_inc(raw_loaded[e], 16)
            for e in range(2, EXPERTS):
                sp.wait_ge(weight_lo, e - 1)
                sp.dma_start(raw[e % 2][:], expert_weights(e)).then_inc(raw_loaded[e % 2], 16)
            for e in range(EXPERTS):
                sp.dma_start(be_rows[:, e, :], t["L0_ffn_be"][e].partition_broadcast(P)).then_inc(rows_loaded, 16)
            sp.wait_ge(planned, PLAN)
            sp.wait_ge(pads_written, 16 * 2 * EXPERTS)
            for n in range(AHEAD):
                load(n, n)
            tiles_in_turn(sp, tile)

        @block.vector
        def _(dve):
            def step(ins, n):
                ins.then_inc(planned, 1)
                dve.wait_ge(planned, n)

            def wide(small):
                return small.unsqueeze(1).broadcast_to([P, SLOTS, EXPERTS])

            counts = keep["counts"]
            dve.tensor_tensor(pad_at[:], consts["own"][:], counts[:], ALU.add).then_inc(pads_placed, 1)
            step(dve.tensor_scalar(padded[:], counts[:], float(P - 1), None, ALU.add), 1)
            step(dve.tensor_scalar(padded_tiles[:], padded[:], P.bit_length() - 1, None, ALU.arith_shift_right), 2)
            step(dve.tensor_copy(tiles[:], padded_tiles[:]), 3)
            dve.tensor_scalar(stride[:], tiles[:], -float(P), float(REGION), ALU.mult, ALU.add).then_inc(planned, 1)
            dve.wait_ge(planned, 4)
            step(dve.tensor_tensor_scan(ends[:], tiles[:], tiles[:], 0.0, ALU.add, ALU.bypass), 5)
            dve.wait_ge(slots_made, 1)
            step(dve.tensor_copy(slot[:], slot_i[:]), 6)
            step(dve.tensor_tensor(past[:], slot[:].unsqueeze(2).broadcast_to([P, SLOTS, EXPERTS]), wide(ends[:]),
                                   ALU.is_ge), 7)
            step(dve.tensor_reduce(expert[:], past[:], AX_X, ALU.add), 8)
            step(dve.tensor_tensor(past[:], past[:], wide(stride[:]), ALU.mult), 9)
            step(dve.tensor_reduce(row[:], past[:], AX_X, ALU.add), 10)
            dve.tensor_scalar(expert_of[:], expert[:], float(EXPERTS - 1), None, ALU.min).then_inc(planned, 1)
            dve.scalar_tensor_tensor(row_of[:], slot[:], float(P), row[:], ALU.mult, ALU.add).then_inc(planned, 1)

            for e in range(EXPERTS):
                dve.wait_ge(weight_hi, e + 1)
                dve.tensor_tensor(w[1][:, e], raw[e % 2][:], w[0][:, e].bitcast(F32), ALU.subtract
                                  ).then_inc(weight_lo, 1)
            dve.wait_ge(rows_loaded, 16 * EXPERTS)
            dve.wait_ge(zeros_made, 3)

            def turn_lo(n, k):
                dve.wait_ge(turned_hi, n + 1)
                hi, lo = x_t[k % 2]
                dve.tensor_tensor(lo[:], turns[:, k % 2], hi[:].bitcast(F32), ALU.subtract).then_inc(turned_lo, 1)

            def measure(n, k):
                dve.wait_ge(mixed, n + 1)
                dve.bn_stats(stats[:], x[k][:, 0:D]).then_inc(stats_made, 1)
                dve.tensor_tensor(to[:, k:k + 1], x[k][:, D + 3:D + 4].bitcast(I32), pad_row[:, bass.ds(n, 1)], ALU.max
                                  ).then_inc(to_made, 1)
                wait_apart(dve, stats_made, n + 1, passed)
                wait_apart(dve, offset_made, n, passed)
                dve.bn_aggr(moments[:], stats[:]).then_inc(measured, 1)

            turn_lo(0, 0)

            def tile(i, k, left):
                n = i * BUFFERS + k
                if left:
                    turn_lo(n + 1, k + 1)
                e = dve.value_load(expert_of[0:1, bass.ds(n, 1)], min_val=0, max_val=EXPERTS - 1)
                dve.wait_ge(summed, n + 1)
                wait(dve, mixed, n - 1)
                dve.tensor_tensor(inner[k % 2][:], sums[:, k % 2, :], be_rows[:, bass.ds(e, 1), :].squeeze(1), ALU.add
                                  ).then_inc(biased, 1)
                if not (isinstance(n, int) and n == 0):
                    measure(n - 1, (k - 1) % BUFFERS)
                dve.wait_ge(clipped, n + 1)
                dve.scalar_tensor_tensor(x[k][:, 0:D], inner[k % 2][:], x[k][:, D + 2:D + 3], x[k][:, 0:D],
                                         ALU.mult, ALU.add).then_inc(mixed, 1)

            tiles_in_turn(dve, tile)
            measure(SLOTS - 1, BUFFERS - 1)

        @block.scalar
        def _(act):
            for e in range(EXPERTS):
                act.wait_ge(raw_loaded[e % 2], 16 * (e // 2 + 1))
                act.activation(w[0][:, e], raw[e % 2][:], ACT.Copy).then_inc(weight_hi, 1)

            def normalize(loads, n, k):
                act.wait_ge(loaded[k], 16 * loads)
                act.activation(xn[k % 2][:], x[k][:, 0:D], ACT.Identity, bias=x[k][:, D + 1:D + 2],
                               scale=x[k][:, D:D + 1]).then_inc(normalized, 1)

            def turn_hi(n, k):
                act.wait_ge(turned, n + 1)
                act.activation(x_t[k % 2][0][:], turns[:, k % 2], ACT.Copy).then_inc(turned_hi, 1)

            normalize(1, 0, 0)
            normalize(1, 1, 1)
            turn_hi(0, 0)

            def tile(i, k, left):
                n = i * BUFFERS + k
                if left:
                    turn_hi(n + 1, k + 1)
                if left > 1:
                    normalize(i + 1 + (k + 2) // BUFFERS, n + 2, (k + 2) % BUFFERS)
                act.wait_ge(biased, n + 1)
                act.activation(inner[k % 2][:], inner[k % 2][:], ACT.Relu).then_inc(clipped, 1)

            tiles_in_turn(act, tile)

        @block.tensor
        def _(pe):
            def turn(n, k):
                pe.wait_ge(normalized, n + 1)
                for c in range(CHUNKS):
                    last = pe.transpose(turns[:, k % 2, c, :], xn[k % 2][:, c * P:(c + 1) * P], consts["ident"][:])
                last.then_inc(turned, 1)

            pe.wait_ge(planned, PLAN)
            turn(0, 0)
            pe.wait_ge(weight_lo, EXPERTS)

            def tile(i, k, left):
                n = i * BUFFERS + k
                if left:
                    turn(n + 1, k + 1)
                e = pe.value_load(expert_of[0:1, bass.ds(n, 1)], min_val=0, max_val=EXPERTS - 1)
                pe.wait_ge(turned_lo, n + 1)
                wait(pe, biased, n - 1)
                for c in range(CHUNKS):
                    last = three_pass(pe, sums[:, k % 2, :], [h[:, c, :] for h in x_t[k % 2]],
                                      [h[:, bass.ds(e, 1), c, :].squeeze(1) for h in w], c == 0, c == CHUNKS - 1)
                last.then_inc(summed, 1)

            tiles_in_turn(pe, tile)


WEIGHT_COUNT = float(D * D)
ROUNDER = 1.5 * 2 ** 23


def quantize_weights(nc, t, consts, keep, staging):
    with ExitStack() as ctx:
        mem = Memory(nc, ctx, "quantize_")
        w = mem.sbuf("w", [P, CHUNKS, D])
        above, below = mem.sbuf("above", [P, CHUNKS, D]), mem.sbuf("below", [P, CHUNKS, D])
        ternary = mem.sbuf("ternary", [P, CHUNKS, D], BF16)
        magnitude, total, threshold = [mem.sbuf(n, [P, 1]) for n in ("magnitude", "total", "threshold")]
        turns = mem.psum("turns", [P, CHUNKS, 2 * D], BF16)
        loaded, magnitudes_summed, totalled, thresholds_made, compared, made, turned, kept = [mem.sem(n) for n in (
            "loaded", "magnitudes_summed", "totalled", "thresholds_made", "compared", "made", "turned", "kept")]
        ctx.callback(mem.clear_semaphores)
        with nc.Block() as block:
            @block.sync
            def _(sp):
                sp.dma_start(w[:], t["L1_ffn_weight"].rearrange("(c p) k -> p c k", p=P)).then_inc(loaded, 16)
                for raw, raw_loaded, source in zip(*staging, weight_sources(t)):
                    sp.dma_start(raw[:], source).then_inc(raw_loaded, 16)

            @block.gpsimd
            def _(pool):
                pool.wait_ge(magnitudes_summed, 1)
                pool.partition_all_reduce(total[:], magnitude[:], P, bass.bass_isa.ReduceOp.add).then_inc(totalled, 1)

            @block.vector
            def _(dve):
                dve.wait_ge(loaded, 16)
                dve.tensor_reduce(magnitude[:], w[:], mybir.AxisListType.XY, ALU.add, apply_absolute_value=True
                                  ).then_inc(magnitudes_summed, 1)
                dve.wait_ge(totalled, 1)
                dve.tensor_scalar(keep["w_scale"][:], total[:], 1 / WEIGHT_COUNT, None, ALU.mult).then_inc(thresholds_made, 1)
                dve.tensor_scalar(threshold[:], total[:], 0.5 / WEIGHT_COUNT, None, ALU.mult).then_inc(thresholds_made, 1)
                dve.wait_ge(thresholds_made, 2)
                dve.tensor_scalar(above[:], w[:], threshold[:], None, ALU.is_gt).then_inc(compared, 1)
                dve.tensor_scalar(below[:], w[:], -1.0, threshold[:], ALU.mult, ALU.is_gt).then_inc(compared, 1)
                dve.wait_ge(compared, 2)
                dve.tensor_tensor(ternary[:], above[:], below[:], ALU.subtract).then_inc(made, 1)

            @block.tensor
            def _(pe):
                pe.wait_ge(made, 1)
                pe.wait_ge(consts["ready"], consts["made"])
                for c in range(CHUNKS):
                    for o in range(CHUNKS):
                        last = pe.transpose(turns[:, c, o * P:(o + 1) * P], ternary[:, o, c * P:(c + 1) * P],
                                            consts["ident_half"][:])
                    last.then_inc(turned, 1)

            @block.scalar
            def _(act):
                for c in range(CHUNKS):
                    act.wait_ge(turned, c + 1)
                    act.activation(keep["ternary_t"][:, c, :], turns[:, c, 0:D], ACT.Copy).then_inc(kept, 1)
                act.wait_ge(kept, CHUNKS)


def attend_context(nc, t, consts, keep, x3):
    with ExitStack() as ctx:
        mem = Memory(nc, ctx, "context_")
        scales = mem.sbuf("scales", [P, TILES, 2])
        stats3, moments3 = mem.sbuf("stats3", [P, TILES, 6]), mem.sbuf("moments3", [P, TILES, 2])
        half = mem.sbuf("half", [P, TILES])
        spread3 = mem.sbuf("spread3", [P, TILES])
        istd3, offset3 = [[mem.sbuf(f"{n}{i}", [P, TILES]) for i in range(2)] for n in ("istd3_", "offset3_")]
        xn = mem.sbuf("xn", [P, TILES, D])
        x_t = [mem.sbuf(f"x_t_{h}", [P, CHUNKS, SEQ], F32R) for h in ("hi", "lo")]
        keys = mem.sbuf("keys", [P, 2, CHUNKS, KEYS], F32R)
        key_bias = mem.sbuf("key_bias", [P, 1])
        values = mem.sbuf("values", [P, 2, D], F32R)
        scores = mem.sbuf("scores", [P, SEQ])
        peak, minus_peak = mem.sbuf("peak", [P, TILES]), mem.sbuf("minus_peak", [P, TILES])
        probs = mem.sbuf("probs", [P, TILES, KEYS])
        total = mem.sbuf("total", [P, TILES])
        share, gain = mem.sbuf("share", [P, TILES]), mem.sbuf("gain", [P, TILES])
        probs_t = [mem.sbuf(f"probs_t_{h}", [P, SEQ], F32R) for h in ("hi", "lo")]
        x3n = [mem.sbuf(f"x3n{i}", [P, D]) for i in range(2)]
        largest = mem.sbuf("largest", [P, TILES])

        score_bank, score_turns, prob_turns = mem.psum("score_bank", [P, SEQ]), mem.psum("score_turns", [P, TILES, P]), \
            mem.psum("prob_turns", [P, TILES, P])
        turns, sums = mem.psum("turns", [P, 2, CHUNKS, P]), mem.psum("sums", [P, 2, D])

        S = {n: mem.sem(n) for n in (
            "filled", "keys_loaded", "bias_loaded", "values_loaded",
            "scales_kept", "xn_ready",
            "turned", "turned_hi", "turned_lo", "scored", "scores_ready", "scores_turned", "peaked", "peak_turned",
            "weighed", "probs_turned", "probs_hi", "probs_lo", "inverted", "gain_made", "attended", "mixed",
            "stats3_made", "moments3_made", "spread3_made", "mean3_turned", "istd3_made", "offset3_made",
            "x3n_ready", "largest_made", "largest_kept", "moments3_kept")}
        passed = consts["passed"]
        LEAD, AHEAD = 2, 4
        x_loaded = [mem.sem(f"x_loaded{k}") for k in range(2)]
        START = 1

        def rounds(eng, iteration):
            def at(j):
                iteration(j, j % 2, load=j + AHEAD < BATCHES, score=j < BATCHES, turn=j + 1 < BATCHES,
                          fetch=j + 2 < BATCHES, mix=1 <= j <= BATCHES, measure=j >= LEAD)

            for j in range(LEAD):
                at(j)
            with eng.Fori(0, (BATCHES - AHEAD - LEAD) // 2) as i:
                for k in range(2):
                    iteration(i * 2 + LEAD + k, k, load=True, score=True, turn=True, fetch=True, mix=True, measure=True)
            for j in range(BATCHES - AHEAD, BATCHES + LEAD):
                at(j)

        def row(n):
            return x3[:, bass.ds(n, 1), 0:D].squeeze(1)

        ctx.callback(mem.clear_semaphores)
        block = ctx.enter_context(nc.Block())

        @block.sync
        def _(sp):
            def load_keys(b):
                sp.dma_start(keys[:].bitcast(F32), t["fold_pairs"][b]).then_inc(S["keys_loaded"], 16)

            def load_bias(b):
                sp.dma_start(key_bias[0:KEYS], t["fold_biases"][b]).then_inc(S["bias_loaded"], 16)

            def load_x(b, k):
                wait_apart(sp, x_loaded[k], 8 * (b - k), passed)
                sp.dma_start(x3[:, bass.ds(TILES * b, TILES), :], t["results"][bass.ds(RESULTS_AT + SEQ * b, SEQ), :].rearrange(
                    "(i p) d -> p i d", p=P)).then_inc(x_loaded[k], 16)

            load_x(0, 0)
            load_keys(0)
            load_bias(0)
            for b in range(1, AHEAD):
                load_x(b, b % 2)

            def iteration(j, k, load, score, turn, fetch, mix, measure):
                if load:
                    load_x(j + AHEAD, k)
                if turn:
                    wait_apart(sp, S["scored"], j + 1, passed)
                    load_keys(j + 1)
                    wait_apart(sp, S["scores_ready"], j + 1, passed)
                    load_bias(j + 1)
                if score:
                    wait_apart(sp, S["attended"], TILES * j, passed)
                    sp.dma_start(values[0:KEYS].bitcast(F32), t["v1_pairs"][j]).then_inc(S["values_loaded"], 16)

            rounds(sp, iteration)

        @block.gpsimd
        def _(pool):
            def scale_of(b, moments, spread, istd, offset, names):
                moments_made, spread_made, mean_turned, istd_made, offset_made = [S[n] for n in names]
                wait_apart(pool, moments_made, TILES * (b + 1), passed)
                pool.tensor_scalar(spread[:], moments[:, :, 1], EPS, None, ALU.add).then_inc(spread_made, 1)
                pool.tensor_scalar(offset[:], moments[:, :, 0], -1.0, None, ALU.mult).then_inc(mean_turned, 1)
                pool.wait_ge(spread_made, b + 1)
                pool.tensor_tensor(istd[:], spread[:], half[:], ALU.pow).then_inc(istd_made, 1)
                pool.wait_ge(mean_turned, b + 1)
                pool.wait_ge(istd_made, b + 1)
                pool.tensor_tensor(offset[:], offset[:], istd[:], ALU.mult).then_inc(offset_made, 1)

            pool.memset(half[:], -0.5).then_inc(S["filled"], 1)
            pool.wait_ge(S["filled"], 1)

            def iteration(j, k, load, score, turn, fetch, mix, measure):
                if mix:
                    if not (isinstance(j, int) and j < LEAD):
                        wait_apart(pool, S["x3n_ready"], START + TILES * (j - 2), passed)
                        wait_apart(pool, S["moments3_kept"], START + 2 * (j - 2), passed)
                    scale_of(j - 1, moments3, spread3, istd3[(k - 1) % 2], offset3[(k - 1) % 2],
                             ("moments3_made", "spread3_made", "mean3_turned", "istd3_made", "offset3_made"))

            rounds(pool, iteration)

        @block.tensor
        def _(pe):
            def turn_x(b, tiles=range(TILES)):
                for i in tiles:
                    n = TILES * b + i
                    pe.wait_ge(S["xn_ready"], n + 1)
                    if not (isinstance(n, int) and n < 2):
                        pe.wait_ge(S["turned_lo"], n - 1)
                    for c in range(CHUNKS):
                        last = pe.transpose(turns[:, i % 2, c, :], xn[:, i, c * P:(c + 1) * P], consts["ident"][:])
                    last.then_inc(S["turned"], 1)

            turn_x(0)

            def iteration(j, k, load, score, turn, fetch, mix, measure):
                if score:
                    pe.wait_ge(S["turned_lo"], TILES * (j + 1))
                    pe.wait_ge(S["keys_loaded"], 16 * (j + 1))
                    wait(pe, S["scores_ready"], j)
                    for c in range(CHUNKS):
                        last = three_pass(pe, score_bank[0:KEYS, :], [keys[:, h, c, :] for h in range(2)],
                                          [h[:, c, :] for h in x_t], c == 0, c == CHUNKS - 1)
                    last.then_inc(S["scored"], 1)
                if turn:
                    turn_x(j + 1, range(2))
                if score:
                    pe.wait_ge(S["scores_ready"], j + 1)
                    wait(pe, S["weighed"], TILES * j)
                    for i in range(TILES):
                        last = pe.transpose(score_turns[:, i, 0:KEYS], scores[0:KEYS, i * P:(i + 1) * P],
                                            consts["ident"][0:KEYS, 0:KEYS])
                    last.then_inc(S["scores_turned"], 1)
                if turn:
                    turn_x(j + 1, range(2, TILES))
                if mix:
                    pe.wait_ge(S["probs_lo"], j)
                    pe.wait_ge(S["values_loaded"], 16 * j)
                    for i in range(TILES):
                        n = TILES * (j - 1) + i
                        if not (isinstance(n, int) and n < 2):
                            pe.wait_ge(S["mixed"], n - 1)
                        three_pass(pe, sums[:, i % 2, :], [h[0:KEYS, i * P:(i + 1) * P] for h in probs_t],
                                   [values[0:KEYS, h, :] for h in range(2)]).then_inc(S["attended"], 1)
                if score:
                    pe.wait_ge(S["weighed"], TILES * (j + 1))
                    for i in range(TILES):
                        last = pe.transpose(prob_turns[0:KEYS, i, :], probs[:, i, :], consts["ident"][:])
                    last.then_inc(S["probs_turned"], 1)

            rounds(pe, iteration)

        @block.scalar
        def _(act):
            def turn_hi(b, tiles=range(TILES)):
                for i in tiles:
                    act.wait_ge(S["turned"], TILES * b + i + 1)
                    act.activation(x_t[0][:, :, i * P:(i + 1) * P], turns[:, i % 2], ACT.Copy).then_inc(S["turned_hi"], 1)

            def normalize(b):
                for i in range(TILES):
                    wait(act, S["turned"], TILES * (b - 1) + i + 1)
                    wait_apart(act, S["scales_kept"], b + 1, passed)
                    act.activation(xn[:, i, :], row(TILES * b + i), ACT.Identity, bias=scales[:, i, 1:2],
                                   scale=scales[:, i, 0:1]).then_inc(S["xn_ready"], 1)

            def normalize_again(b, k, tiles):
                for i in tiles:
                    n = TILES * b + i
                    if not (isinstance(n, int) and n < 2):
                        act.wait_ge(S["largest_made"], START + n - min(i, 1))
                    wait_apart(act, S["offset3_made"], b + 1, passed)
                    act.activation(x3n[i % 2][:], row(n), ACT.Identity, bias=offset3[k % 2][:, i:i + 1],
                                   scale=istd3[k % 2][:, i:i + 1]).then_inc(S["x3n_ready"], 1)

            act.sem_inc(S["x3n_ready"], START)
            normalize(0)
            turn_hi(0)
            normalize(1)

            def iteration(j, k, load, score, turn, fetch, mix, measure):
                if score:
                    act.wait_ge(S["bias_loaded"], 16 * (j + 1))
                    wait(act, S["scores_turned"], j)
                    act.wait_ge(S["scored"], j + 1)
                    act.activation(scores[0:KEYS, :], score_bank[0:KEYS, :], ACT.Identity, bias=key_bias[0:KEYS, :],
                                   scale=D ** -0.5).then_inc(S["scores_ready"], 1)
                if turn:
                    turn_hi(j + 1, range(2))
                if measure:
                    normalize_again(j - 2, k, range(2))
                if turn:
                    turn_hi(j + 1, range(2, TILES))
                if score:
                    act.wait_ge(S["peak_turned"], j + 1)
                    wait(act, S["probs_turned"], j)
                    wait(act, S["inverted"], j)
                    for i in range(TILES):
                        act.activation(probs[:, i, :], score_turns[:, i, 0:KEYS], ACT.Exp, bias=minus_peak[:, i:i + 1],
                                       accum_out=total[:, i:i + 1]).then_inc(S["weighed"], 1)
                if measure:
                    normalize_again(j - 2, k, range(2, TILES))
                if fetch:
                    normalize(j + 2)
                if score:
                    act.wait_ge(S["probs_turned"], j + 1)
                    wait(act, S["attended"], TILES * j)
                    act.activation(probs_t[0][0:KEYS, :], prob_turns[0:KEYS].rearrange("p i n -> p (i n)"), ACT.Copy
                                   ).then_inc(S["probs_hi"], 1)

            rounds(act, iteration)

        @block.vector
        def _(dve):
            def keep_scales(b, k):
                wait(dve, S["xn_ready"], TILES * b)
                wait_apart(dve, x_loaded[k], 8 * (b - k) + 16, passed)
                dve.tensor_copy(scales[:], x3[:, bass.ds(TILES * b, TILES), D:RESULT]).then_inc(S["scales_kept"], 1)

            def turn_lo(b, tiles=range(TILES)):
                for i in tiles:
                    dve.wait_ge(S["turned_hi"], TILES * b + i + 1)
                    hi, lo = [h[:, :, i * P:(i + 1) * P] for h in x_t]
                    dve.tensor_tensor(lo, turns[:, i % 2], hi.bitcast(F32), ALU.subtract).then_inc(S["turned_lo"], 1)

            dve.sem_inc(S["moments3_kept"], START)
            dve.sem_inc(S["largest_made"], START)
            keep_scales(0, 0)
            turn_lo(0)
            keep_scales(1, 1)

            def iteration(j, k, load, score, turn, fetch, mix, measure):
                if turn:
                    turn_lo(j + 1, range(2))
                if score:
                    dve.wait_ge(S["scores_turned"], j + 1)
                    dve.tensor_reduce(peak[:], score_turns[:, :, 0:KEYS], AX_X, ALU.max).then_inc(S["peaked"], 1)
                    dve.wait_ge(S["peaked"], j + 1)
                    dve.tensor_scalar(minus_peak[:], peak[:], -1.0, None, ALU.mult).then_inc(S["peak_turned"], 1)
                if turn:
                    turn_lo(j + 1, range(2, TILES))
                if fetch:
                    keep_scales(j + 2, k)
                if measure:
                    wait(dve, S["largest_kept"], j - 2 + 1)
                for i in range(TILES):
                    if measure:
                        dve.wait_ge(S["x3n_ready"], START + TILES * (j - 2) + i + 1)
                        dve.tensor_reduce(largest[:, i:i + 1], x3n[i % 2][:], AX_X, ALU.max, apply_absolute_value=True
                                          ).then_inc(S["largest_made"], 1)
                    if mix:
                        n = TILES * (j - 1) + i
                        dve.wait_ge(S["gain_made"], j)
                        dve.wait_ge(S["attended"], n + 1)
                        dve.scalar_tensor_tensor(row(n), sums[:, i % 2, :], gain[:, i:i + 1], row(n), ALU.mult, ALU.add
                                                 ).then_inc(S["mixed"], 1)
                if measure:
                    wait_apart(dve, S["offset3_made"], j - 1, passed)
                    dve.tensor_copy(keep["istd3"][:, bass.ds(TILES * (j - 2), TILES)], istd3[k % 2][:]
                                    ).then_inc(S["moments3_kept"], 1)
                    dve.tensor_copy(keep["offset3"][:, bass.ds(TILES * (j - 2), TILES)], offset3[k % 2][:]
                                    ).then_inc(S["moments3_kept"], 1)
                    dve.wait_ge(S["largest_made"], START + TILES * (j - 1))
                    dve.tensor_tensor(keep["largest"][:], keep["largest"][:], largest[:], ALU.max
                                      ).then_inc(S["largest_kept"], 1)
                if mix:
                    for i in range(TILES):
                        n = TILES * (j - 1) + i
                        wait_apart(dve, S["mixed"], n + 1, passed)
                        dve.bn_stats(stats3[:, i, :], row(n)).then_inc(S["stats3_made"], 1)
                    wait(dve, S["spread3_made"], j - 1)
                    wait_apart(dve, S["mean3_turned"], j - 1, passed)
                    for i in range(TILES):
                        n = TILES * (j - 1) + i
                        wait_apart(dve, S["stats3_made"], n + 1, passed)
                        dve.bn_aggr(moments3[:, i, :], stats3[:, i, :]).then_inc(S["moments3_made"], 1)
                if score:
                    dve.wait_ge(S["weighed"], TILES * (j + 1))
                    wait(dve, S["mixed"], TILES * j)
                    dve.reciprocal(share[:], total[:]).then_inc(S["inverted"], 1)
                    dve.wait_ge(S["inverted"], j + 1)
                    dve.tensor_scalar(gain[:], share[:], consts["gates"][:, 1:2], None, ALU.mult).then_inc(S["gain_made"], 1)
                    dve.wait_ge(S["probs_hi"], j + 1)
                    dve.tensor_tensor(probs_t[1][0:KEYS, :], prob_turns[0:KEYS].rearrange("p i n -> p (i n)"),
                                      probs_t[0][0:KEYS, :].bitcast(F32), ALU.subtract).then_inc(S["probs_lo"], 1)

            dve.memset(keep["largest"][:], 0.0).then_inc(S["largest_kept"], 1)
            rounds(dve, iteration)


def quantized_layer(nc, t, consts, keep, x3):
    with ExitStack() as ctx:
        mem = Memory(nc, ctx, "quantized_")
        COUNT = BATCHES * TILES
        ROUND = 4
        LEAD = ROUND - 1
        bias_row = mem.sbuf("bias_row", [P, D])
        top, largest, unit, per_unit, gain = [mem.sbuf(n, [P, 1]) for n in ("top", "largest", "unit", "per_unit", "gain")]
        scale, offset = mem.sbuf("scale", [P, COUNT]), mem.sbuf("offset", [P, COUNT])
        scaled = [mem.sbuf(f"scaled{i}", [P, D]) for i in range(ROUND)]
        whole = [mem.sbuf(f"whole{i}", [P, D], BF16) for i in range(ROUND)]
        whole_t = [mem.sbuf(f"whole_t{i}", [P, CHUNKS, P], BF16) for i in range(2)]
        turns = mem.psum("turns", [P, 2, 2 * D], BF16)
        sums = mem.psum("sums", [P, 2, D])
        S = {n: mem.sem(n) for n in ("row_loaded", "row_scaled", "step", "reduced", "scaled", "rounded", "turned", "turned_kept",
                                     "summed", "biased", "mixed", "stored")}
        passed = consts["passed"]

        def tiles_in_turn(eng, tile):
            for k in range(ROUND):
                tile(k, k, ROUND)
            with eng.Fori(1, COUNT // ROUND - 1) as i:
                for k in range(ROUND):
                    tile(i * ROUND + k, k, ROUND)
            for k in range(ROUND):
                tile(COUNT - ROUND + k, k, ROUND - 1 - k)

        def row(n):
            return x3[:, bass.ds(n, 1), 0:D].squeeze(1)

        block = ctx.enter_context(nc.Block())

        @block.sync
        def _(sp):
            sp.dma_start(bias_row[:], t["L1_ffn_bias"].partition_broadcast(P)).then_inc(S["row_loaded"], 16)
            out = t["out"].rearrange("b (i p) d -> (b i) p d", p=P)

            def tile(n, k, left):
                wait_apart(sp, S["mixed"], n + 1, passed)
                sp.dma_start(out[bass.ds(n, 1)].squeeze(0), row(n)).then_inc(S["stored"], 16)

            tiles_in_turn(sp, tile)
            sp.wait_ge(S["stored"], 16 * COUNT)

        @block.gpsimd
        def _(pool):
            pool.wait_ge(S["step"], 1)
            pool.partition_all_reduce(largest[:], top[:], P, bass.bass_isa.ReduceOp.max).then_inc(S["reduced"], 1)
            pool.wait_ge(S["row_scaled"], 1)

            def tile(n, k, left):
                wait_apart(pool, S["scaled"], n + 1, passed)
                pool.tensor_tensor(row(n), row(n), bias_row[:], ALU.add).then_inc(S["biased"], 1)

            tiles_in_turn(pool, tile)

        @block.vector
        def _(dve):
            dve.tensor_reduce(top[:], keep["largest"][:], AX_X, ALU.max).then_inc(S["step"], 1)
            dve.wait_ge(S["row_loaded"], 16)
            dve.tensor_scalar(bias_row[:], bias_row[:], consts["gates"][:, 3:4], None, ALU.mult).then_inc(S["row_scaled"], 1)
            dve.wait_ge(S["reduced"], 1)
            dve.tensor_scalar(unit[:], largest[:], 1 / 127.0, None, ALU.mult).then_inc(S["step"], 1)
            dve.wait_ge(S["step"], 2)
            dve.reciprocal(per_unit[:], unit[:]).then_inc(S["step"], 1)
            dve.tensor_scalar(gain[:], unit[:], keep["w_scale"][:], consts["gates"][:, 3:4], ALU.mult, ALU.mult
                              ).then_inc(S["step"], 1)
            dve.wait_ge(S["step"], 4)
            dve.tensor_scalar(scale[:], keep["istd3"][:], per_unit[:], None, ALU.mult).then_inc(S["step"], 1)
            dve.tensor_scalar(offset[:], keep["offset3"][:], per_unit[:], None, ALU.mult).then_inc(S["step"], 1)
            dve.wait_ge(S["step"], 6)

            def round_tile(n, k):
                wait(dve, S["turned"], n - LEAD)
                dve.wait_ge(S["scaled"], n + 1)
                dve.tensor_scalar(whole[k % ROUND][:], scaled[k % ROUND][:], ROUNDER, ROUNDER, ALU.add, ALU.subtract
                                  ).then_inc(S["rounded"], 1)

            for n in range(LEAD):
                round_tile(n, n)

            def tile(n, k, left):
                dve.wait_ge(S["biased"], n + 1)
                dve.wait_ge(S["summed"], n + 1)
                dve.scalar_tensor_tensor(row(n), sums[:, k % 2, :], gain[:], row(n), ALU.mult, ALU.add
                                         ).then_inc(S["mixed"], 1)
                if left >= LEAD:
                    round_tile(n + LEAD, k + LEAD)

            tiles_in_turn(dve, tile)

        @block.tensor
        def _(pe):
            def turn(n, k):
                pe.wait_ge(S["rounded"], n + 1)
                wait(pe, S["turned_kept"], n - 1)
                for c in range(CHUNKS):
                    last = pe.transpose(turns[:, k % 2, c * P:(c + 1) * P], whole[k % ROUND][:, c * P:(c + 1) * P],
                                        consts["ident_half"][:])
                last.then_inc(S["turned"], 1)

            turn(0, 0)

            def tile(n, k, left):
                if left:
                    turn(n + 1, k + 1)
                pe.wait_ge(S["turned_kept"], n + 1)
                wait(pe, S["mixed"], n - 1)
                for c in range(CHUNKS):
                    last = pe.matmul(sums[:, k % 2, :], whole_t[k % 2][:, c, :], keep["ternary_t"][:, c, :],
                                     start=c == 0, stop=c == CHUNKS - 1)
                last.then_inc(S["summed"], 1)

            tiles_in_turn(pe, tile)

        @block.scalar
        def _(act):
            def scale_tile(n, k):
                wait_apart(act, S["rounded"], n - LEAD, passed)
                act.activation(scaled[k % ROUND][:], row(n), ACT.Identity, bias=offset[:, bass.ds(n, 1)],
                               scale=scale[:, bass.ds(n, 1)]).then_inc(S["scaled"], 1)

            act.wait_ge(S["step"], 6)
            for n in range(LEAD):
                scale_tile(n, n)

            def tile(n, k, left):
                act.wait_ge(S["turned"], n + 1)
                wait(act, S["summed"], n - 1)
                act.activation(whole_t[k % 2][:], turns[:, k % 2, 0:D].rearrange("p (c n) -> p c n", n=P), ACT.Copy
                               ).then_inc(S["turned_kept"], 1)
                if left >= LEAD:
                    scale_tile(n + LEAD, k + LEAD)

            tiles_in_turn(act, tile)


def flamingo(nc, t):
    with ExitStack() as ctx:
        mem = Memory(nc, ctx)
        t.update(scratch(nc))
        consts = constants(nc, mem, t)
        keep = {"counts": mem.sbuf("counts", [P, EXPERTS]), 
                "x_scales": mem.sbuf("x_scales", [P, BATCHES * TILES, 2]),
                "w_scale": mem.sbuf("w_scale", [P, 1]), "ternary_t": mem.sbuf("ternary_t", [P, CHUNKS, D], BF16),
                "istd3": mem.sbuf("istd3", [P, BATCHES * TILES]), "offset3": mem.sbuf("offset3", [P, BATCHES * TILES]),
                "largest": mem.sbuf("largest", [P, TILES])}
        with ExitStack() as first:
            weights = Memory(nc, first)
            hold = {n: [weights.sbuf(f"{n}_{h}", [P, CHUNKS, D], F32R) for h in ("hi", "lo")] for n in ("wq", "wo", "wg")}
            staging_loaded = [mem.sem(f"staging_loaded{i}") for i in range(3)]
            with ExitStack() as second:
                staging = [Memory(nc, second).sbuf(f"staging{i}", [P, CHUNKS, D]) for i in range(3)], staging_loaded
                quantize_weights(nc, t, consts, keep, staging)
                prepare(nc, hold, t, consts, keep, staging)
            attend_and_route(nc, hold, t, consts, keep)
        run_experts(nc, t, consts, keep)
        x3 = mem.sbuf("x3", [P, BATCHES * TILES, RESULT])
        attend_context(nc, t, consts, keep, x3)
        quantized_layer(nc, t, consts, keep, x3)


_INS = ['x', 'ctx_1024', 'g_xattn', 'g_ffn', 'L0_xattn_Wq', 'L0_xattn_bq', 'L0_xattn_Wkv', 'L0_xattn_bkv',
        'L0_xattn_Wo', 'L0_xattn_bo', 'L0_ffn_Wg', 'L0_ffn_bg', 'L0_ffn_We', 'L0_ffn_be', 'L1_xattn_Wq',
        'L1_xattn_bq', 'L1_ffn_weight', 'L1_ffn_bias']


def kernel(**inputs):
    import numpy as _np
    import concourse.bacc as _bacc
    from concourse import mybir as _mybir
    from concourse.bass_utils import run_bass_kernel_spmd as _run

    nc = _bacc.Bacc("TRN2", target_bir_lowering=False, num_devices=1)
    arrays, tensors = {}, {}
    for name in _INS:
        a = _np.ascontiguousarray(inputs[name])
        arrays[f"in_{name}"] = a
        tensors[name] = nc.dram_tensor(f"in_{name}", a.shape, _mybir.dt.from_np(a.dtype), kind="ExternalInput").ap()
    tensors["out"] = nc.dram_tensor("out_x", (BATCHES, SEQ, D), F32, kind="ExternalOutput").ap()
    flamingo(nc, tensors)
    return _run(nc, [arrays], core_ids=[0]).results[0]["out_x"]
```
